# Optimizing a Trainium2 kernel written in Bass

```python
import numpy as np
import jax
import jax.numpy as jnp

def _softmax(x, axis=-1):
    return jax.nn.softmax(x, axis=axis)

def _gelu(x):
    return jax.nn.gelu(x, approximate=True)

def _silu(x):
    return jax.nn.silu(x)

def _sigmoid(x):
    return jax.nn.sigmoid(x)

def _layernorm(x, axis=-1, eps=1e-05):
    m = jnp.mean(x, axis=axis, keepdims=True)
    v = jnp.var(x, axis=axis, keepdims=True)
    return (x - m) / jnp.sqrt(v + eps)

def _scatter_add(tgt, idx, src, axis=0):
    return tgt.at[idx].add(src)

def _segment_sum(src, seg, n):
    return jax.ops.segment_sum(src, seg, n)
kernel_name = 'mk_gnn_resnorm_d2_gnn_r8_ab593d'

def setup_inputs(seed: int=0):
    np.random.seed(seed)
    _w = jnp.asarray

    def _rec_inputs():
        import jax
        import jax.numpy as jnp
        _gk = jax.random.key(seed)
        x = -6.415e-05 + 1 * jax.random.normal(jax.random.fold_in(_gk, 1), (1250, 1024), jnp.float32)
        src = jax.random.randint(jax.random.fold_in(_gk, 2), (20000,), 0, 1250, jnp.int32)
        dst = jax.random.randint(jax.random.fold_in(_gk, 3), (20000,), 0, 1250, jnp.int32)
        _o = jnp.argsort(dst, stable=True)
        src = src[_o]
        dst = dst[_o]
        edge_type_8 = jax.random.randint(jax.random.fold_in(_gk, 12), (20000,), 0, 8, jnp.int32)
        return (x, src, dst, edge_type_8)
    x, src, dst, edge_type_8 = _rec_inputs()

    def _L0_gnn_setup():
        import jax, jax.numpy as jnp
        import numpy as np
        N, D, R, E = (1250, 1024, 8, 10000)

        def _rgcn(x, edge_index, edge_type, weight, root, bias):
            src, dst = (edge_index[0], edge_index[1])
            msgs = x[src]
            out = x @ root + bias
            n = x.shape[0]
            for r in range(weight.shape[0]):
                mask = (edge_type == r).astype(x.dtype)
                sums = jax.ops.segment_sum(msgs * mask[:, None], dst, num_segments=n)
                cnt = jax.ops.segment_sum(mask, dst, num_segments=n)
                mean = sums / jnp.maximum(cnt, 1.0)[:, None]
                out = out + mean @ weight[r]
            return out
        key = jax.random.key(seed)
        ks = jax.random.split(key, 8)
        s = 1.0 / np.sqrt(D)
        x = jax.random.normal(ks[0], (N, D), dtype=jnp.float32)
        edge_index = jax.random.randint(ks[1], (2, E), 0, N, dtype=jnp.int64)
        edge_type = jax.random.randint(ks[2], (E,), 0, R, dtype=jnp.int64)
        weight = jax.random.normal(ks[3], (R, D, D), dtype=jnp.float32) * s
        root = jax.random.normal(ks[4], (D, D), dtype=jnp.float32) * s
        bias = jnp.zeros((D,), dtype=jnp.float32)
        w_gate = jax.random.normal(ks[5], (2 * D, D), dtype=jnp.float32) * (1.0 / np.sqrt(2 * D))
        b_gate = jnp.zeros((D,), dtype=jnp.float32)
        return {'x': x, 'edge_index': edge_index, 'edge_type': edge_type, 'weight': weight, 'root': root, 'bias': bias, 'w_gate': w_gate, 'b_gate': b_gate}
    _L0_gnn_all = _L0_gnn_setup()
    _L0_gnn_in = {k: v for k, v in _L0_gnn_all.items() if k in ('weight', 'root', 'bias', 'w_gate', 'b_gate')}
    del _L0_gnn_all

    def _L1_gnn_setup():
        import jax, jax.numpy as jnp
        import numpy as np
        N_NODES = 1250
        N_EDGES = 20000
        DIM = 1024
        key = jax.random.key(seed)
        k1, k2, k3 = jax.random.split(key, 3)
        x = jax.random.normal(k1, (N_NODES, DIM), dtype=jnp.float32)
        edge_index = jax.random.randint(k2, (2, N_EDGES), 0, N_NODES, dtype=jnp.int64)
        W = jax.random.normal(k3, (DIM, DIM), dtype=jnp.float32) * (1.0 / np.sqrt(DIM))
        b = jnp.zeros((DIM,), dtype=jnp.float32)
        return {'x': x, 'edge_index': edge_index, 'W': W, 'b': b}
    _L1_gnn_all = _L1_gnn_setup()
    _L1_gnn_in = {k: v for k, v in _L1_gnn_all.items() if k in ('W', 'b')}
    del _L1_gnn_all
    return {'x': x, 'src': src, 'dst': dst, 'edge_type_8': edge_type_8, 'L0_gnn_weight': _L0_gnn_in['weight'], 'L0_gnn_root': _L0_gnn_in['root'], 'L0_gnn_bias': _L0_gnn_in['bias'], 'L0_gnn_w_gate': _L0_gnn_in['w_gate'], 'L0_gnn_b_gate': _L0_gnn_in['b_gate'], 'L1_gnn_W': _L1_gnn_in['W'], 'L1_gnn_b': _L1_gnn_in['b']}

def reference(x, src, dst, edge_type_8, L0_gnn_weight, L0_gnn_root, L0_gnn_bias, L0_gnn_w_gate, L0_gnn_b_gate, L1_gnn_W, L1_gnn_b):
    import jax
    import jax.numpy as jnp

    def _L0_gnn_ref(x, edge_index, edge_type, weight, root, bias, w_gate, b_gate):
        import jax, jax.numpy as jnp
        import numpy as np
        N, D, R, E = (1250, 1024, 8, 10000)

        def _rgcn(x, edge_index, edge_type, weight, root, bias):
            src, dst = (edge_index[0], edge_index[1])
            msgs = x[src]
            out = x @ root + bias
            n = x.shape[0]
            for r in range(weight.shape[0]):
                mask = (edge_type == r).astype(x.dtype)
                sums = jax.ops.segment_sum(msgs * mask[:, None], dst, num_segments=n)
                cnt = jax.ops.segment_sum(mask, dst, num_segments=n)
                mean = sums / jnp.maximum(cnt, 1.0)[:, None]
                out = out + mean @ weight[r]
            return out
        u = _rgcn(x, edge_index, edge_type, weight, root, bias)
        z = jnp.concatenate([u, x], axis=1) @ w_gate + b_gate
        h = jnp.tanh(u) * z + x * (1.0 - z)
        return h

    def _L1_gnn_ref(x, edge_index, W, b):
        import jax, jax.numpy as jnp
        import numpy as np
        N_NODES = 1250
        N_EDGES = 20000
        DIM = 1024
        'GCNConv (add_self_loops=True, symmetric norm) -> Dropout(eval=identity) -> ReLU.'
        n = x.shape[0]
        loops = jnp.arange(n, dtype=edge_index.dtype)
        src = jnp.concatenate([edge_index[0], loops])
        dst = jnp.concatenate([edge_index[1], loops])
        deg = jax.ops.segment_sum(jnp.ones_like(dst, dtype=x.dtype), dst, num_segments=n)
        dinv = jnp.where(deg > 0, jax.lax.rsqrt(deg), jnp.zeros_like(deg))
        norm = dinv[src] * dinv[dst]
        h = x @ W
        msg = h[src] * norm[:, None]
        out = jax.ops.segment_sum(msg, dst, num_segments=n) + b
        return jax.nn.relu(out)
    edge_index = jnp.stack([src, dst])
    x = _layernorm(x + _L0_gnn_ref(x, edge_index, edge_type_8, L0_gnn_weight, L0_gnn_root, L0_gnn_bias, L0_gnn_w_gate, L0_gnn_b_gate), axis=-1)
    x = _layernorm(x + _L1_gnn_ref(x, edge_index, L1_gnn_W, L1_gnn_b), axis=-1)
    return x

_drawn_inputs = setup_inputs


def setup_inputs(seed=0):
    import zlib

    import numpy as np

    out = dict(_drawn_inputs(seed))
    spreads = {'L0_gnn_bias': (0.0, 0.1), 'L0_gnn_b_gate': (0.0, 0.1), 'L1_gnn_b': (0.0, 0.1)}
    factors = {}
    for name, (base, spread) in spreads.items():
        noise = np.random.default_rng([zlib.crc32(name.encode()), seed]).standard_normal(out[name].shape)
        drawn = base * np.exp(spread * noise) if base else spread * noise
        out[name] = jnp.asarray(drawn.astype(out[name].dtype))
    for name, factor in factors.items():
        out[name] = (out[name] * factor).astype(out[name].dtype)
    return out
```

```python
import concourse.bass as bass
from concourse import mybir
from contextlib import ExitStack

F32 = mybir.dt.float32
F32R = mybir.dt.float32r
F16 = mybir.dt.float16
I32 = mybir.dt.int32
I16 = mybir.dt.int16
ALU = mybir.AluOpType
ACT = mybir.ActivationFunctionType
AXIS_X = mybir.AxisListType.X

P = 128
N, D, R, E = 1250, 1024, 8, 20000
NT = (N + P - 1) // P
NPAD = NT * P
LAST = N - (NT - 1) * P
KT = D // P
HW = 512
EPART, ECOL = 125, E // 125
PAIR = 2 * P
NPAIR = (E + NT * (PAIR - 1)) // PAIR
ETILES = 2 * NPAIR
NKEY = NT * R
FAR = 1 << 20
RING = 8
EPS = 1e-5

UNITS_Y = 2 * R
TILES_BODY = 2 * NT
SUBSTEPS = 2 * TILES_BODY
PAIRS_BODY = NPAIR // 2
YROWS = R * NPAD
AHEAD = 2


def pairs_of_substep():
    extra = PAIRS_BODY - SUBSTEPS
    out, at = [], 0
    for s in range(SUBSTEPS):
        k = 1 + ((s + 1) * extra // SUBSTEPS - s * extra // SUBSTEPS)
        out.append(range(at, at + k))
        at += k
    return out


PAIRS_OF = pairs_of_substep()


class Chain:

    def __init__(self, eng, sem):
        self.eng, self.sem, self.at, self.steps = eng, sem, 0, 0

    def link(self, ins):
        ins.then_inc(self.sem, 1)
        self.at = self.at + 1
        self.steps += 1
        self.eng.wait_ge(self.sem, self.at)

    def enter(self, turn, per_turn):
        self.before, self.steps = self.at, 0
        self.at = turn * per_turn + self.before

    def leave(self, turns, per_turn):
        assert self.steps == per_turn, (self.steps, per_turn)
        self.at = self.before + turns * per_turn


def gnn_resnorm_kernel(nc, x, src, dst, edge_type, w_rel, w_root, b_root, w_gate, b_gate, w_gcn, b_gcn, out):
    def dram(name, shape, dt=F32):
        return nc.dram_tensor(name, shape, dt, kind="Internal").ap()

    y_d = [dram(f"y_half{h}", (YROWS, HW)) for h in range(2)]
    rootgate_d = dram("rootgate", (2 * NPAD, D))
    agg_d = dram("agg", (2 * NPAD, HW))
    x1_d = dram("x1", (NPAD, D))
    count_d = dram("edge_count", (P, NT * NPAD), I16)
    hhi_d = dram("h_hi", (KT * P, D))
    hlo_d = dram("h_lo", (KT * P, D))
    rec_d = dram("records", (P * ETILES, 4), I32)
    inv_d = dram("inverse_count", (P * NKEY, 1))

    ctx = ExitStack()
    with ctx:
        KB = 1024
        base = (nc.sbuf_base + 63) // 64 * 64
        at = {}
        for name, size in (("xt_hi", KT * NPAD * 4), ("xt_lo", KT * NPAD * 4), ("w_hi", 32 * KB), ("w_lo", 32 * KB),
                           ("work", 28 * KB), ("split_hi", 8 * KB), ("split_lo", 8 * KB), ("raw_w", 4 * KB),
                           ("stage", 4 * KB), ("onehot", 2 * KB)):
            at[name] = base
            base += size

        def place(name, shape, dt, where, skip=0):
            return nc.alloc_sbuf_tensor_at(name, shape, dt, offset=at[where] + skip)

        def small(name, shape, dt):
            nonlocal base
            t = nc.alloc_sbuf_tensor_at(name, shape, dt, offset=base)
            size = mybir.dt.size(dt)
            for s in shape[1:]:
                size *= s
            base += (size + 31) // 32 * 32
            return t

        XHI = place("XHI", [P, KT * NPAD], F32R, "xt_hi")
        XLO = place("XLO", [P, KT * NPAD], F32R, "xt_lo")
        WHI = place("WHI", [P, 2 * KT * HW], F32R, "w_hi")
        WLO = place("WLO", [P, 2 * KT * HW], F32R, "w_lo")
        WORK = place("WORK", [P, 7 * D], F32, "work")
        SPHI = place("SPHI", [P, 2 * D], F32R, "split_hi")
        SPLO = place("SPLO", [P, 2 * D], F32R, "split_lo")
        STAGE = place("STAGE", [P, 2, HW], F32, "stage")
        ONEHOT = place("ONEHOT", [P, 2, 2, P], F32R, "onehot")
        xhi = XHI[:, :].rearrange("p (k n) -> p k n", k=KT)
        xlo = XLO[:, :].rearrange("p (k n) -> p k n", k=KT)
        GCN = 2 * KT * HW
        gcn_hi = XHI[:, 0:GCN].rearrange("p (k n) -> p k n", k=KT)
        gcn_lo = XLO[:, 0:GCN].rearrange("p (k n) -> p k n", k=KT)
        UT = GCN
        ut_hi, ut_lo = XHI[:, UT:UT + D], XLO[:, UT:UT + D]
        BIAS_ROOT = place("BIAS_ROOT", [P, D], F32, "xt_hi", (UT + D) * 4)
        BIAS_GATE = place("BIAS_GATE", [P, D], F32, "xt_lo", (UT + D) * 4)
        BIAS_GCN = place("BIAS_GCN", [P, D], F32, "xt_hi", 4 * NPAD * 4)
        wraw = place("WRAW", [P, 2 * KT * HW], F32, "w_lo")[:, :].rearrange("p (b k n) -> p b k n", b=2, k=KT)
        gcn_raw = place("GCNRAW", [P, GCN], F32, "xt_lo")[:, :].rearrange("p (k n) -> p k n", k=KT)
        whi = WHI[:, :].rearrange("p (b k n) -> p b k n", b=2, k=KT)
        wlo = WLO[:, :].rearrange("p (b k n) -> p b k n", b=2, k=KT)
        hhi = WHI[:, :].rearrange("p (s n) -> p s n", s=KT)
        hlo = WLO[:, :].rearrange("p (s n) -> p s n", s=KT)
        sp_hi = SPHI[:, :].rearrange("p (r e n) -> p r e n", r=2, e=2)
        sp_lo = SPLO[:, :].rearrange("p (r e n) -> p r e n", r=2, e=2)
        HST_HI = place("HST_HI", [P, D], F32R, "stage")
        HST_LO = place("HST_LO", [P, D], F32R, "raw_w")
        CIN = [place("CIN0", [P, NPAD], I16, "stage"), place("CIN1", [P, NPAD], I16, "raw_w")]
        U = WORK[:, 0:NT * HW].rearrange("p (g n) -> p g n", g=NT)
        COUNT = WORK[:, 0:NT * NPAD // 2].bitcast(I16).rearrange("p (g n) -> p g n", g=NT)
        RAWG = WORK[:, 5 * D:7 * D].rearrange("p (r n) -> p r n", r=4)
        XIN = WORK[:, 5 * D:7 * D].rearrange("p (r n) -> p r n", r=2)
        slot = [WORK[:, s * D:(s + 1) * D] for s in (5, 6, 2, 3, 0, 1, 4)]
        CHUNK = 16
        KEYHOT = place("KEYHOT", [P, 2, CHUNK, NKEY], F16, "split_hi")
        LOCHOT = place("LOCHOT", [P, 2, CHUNK, P], F16, "split_lo")
        DSTHOT = place("DSTHOT", [P, 3, NPAD], F16, "split_hi")
        DSTHOT3 = place("DSTHOT3", [P, 1, NPAD], F16, "split_lo")
        SRCHOT = place("SRCHOT", [P, 4, P], F16, "split_lo", 2 * NPAD)
        PADREC = place("PADREC", [P, ETILES, 4], I32, "split_hi")
        MEMB = WORK[0:EPART, 0:NT * ECOL].rearrange("p (g c) -> p g c", g=NT)
        SCAN = [WORK[0:EPART, (1 + b) * NT * ECOL:(2 + b) * NT * ECOL].rearrange("p (g c) -> p g c", g=NT) for b in range(2)]

        def temp(n, dt=F32):
            return WORK[0:EPART, NT * ECOL + n * ECOL:NT * ECOL + (n + 1) * ECOL].bitcast(dt)

        T_SRC, T_DST, T_TYPE, T_LOC, T_GRP, T_GRPF = temp(0, I32), temp(1, I32), temp(2, I32), temp(3, I32), temp(4, I32), temp(5)
        T_LOCF = temp(6)
        O_POS = temp(0)
        O_POSI, O_LANE, O_TILE = temp(1, I32), temp(2, I32), temp(3, I32)
        EARLIER = WORK[0:EPART, 3 * NT * ECOL:3 * NT * ECOL + EPART]
        ONES = WORK[0:EPART, 3 * NT * ECOL + P:3 * NT * ECOL + 2 * P]
        KEY = place("KEY", [EPART, ECOL], F32, "onehot")

        REC = small("REC", [P, ETILES, 4], I32)
        W_EDGE = small("W_EDGE", [P, ETILES], F32)
        SRC_LOC = small("SRC_LOC", [P, ETILES], F32)
        CELL = small("CELL", [P, ETILES], F32)
        ADDR = small("ADDR", [EPART, ECOL], I32)
        IOTA = small("IOTA", [P, NPAD], F16)
        IDENT = small("IDENT", [P, P], F32)
        IDX = small("IDX", [P, 2, RING], I32)
        RREC = small("RREC", [P, 2, RING, 4], I32)
        WGOT = small("WGOT", [P, 2, RING], F32)
        GROUP = small("GROUP", [1, NPAIR], I32)
        INV = small("INV", [P, NKEY], F32)
        DINV = small("DINV", [P, NT], F32)
        T10 = place("T10", [P, 4, NT], F32, "onehot", 768)
        T10I = place("T10I", [P, NT], I32, "onehot", 928)
        DEG = place("DEG", [P, NT], F32, "onehot", 1792)
        STATS = small("STATS", [P, 2, 6], F32)
        MV = small("MV", [P, 2], F32)
        VAR = small("VAR", [P, 1], F32)
        RSTD = small("RSTD", [P, 1], F32)
        MINUS_HALF = small("MINUS_HALF", [P, NT], F32)
        assert base <= nc.sbuf_usable_end, (base, nc.sbuf_usable_end)
        PAIRSUM = place("PAIRSUM", [1, 2, NPAIR], F32, "onehot", 1024)

        PG = ctx.enter_context(nc.psum_tensor("PG", [P, 4, HW], F32))
        PM = ctx.enter_context(nc.psum_tensor("PM", [P, 4, HW], F32))
        PMALL = PM[:, :, :].rearrange("p b n -> p (b n)")

        def sem(name):
            return ctx.enter_context(nc.semaphore(name))

        x_in = [sem(f"x_in{b}") for b in range(2)]
        x_turned = sem("x_turned")
        x_hi = sem("x_hi")
        x_split = sem("x_split")
        w0_in = [sem(f"w0_in{k}") for k in range(KT)]
        w_in = [sem(f"w_in{b}") for b in range(2)]
        w_hi = sem("w_hi")
        w_split = sem("w_split")
        gemm_done = sem("gemm_done")
        evac_done = sem("evac_done")
        y_out = [sem(f"y_out{b}") for b in range(2)]
        edges_in = sem("edges_in")
        consts = sem("consts")
        rows_total = sem("rows_total")
        offsets = sem("offsets")
        pos_ready = sem("pos_ready")
        pad_set = sem("pad_set")
        pad_out = sem("pad_out")
        idx_set = sem("idx_set")
        scattered = [sem(f"scattered{b}") for b in range(2)]
        sorted_in = sem("sorted_in")
        chunk_ready = sem("chunk_ready")
        chunk_done = sem("chunk_done")
        inv_ready = sem("inv_ready")
        inv_out = sem("inv_out")
        w_got = [sem(f"w_got{b}") for b in range(2)]
        w_ready = sem("w_ready")
        deg_ready = sem("deg_ready")
        dinv_ready = sem("dinv_ready")
        hot_ready = sem("hot_ready")
        cells_done = sem("cells_done")
        cells_added = sem("cells_added")
        count_out = sem("count_out")
        work_clear = sem("work_clear")
        got = [sem(f"got{b}") for b in range(4)]
        msg_hi = sem("msg_hi")
        msg_split = sem("msg_split")
        pair_ready = sem("pair_ready")
        pair_done = sem("pair_done")
        pair_added = sem("pair_added")
        agg_out = sem("agg_out")
        agg1_out = sem("agg1_out")
        bias_in = sem("bias_in")
        bias_gate_in = sem("bias_gate_in")
        u_in = sem("u_in")
        z_in = sem("z_in")
        root_ready = sem("root_ready")
        gate_ready = sem("gate_ready")
        u_ready = sem("u_ready")
        u_turned = sem("u_turned")
        u_hi = sem("u_hi")
        u_split = sem("u_split")
        tanh_done = sem("tanh_done")
        z_done = sem("z_done")
        z_read = sem("z_read")
        x1_ready = sem("x1_ready")
        x1_turned = sem("x1_turned")
        x1_hi = sem("x1_hi")
        x1_split = sem("x1_split")
        x1_out = sem("x1_out")
        var_ready = sem("var_ready")
        rstd_ready = sem("rstd_ready")
        h_done = sem("h_done")
        h_hi = sem("h_hi")
        h_split = sem("h_split")
        h_out = sem("h_out")
        h_in = [sem(f"h_in{s}") for s in range(KT)]
        c_in = [sem(f"c_in{b}") for b in range(2)]
        c_split = sem("c_split")
        conv_done = sem("conv_done")
        conv_read = sem("conv_read")
        res_in = [sem(f"res_in{b}") for b in range(2)]
        bias1_in = sem("bias1_in")
        out_ready = sem("out_ready")
        out_done = [sem(f"out_done{b}") for b in range(2)]
        passed_pool = sem("passed_pool")
        passed_dve = sem("passed_dve")
        dve_chain = sem("dve_chain")
        pool_chain = sem("pool_chain")

        block = ctx.enter_context(nc.Block())

        def after(eng, s, value):
            if not (isinstance(value, int) and value <= 0):
                eng.wait_ge(s, value)

        @block.sync
        def _(sp):
            def load_w(raw, b, weight, h):
                for c in range(2):
                    rows = weight[c * (D // 2):(c + 1) * (D // 2), h * HW:(h + 1) * HW]
                    sp.dma_start(raw[:, c * (KT // 2):(c + 1) * (KT // 2), :],
                                 rows.rearrange("(k p) n -> p k n", p=P)).then_inc(w_in[b], 16)

            def load_unit(n, b, weight, h):
                sp.wait_ge(gemm_done, (n - 1) * NT)
                load_w(wraw[:, b, :, :], b, weight, h)

            def load_x(t):
                if t >= 2:
                    sp.wait_ge(x_turned, 2 * (t - 1))
                rows = min(P, N - t * P)
                sp.dma_start(XIN[0:rows, t % 2, :], x[t * P:t * P + rows, :]).then_inc(x_in[t % 2], 16)

            def first_unit(k):
                sp.dma_start(wraw[:, 0, k, :], w_rel[0][k * P:(k + 1) * P, 0:HW]).then_inc(w0_in[k], 16)

            load_x(0)
            for k in range(KT // 2):
                first_unit(k)
            load_x(1)
            for k in range(KT // 2, KT):
                first_unit(k)
            for temp_i, a in ((T_SRC, src), (T_DST, dst), (T_TYPE, edge_type)):
                sp.dma_start(temp_i, a.rearrange("(p c) -> p c", p=EPART)).then_inc(edges_in, 16)
            load_x(2)
            load_x(3)
            load_w(wraw[:, 1, :, :], 1, w_rel[1], 0)
            for t in range(4, NT):
                load_x(t)
            for h in range(2):
                with sp.Fori(1 - h, R // 2) as i:
                    for b in range(2):
                        weight = w_rel[bass.ds(2 * i + b, 1), :, :].rearrange("a p n -> (a p) n")
                        load_unit(2 * i + (b + h * R), b, weight, h)
            for n, (weight, h) in enumerate([(w_root, 0), (w_root, 1), (w_gate[D:2 * D], 0), (w_gate[D:2 * D], 1),
                                             (w_gate[0:D], 0)]):
                load_unit(UNITS_Y + n, n % 2, weight, h)

            def load_sums(t, h):
                sp.dma_start(slot[0][:, h * HW:(h + 1) * HW], agg_d[bass.ds(t * P + h * NPAD, P), :]).then_inc(u_in, 16)

            def load_root(t):
                sp.dma_start(slot[1], rootgate_d[bass.ds(t * P, P), :]).then_inc(u_in, 16)

            def load_u(t):
                after(sp, u_ready, t)
                for h in range(2):
                    load_sums(t, h)
                load_root(t)

            def load_z(t):
                after(sp, x1_ready, t)
                sp.dma_start(slot[2], rootgate_d[bass.ds(t * P + NPAD, P), :]).then_inc(z_in, 16)
                if isinstance(t, int) and t == NT - 1:
                    sp.dma_start(slot[3][0:LAST, :], x[t * P:N, :]).then_inc(z_in, 16)
                else:
                    sp.dma_start(slot[3], x[bass.ds(t * P, P), :]).then_inc(z_in, 16)

            def spill_sums(g0, g1):
                sp.dma_start(agg_d[NPAD + g0 * P:NPAD + g1 * P, :].rearrange("(g p) n -> p g n", p=P), U[:, g0:g1, :]).then_inc(agg1_out, 16)

            for b in range(2):
                sp.wait_ge(y_out[b], 16 * (UNITS_Y + 2) * NT // 2)
            sp.wait_ge(agg_out, 16)
            sp.wait_ge(msg_split, 2 * ETILES)
            load_root(0)
            load_sums(0, 0)
            load_unit(UNITS_Y + 5, 1, w_gate[0:D], 1)
            sp.wait_ge(gemm_done, (UNITS_Y + 4) * NT)
            sp.dma_start(BIAS_ROOT[:, :], b_root.partition_broadcast(P)).then_inc(bias_in, 16)
            sp.wait_ge(pair_added, 2 * NPAIR + AHEAD)
            spill_sums(0, 4)
            sp.wait_ge(agg1_out, 16)
            load_sums(0, 1)
            spill_sums(4, NT)
            sp.dma_start(BIAS_GATE[:, :], b_gate.partition_broadcast(P)).then_inc(bias_gate_in, 16)
            load_w(gcn_raw[:, :, 0:HW], 0, w_gcn, 0)
            load_u(1)
            for b in range(2):
                sp.wait_ge(y_out[b], 16 * (UNITS_Y + 4) * NT // 2)
            sp.wait_ge(agg1_out, 32)
            load_z(0)
            sp.wait_ge(w_split, (UNITS_Y + 6) * KT)
            load_w(gcn_raw[:, :, HW:D], 1, w_gcn, 1)
            load_u(2)
            with sp.Fori(0, NT - 3) as i:
                load_z(i + 1)
                load_u(i + 3)
            load_z(NT - 2)
            load_z(NT - 1)

            sp.wait_ge(z_done, NT)
            for s in range(KT):
                sp.wait_ge(h_out, 32 * (s + 1))
                sp.dma_start(hhi[:, s, :].bitcast(F32), hhi_d[s * P:(s + 1) * P, :]).then_inc(h_in[s], 16)
                sp.dma_start(hlo[:, s, :].bitcast(F32), hlo_d[s * P:(s + 1) * P, :]).then_inc(h_in[s], 16)

            def load_c(d, b):
                after(sp, c_split, d - 1)
                sp.dma_start(CIN[b][:, :], count_d[:, bass.ds(d * NPAD, NPAD)]).then_inc(c_in[b], 16)

            def load_res(d, b):
                after(sp, out_ready, d - 1)
                sp.dma_start(slot[b], x1_d[bass.ds(d * P, P), :]).then_inc(res_in[b], 16)

            sp.wait_ge(x1_out, 16 * NT)
            sp.wait_ge(h_done, NT)
            sp.dma_start(BIAS_GCN[:, :], b_gcn.partition_broadcast(P)).then_inc(bias1_in, 16)
            for b in range(2):
                load_c(b, b)
                load_res(b, b)
            with sp.Fori(1, NT // 2) as i:
                for b in range(2):
                    load_c(2 * i + b, b)
                    load_res(2 * i + b, b)

        @block.gpsimd
        def _(pool):
            chain = Chain(pool, pool_chain)
            link = chain.link
            link(nc.gpsimd.memset(IDENT[:, :], 0.0))
            nc.gpsimd.affine_select(out=IDENT[:, :], in_=IDENT[:, :], compare_op=ALU.not_equal, fill=1.0, base=0,
                                    pattern=[[-1, P]], channel_multiplier=1).then_inc(consts, 1)
            nc.gpsimd.iota(IOTA[:, :], pattern=[[1, NPAD]], base=0, channel_multiplier=0,
                           allow_small_or_imprecise_dtypes=True).then_inc(consts, 1)
            link(nc.gpsimd.memset(EARLIER, 1.0))
            nc.gpsimd.affine_select(out=EARLIER, in_=EARLIER, compare_op=ALU.is_gt, fill=0.0, base=0,
                                    pattern=[[1, EPART]], channel_multiplier=-1).then_inc(consts, 1)
            nc.gpsimd.memset(ONES, 1.0).then_inc(consts, 1)
            nc.gpsimd.memset(MINUS_HALF[:, :], -0.5).then_inc(consts, 1)
            nc.gpsimd.iota(PAIRSUM[:, 1, :], pattern=[[PAIR, NPAIR]], base=0, channel_multiplier=0,
                           allow_small_or_imprecise_dtypes=True).then_inc(consts, 1)
            link(nc.gpsimd.memset(WGOT[:, :, :], 0.0))
            nc.gpsimd.memset(PADREC[:, :, 0:2], FAR).then_inc(pad_set, 1)
            nc.gpsimd.memset(PADREC[:, :, 2:3].bitcast(F32), -1.0).then_inc(pad_set, 1)
            nc.gpsimd.memset(PADREC[:, :, 3:4], 0).then_inc(pad_set, 1)
            pool.wait_ge(pad_set, 3)
            pool.dma_start(rec_d.rearrange("(p t) f -> p (t f)", p=P),
                           PADREC[:, :, :].rearrange("p t f -> p (t f)")).then_inc(pad_out, 16)
            pool.wait_ge(pad_out, 16)

            pool.wait_ge(pos_ready, 1)

            def scatter_half(i, b, peeled):
                if not peeled:
                    pool.wait_ge(scattered[b], i * (16 * RING))
                pool.wait_ge(pos_ready, 1)
                col = bass.ds(i * (2 * RING) + b * RING, RING)
                nc.gpsimd.tensor_copy(IDX[0:EPART, b, :], ADDR[:, col]).then_inc(idx_set, 1)
                nc.gpsimd.tensor_copy(RREC[0:EPART, b, :, :], REC[0:EPART, col, :]).then_inc(idx_set, 1)
                pool.wait_ge(idx_set, i * 4 + (2 * b + 2))
                pool.sem_inc(passed_pool, 1)
                for j in range(RING):
                    pool.indirect_dma_start(
                        out=rec_d, out_offset=bass.IndirectOffsetOnAxis(ap=IDX[0:EPART, b, j:j + 1], axis=0),
                        in_=RREC[0:EPART, b, j, :], in_offset=None).then_inc(scattered[b], 16)

            turns = ECOL // (2 * RING)
            for b in range(2):
                scatter_half(0, b, True)
            with pool.Fori(1, turns) as i:
                for b in range(2):
                    scatter_half(i, b, False)
            for b in range(2):
                pool.wait_ge(scattered[b], 16 * RING * turns)
            pool.wait_ge(chunk_ready, ECOL // CHUNK)
            pool.dma_start(REC[:, :, :].rearrange("p t f -> p (t f)"),
                           rec_d.rearrange("(p t) f -> p (t f)", p=P)).then_inc(sorted_in, 16)
            pool.wait_ge(sorted_in, 16)

            pool.wait_ge(deg_ready, 1)
            nc.gpsimd.tensor_tensor(DINV[:, :], DEG[:, :], MINUS_HALF[:, :], ALU.pow).then_inc(dinv_ready, 1)
            pool.wait_ge(inv_ready, 1)
            pool.dma_start(inv_d.rearrange("(p k) a -> p (k a)", p=P), INV[:, :]).then_inc(inv_out, 16)
            pool.wait_ge(inv_out, 16)

            IDX_BASE = 2 * 2 * turns

            def weight_half(i, b, peeled):
                tiles = bass.ds(i * (2 * RING) + b * RING, RING)
                if not peeled:
                    pool.wait_ge(w_got[b], i * (16 * RING))
                    pool.wait_ge(sorted_in, 16)
                    nc.gpsimd.tensor_copy(W_EDGE[:, bass.ds((i - 1) * (2 * RING) + b * RING, RING)], WGOT[:, b, :]).then_inc(w_ready, 1)
                    pool.wait_ge(w_ready, (i - 1) * 2 + (b + 1))
                pool.wait_ge(sorted_in, 16)
                nc.gpsimd.tensor_copy(IDX[:, b, :], REC[:, tiles, 1]).then_inc(idx_set, 1)
                pool.wait_ge(idx_set, i * 2 + (IDX_BASE + b + 1))
                pool.sem_inc(passed_pool, 1)
                for j in range(RING):
                    pool.indirect_dma_start(
                        out=WGOT[:, b, j:j + 1], out_offset=None, in_=inv_d,
                        in_offset=bass.IndirectOffsetOnAxis(ap=IDX[:, b, j:j + 1], axis=0),
                        bounds_check=P * NKEY - 1, oob_is_err=False).then_inc(w_got[b], 16)

            turns_w = ETILES // (2 * RING)
            for b in range(2):
                weight_half(0, b, True)
            with pool.Fori(1, turns_w) as i:
                for b in range(2):
                    weight_half(i, b, False)
            for b in range(2):
                pool.wait_ge(w_got[b], 16 * RING * turns_w)
                nc.gpsimd.tensor_copy(W_EDGE[:, (turns_w - 1) * 2 * RING + b * RING:(turns_w - 1) * 2 * RING + (b + 1) * RING],
                                      WGOT[:, b, :]).then_inc(w_ready, 1)
            IDX_BASE2 = IDX_BASE + 2 * turns_w

            pool.wait_ge(cells_added, NPAIR + AHEAD)
            pool.dma_start(count_d, COUNT.rearrange("p g n -> p (g n)")).then_inc(count_out, 16)

            for run in range(2):
                for b in range(2):
                    pool.wait_ge(y_out[b], 16 * R * NT // 2 * (run + 1))
                pool.wait_ge(work_clear, run + 1)

                def gather_half(i, b, peeled, run=run):
                    if not (peeled and run == 0):
                        pool.wait_ge(msg_split, i * (2 * RING) + (run * ETILES + b * RING - RING))
                    pool.wait_ge(sorted_in, 16)
                    nc.gpsimd.tensor_copy(IDX[:, b, :], REC[:, bass.ds(i * (2 * RING) + b * RING, RING), 0]).then_inc(idx_set, 1)
                    pool.wait_ge(idx_set, i * 2 + (IDX_BASE2 + run * 2 * turns_w + b + 1))
                    for j in range(RING):
                        tile = i * (2 * RING) + (run * ETILES + b * RING + j)
                        after(pool, msg_split, tile - 3)
                        pool.sem_inc(passed_pool, 1)
                        pool.indirect_dma_start(
                            out=RAWG[:, j % 4, :], out_offset=None, in_=y_d[run],
                            in_offset=bass.IndirectOffsetOnAxis(ap=IDX[:, b, j:j + 1], axis=0),
                            bounds_check=YROWS - 1, oob_is_err=False).then_inc(got[j % 4], 16)

                if run == 0:
                    pool.wait_ge(w_ready, 2 * turns_w)
                for b in range(2):
                    if run == 0 and b == 0:
                        gather_half(0, b, True)
                    else:
                        gather_half(0, b, False)
                with pool.Fori(1, turns_w) as i:
                    for b in range(2):
                        gather_half(i, b, False)
                if run == 0:
                    pool.wait_ge(pair_added, NPAIR + AHEAD)
                    pool.dma_start(agg_d[0:NPAD, :].rearrange("(g p) n -> p g n", p=P), U).then_inc(agg_out, 16)

            pool.wait_ge(bias_in, 16)

            def add_root(t):
                pool.wait_ge(u_in, t * 48 + 48)
                nc.gpsimd.tensor_tensor(slot[1], slot[1], BIAS_ROOT[:, :], ALU.add).then_inc(root_ready, 1)

            def add_gate(t):
                pool.wait_ge(z_in, t * 32 + 32)
                nc.gpsimd.tensor_tensor(slot[2], slot[2], BIAS_GATE[:, :], ALU.add).then_inc(gate_ready, 1)

            def rstd(t):
                pool.wait_ge(var_ready, t + 1)
                nc.gpsimd.tensor_tensor(RSTD[:, :], VAR[:, :], MINUS_HALF[:, 0:1], ALU.pow).then_inc(rstd_ready, 1)

            add_root(0)
            add_root(1)
            pool.wait_ge(bias_gate_in, 16)
            add_gate(0)
            rstd(0)
            add_root(2)
            with pool.Fori(0, NT - 3) as i:
                add_gate(i + 1)
                rstd(i + 1)
                add_root(i + 3)
            for t in (NT - 2, NT - 1):
                add_gate(t)
                rstd(t)
            with pool.Fori(NT, 2 * NT) as t:
                rstd(t)
            pool.wait_ge(count_out, 16)
            pool.wait_ge(agg_out, 16)
            pool.wait_ge(agg1_out, 32)

        @block.tensor
        def _(pe):
            def turn_x(t):
                pe.wait_ge(x_in[t % 2], 16 * (t // 2 + 1))
                if t == 0:
                    pe.wait_ge(consts, 1)
                for half in range(2):
                    g = 2 * t + half
                    after(pe, x_split, g - 3)
                    for j in range(4):
                        k = 4 * half + j
                        last = pe.transpose(PM[:, g % 4, j * P:(j + 1) * P], XIN[:, t % 2, k * P:(k + 1) * P], IDENT[:, :])
                    last.then_inc(x_turned, 1)

            def gemm(i, jt, b, first_unit=False):
                j, t = jt // NT, jt % NT
                q = i * TILES_BODY + jt
                bank = jt % 4
                if b == 0:
                    if t == 0 and not first_unit:
                        pe.wait_ge(w_split, i * (2 * KT) + KT * (j + 1))
                    if first_unit:
                        pe.wait_ge(x_split, 2 * (t + 1))
                    after(pe, evac_done, q - 3)
                for k in range(4 * b, 4 * b + 4):
                    if first_unit and t == 0:
                        pe.wait_ge(w_split, k + 1)
                    for n, (lhs, rhs) in enumerate(((xhi, whi), (xhi, wlo), (xlo, whi))):
                        last = pe.matmul(PG[:, bank, :], lhs[:, k, t * P:(t + 1) * P], rhs[:, j % 2, k, :],
                                         start=(k == 0 and n == 0), stop=(k == KT - 1 and n == 2))
                if b == 1:
                    last.then_inc(gemm_done, 1)

            def count_pair(i, pr):
                pair = (i - 4) * PAIRS_BODY + pr
                pe.wait_ge(hot_ready, pair + 1)
                pe.wait_ge(cells_added, pair + AHEAD)
                for e in range(2):
                    s = (2 * pr + e) % 4
                    hot = DSTHOT[:, s, :] if s < 3 else DSTHOT3[:, 0, :]
                    for c0, c1 in ((0, HW), (HW, 2 * HW), (2 * HW, NPAD)):
                        last = pe.matmul(PMALL[:, c0:c1], SRCHOT[:, s, :], hot[:, c0:c1], start=(e == 0), stop=(e == 1))
                last.then_inc(cells_done, 1)

            def message_pair(i, pr):
                pair = (i - 6) * PAIRS_BODY + pr
                pe.wait_ge(pair_ready, pair * 2 + 2)
                pe.wait_ge(msg_split, pair * 2 + 2)
                pe.wait_ge(pair_added, pair - 1 + AHEAD)
                for e in range(2):
                    for n, part in enumerate((sp_hi, sp_lo)):
                        last = pe.matmul(PM[:, pr % 2, :], ONEHOT[:, pr % 2, e, :], part[:, pr % 2, e, :],
                                         start=(e == 0 and n == 0), stop=(e == 1 and n == 1))
                last.then_inc(pair_done, 1)

            def body(i, pair_step):
                for s in range(SUBSTEPS):
                    gemm(i, s // 2, s % 2)
                    if pair_step is not None:
                        for pr in PAIRS_OF[s]:
                            pair_step(i, pr)

            pe.sem_inc(cells_done, AHEAD)
            pe.sem_inc(pair_done, AHEAD)
            turn_x(0)
            for jt in range(TILES_BODY):
                gemm(0, jt, 0, first_unit=jt < NT)
                if jt == 0:
                    turn_x(1)
                gemm(0, jt, 1, first_unit=jt < NT)
                if jt + 2 < NT:
                    turn_x(jt + 2)
                if jt == 14:
                    pe.wait_ge(rows_total, 1)
                    pe.wait_ge(consts, 4)
                    pe.matmul(PM[0:EPART, 0, 0:NT], EARLIER, T10[0:EPART, 0, :], start=True, stop=True)
                    pe.matmul(PM[:, 1, 0:NT], WORK[0:EPART, 3 * NT * ECOL + P:3 * NT * ECOL + 2 * P], T10[0:EPART, 0, :],
                              start=True, stop=True).then_inc(offsets, 1)
            for jt in range(TILES_BODY):
                gemm(1, jt, 0)
                gemm(1, jt, 1)
                if 1 <= jt <= ECOL // CHUNK:
                    c = jt - 1
                    pe.wait_ge(chunk_ready, c + 1)
                    for e in range(CHUNK):
                        last = pe.matmul(PM[:, 3, 0:NKEY], LOCHOT[0:EPART, c % 2, e, :], KEYHOT[0:EPART, c % 2, e, :],
                                         start=(c == 0 and e == 0), stop=(c == ECOL // CHUNK - 1 and e == CHUNK - 1))
                    last.then_inc(chunk_done, 1)
            with pe.Fori(2, 4) as i:
                body(i, None)
            with pe.Fori(4, 6) as i:
                body(i, count_pair)
            with pe.Fori(6, 10) as i:
                body(i, message_pair)

            def turn_u(t):
                pe.wait_ge(u_ready, t + 1)
                after(pe, u_split, t)
                for k in range(KT):
                    last = pe.transpose(PM[:, k // 4, (k % 4) * P:(k % 4 + 1) * P], slot[4][:, k * P:(k + 1) * P], IDENT[:, :])
                last.then_inc(u_turned, 1)

            def gate(t):
                pe.wait_ge(u_split, t + 1)
                after(pe, z_read, t)
                for h in range(2):
                    for k in range(KT):
                        for n, (lhs, rhs) in enumerate(((ut_hi, whi), (ut_hi, wlo), (ut_lo, whi))):
                            last = pe.matmul(PG[:, h, :], lhs[:, k * P:(k + 1) * P], rhs[:, h, k, :],
                                             start=(k == 0 and n == 0), stop=(k == KT - 1 and n == 2))
                last.then_inc(z_done, 1)

            def turn_x1(t):
                pe.wait_ge(x1_ready, t + 1)
                after(pe, x1_split, t)
                for k in range(KT):
                    last = pe.transpose(PM[:, 2 + k // 4, (k % 4) * P:(k % 4 + 1) * P], slot[6][:, k * P:(k + 1) * P], IDENT[:, :])
                last.then_inc(x1_turned, 1)

            def conv_in(t):
                pe.wait_ge(x1_split, t + 1)
                after(pe, h_split, t)
                for h in range(2):
                    for k in range(KT):
                        for n, (lhs, rhs) in enumerate(((SPHI, gcn_hi), (SPHI, gcn_lo), (SPLO, gcn_hi))):
                            last = pe.matmul(PG[:, 2 + h, :], lhs[:, k * P:(k + 1) * P], rhs[:, k, h * HW:(h + 1) * HW],
                                             start=(k == 0 and n == 0), stop=(k == KT - 1 and n == 2))
                last.then_inc(h_done, 1)

            pe.wait_ge(w_split, (UNITS_Y + 6) * KT)
            turn_u(0)
            gate(0)
            turn_u(1)
            gate(1)
            turn_x1(0)
            turn_u(2)
            pe.wait_ge(w_split, (UNITS_Y + 8) * KT)
            conv_in(0)
            turn_x1(1)
            with pe.Fori(1, NT - 2) as i:
                gate(i + 1)
                turn_u(i + 2)
                conv_in(i)
                turn_x1(i + 1)
            gate(NT - 1)
            conv_in(NT - 2)
            turn_x1(NT - 1)
            conv_in(NT - 1)

            def conv(d, b, first):
                pe.wait_ge(c_split, d + 1)
                after(pe, conv_read, d - 1)
                order = [KT, KT + 1] + list(range(KT))
                for at_s, s in enumerate(order):
                    if first and s < KT:
                        pe.wait_ge(h_in[s], 32)
                    if first and s >= KT:
                        pe.wait_ge(h_split, s + 1)
                    c_hi = XHI[:, b * NPAD + s * P:b * NPAD + (s + 1) * P]
                    c_lo = XLO[:, b * NPAD + s * P:b * NPAD + (s + 1) * P]
                    if s < KT:
                        r_hi, r_lo = hhi[:, s, :], hlo[:, s, :]
                    elif s == KT:
                        r_hi, r_lo = SPHI[:, D:2 * D], SPLO[:, D:2 * D]
                    else:
                        r_hi, r_lo = ut_hi, ut_lo
                    for n, (lhs, rhs) in enumerate(((c_hi, r_hi), (c_hi, r_lo), (c_lo, r_hi))):
                        for h in range(2):
                            last = pe.matmul(PG[:, 2 * b + h, :], lhs, rhs[:, h * HW:(h + 1) * HW],
                                             start=(at_s == 0 and n == 0), stop=(at_s == NT - 1 and n == 2))
                last.then_inc(conv_done, 1)

            for b in range(2):
                conv(b, b, b == 0)
            with pe.Fori(1, NT // 2) as i:
                for b in range(2):
                    conv(2 * i + b, b, False)

        @block.scalar
        def _(act):
            def x_high(t):
                for half in range(2):
                    g = 2 * t + half
                    act.wait_ge(x_turned, g + 1)
                    nc.scalar.activation(xhi[:, 4 * half:4 * half + 4, t * P:(t + 1) * P],
                                         PM[:, g % 4, :].rearrange("p (k n) -> p k n", k=4), ACT.Copy).then_inc(x_hi, 1)

            def w_high(k, high, raw):
                nc.scalar.activation(high[:, k, :], raw[:, k, :], ACT.Copy).then_inc(w_hi, 1)

            def evac(i, jt, dest):
                q = i * TILES_BODY + jt
                b = jt % 2
                act.wait_ge(gemm_done, q + 1)
                after(act, y_out[b], i * (16 * NT) + 16 * (jt // 2))
                nc.scalar.activation(STAGE[:, b, :], PG[:, jt % 4, :], ACT.Copy).then_inc(evac_done, 1)

            def store_y(i, jt, dest):
                q = i * TILES_BODY + jt
                b = jt % 2
                act.wait_ge(evac_done, q + 1)
                act.dma_start(dest(i, jt), STAGE[:, b, :]).then_inc(y_out[b], 16)

            def w_high_next(i, jt):
                j, k = jt // NT, jt % NT - 1
                b = (j + 1) % 2
                if 0 <= k < KT:
                    if k == 0:
                        act.wait_ge(w_in[b], i * 32 + 32)
                    w_high(k, whi[:, b, :, :], wraw[:, b, :, :])

            def msg_high(i, pr):
                for e in range(2):
                    tl = 2 * pr + e
                    tile = (i - 6) * (2 * PAIRS_BODY) + tl
                    act.wait_ge(got[tl % 4], (tile - tl % 4) * 4 + 16)
                    if e == 0:
                        act.wait_ge(pair_done, (i - 6) * PAIRS_BODY + (pr - 1 + AHEAD))
                    act.wait_ge(w_ready, 2 * (ETILES // (2 * RING)))
                    col = bass.ds(turn_tile(i, tl), 1)
                    nc.scalar.activation(sp_hi[:, pr % 2, e, :], RAWG[:, tl % 4, :], ACT.Copy,
                                         scale=W_EDGE[:, col]).then_inc(msg_hi, 1)

            def turn_tile(i, tl):
                return (i - (6 if run_of[0] == 0 else 8)) * (2 * PAIRS_BODY) + tl

            run_of = [0]

            def body(i, dest, messages):
                for s in range(SUBSTEPS):
                    if messages:
                        for pr in PAIRS_OF[s]:
                            msg_high(i, pr)
                    if s % 2 == 0 and s > 0:
                        evac(i, s // 2 - 1, dest)
                        w_high_next(i, s // 2 - 1)
                        store_y(i, s // 2 - 1, dest)
                evac(i, TILES_BODY - 1, dest)
                store_y(i, TILES_BODY - 1, dest)

            def y_dest(h):
                return lambda i, jt: y_d[h][bass.ds((i - 4 * h) * (TILES_BODY * P) + jt * P, P), :]

            def rootgate_dest(i, jt):
                return rootgate_d[bass.ds((i - 8) * NPAD + (jt % NT) * P, P), (jt // NT) * HW:(jt // NT + 1) * HW]

            x_high(0)
            for k in range(KT):
                if k == KT // 2:
                    x_high(1)
                act.wait_ge(w0_in[k], 16)
                w_high(k, whi[:, 0, :, :], wraw[:, 0, :, :])
            for jt in range(TILES_BODY):
                evac(0, jt, y_dest(0))
                store_y(0, jt, y_dest(0))
                if jt + 2 < NT:
                    x_high(jt + 2)
                w_high_next(0, jt)
            with act.Fori(1, 4) as i:
                body(i, y_dest(0), False)
            with act.Fori(4, 6) as i:
                body(i, y_dest(1), False)
            with act.Fori(6, 8) as i:
                body(i, y_dest(1), True)
            run_of[0] = 1
            with act.Fori(8, 10) as i:
                body(i, rootgate_dest, True)

            act.wait_ge(w_in[1], (UNITS_Y + 6) // 2 * 32)
            for k in range(KT):
                w_high(k, whi[:, 1, :, :], wraw[:, 1, :, :])

            def gcn_high(h):
                cols = slice(h * HW, (h + 1) * HW)
                act.wait_ge(w_in[h], (UNITS_Y + 7 + h) // 2 * 32)
                for k in range(KT):
                    w_high(k, gcn_hi[:, :, cols], gcn_raw[:, :, cols])

            def u_high(t):
                act.wait_ge(u_turned, t + 1)
                after(act, z_done, t)
                for half in range(2):
                    nc.scalar.activation(ut_hi[:, half * HW:(half + 1) * HW], PM[:, half, :], ACT.Copy).then_inc(u_hi, 1)

            def tanh_u(t):
                act.wait_ge(u_ready, t + 1)
                after(act, x1_ready, t)
                nc.scalar.activation(slot[5], slot[4], ACT.Tanh).then_inc(tanh_done, 1)

            def h_high(t, d0, d1):
                act.wait_ge(h_done, t + 1)
                act.wait_ge(dinv_ready, 1)
                for half, d_ap in ((0, d0), (1, d1)):
                    nc.scalar.activation(d_ap, PG[:, 2 + half, :], ACT.Copy, scale=DINV[:, bass.ds(t, 1)]).then_inc(h_hi, 1)

            def x1_high(t):
                act.wait_ge(x1_turned, t + 1)
                after(act, h_done, t)
                for half in range(2):
                    nc.scalar.activation(SPHI[:, half * HW:(half + 1) * HW], PM[:, 2 + half, :], ACT.Copy).then_inc(x1_hi, 1)
                act.dma_start(x1_d[bass.ds(t * P, P), :], slot[6]).then_inc(x1_out, 16)

            def h_store(t):
                act.wait_ge(h_split, t + 1)
                act.dma_start(hhi_d[bass.ds(t * P, P), :], HST_HI[:, :].bitcast(F32)).then_inc(h_out, 16)
                act.dma_start(hlo_d[bass.ds(t * P, P), :], HST_LO[:, :].bitcast(F32)).then_inc(h_out, 16)

            u_high(0)
            tanh_u(0)
            gcn_high(0)
            u_high(1)
            tanh_u(1)
            gcn_high(1)
            x1_high(0)
            for b in range(2):
                act.wait_ge(y_out[b], 16 * (UNITS_Y + 4) * NT // 2)

            def tile_body(t, staged):
                if t_in(t + 2):
                    u_high(t + 2)
                if staged:
                    after(act, h_out, t * 32)
                    h_high(t, HST_HI[:, 0:HW], HST_HI[:, HW:D])
                else:
                    place_h = SPHI[:, D:2 * D] if t == NT - 2 else ut_hi
                    h_high(t, place_h[:, 0:HW], place_h[:, HW:D])
                if t_in(t + 1):
                    x1_high(t + 1)
                if t_in(t + 2):
                    tanh_u(t + 2)
                if staged:
                    h_store(t)

            def t_in(t):
                return not isinstance(t, int) or t < NT

            tile_body(0, True)
            with act.Fori(1, NT - 2) as i:
                tile_body(i, True)
            tile_body(NT - 2, False)
            tile_body(NT - 1, False)
            act.wait_ge(h_out, 32 * KT)
            act.wait_ge(x1_out, 16 * NT)

            def store(d, b, rows):
                act.wait_ge(out_ready, d + 1)
                if rows == P:
                    act.dma_start(out[bass.ds(d * P, P), :], slot[2 + b]).then_inc(out_done[b], 16)
                else:
                    act.dma_start(out[d * P:N, :], slot[2 + b][0:rows, :]).then_inc(out_done[b], 16)

            with act.Fori(0, NT // 2 - 1) as i:
                for b in range(2):
                    store(2 * i + b, b, P)
            store(NT - 2, 0, P)
            store(NT - 1, 1, LAST)
            for b in range(2):
                act.wait_ge(out_done[b], 16 * NT // 2)

        @block.vector
        def _(dve):
            chain = Chain(dve, dve_chain)
            link = chain.link
            V = nc.vector

            def x_low(t):
                for half in range(2):
                    g = 2 * t + half
                    dve.wait_ge(x_hi, g + 1)
                    dst_ap = xlo[:, 4 * half:4 * half + 4, t * P:(t + 1) * P]
                    hi_ap = xhi[:, 4 * half:4 * half + 4, t * P:(t + 1) * P].bitcast(F32)
                    V.tensor_tensor(dst_ap, PM[:, g % 4, :].rearrange("p (k n) -> p k n", k=4), hi_ap,
                                    ALU.subtract).then_inc(x_split, 1)

            def w_low(m, k, high, low, raw):
                dve.wait_ge(w_hi, m + 1)
                V.tensor_tensor(low[:, k, :], raw[:, k, :], high[:, k, :].bitcast(F32), ALU.subtract).then_inc(w_split, 1)

            def w_low_next(i, jt):
                j, k = jt // NT, jt % NT - 1
                b = (j + 1) % 2
                if 0 <= k < KT:
                    w_low(i * (2 * KT) + (KT * (j + 1) + k), k, whi[:, b, :, :], wlo[:, b, :, :], wraw[:, b, :, :])

            def edge_fields():
                dve.wait_ge(edges_in, 48)
                V.tensor_scalar(T_GRP, T_DST, 7, None, ALU.logical_shift_right)
                link(V.tensor_scalar(T_LOC, T_DST, P - 1, None, ALU.bitwise_and))
                V.tensor_copy(T_GRPF, T_GRP)
                V.tensor_copy(T_LOCF, T_LOC)
                link(V.tensor_copy(REC[0:EPART, 0:ECOL, 2].bitcast(F32), T_LOC))
                link(V.scalar_tensor_tensor(KEY[:, :], T_GRPF, float(R), T_TYPE, ALU.mult, ALU.add))
                V.scalar_tensor_tensor(REC[0:EPART, 0:ECOL, 1], T_LOCF, float(NKEY), KEY[:, :], ALU.mult, ALU.add)
                V.scalar_tensor_tensor(REC[0:EPART, 0:ECOL, 0], T_TYPE, float(NPAD), T_SRC, ALU.mult, ALU.add)
                link(V.tensor_copy(REC[0:EPART, 0:ECOL, 3], T_SRC))

            def membership():
                for g in range(NT):
                    last = V.tensor_scalar(MEMB[:, g, :], T_GRPF, float(g), None, ALU.is_equal)
                link(last)

            def scan_step(n):
                a = MEMB if n == 0 else SCAN[(n - 1) % 2]
                b, s = SCAN[n % 2], 1 << n
                V.tensor_copy(b[:, :, 0:s], a[:, :, 0:s])
                link(V.tensor_tensor(b[:, :, s:ECOL], a[:, :, s:ECOL], a[:, :, 0:ECOL - s], ALU.add))

            SCANS = (ECOL - 1).bit_length()
            PREFIX = SCAN[(SCANS - 1) % 2]

            def group_starts():
                dve.wait_ge(offsets, 1)
                link(V.tensor_scalar(T10I[:, :], PM[:, 1, 0:NT], float(PAIR - 1), None, ALU.add))
                link(V.tensor_scalar(T10I[:, :], T10I[:, :], 8, 8, ALU.logical_shift_right, ALU.logical_shift_left))
                link(V.tensor_copy(T10[:, 1, :], T10I[:, :]))
                link(V.memset(T10[:, 2, 0:1], 0.0))
                for g in range(1, NT):
                    link(V.tensor_tensor(T10[:, 2, g:g + 1], T10[:, 2, g - 1:g], T10[:, 1, g - 1:g], ALU.add))
                link(V.scalar_tensor_tensor(T10[0:EPART, 3, :], PM[0:EPART, 0, 0:NT], -1.0, T10[0:EPART, 2, :], ALU.add, ALU.add))

            def positions_a():
                link(V.tensor_tensor(PREFIX, PREFIX, T10[0:EPART, 3, :].unsqueeze(2).to_broadcast([EPART, NT, ECOL]), ALU.add))
                link(V.tensor_tensor(PREFIX, PREFIX, MEMB, ALU.mult))

            def positions_b():
                link(V.tensor_reduce(O_POS, PREFIX.rearrange("p g c -> p c g"), AXIS_X, ALU.add))
                link(V.tensor_copy(O_POSI, O_POS))
                V.tensor_scalar(O_LANE, O_POSI, P - 1, None, ALU.bitwise_and)
                link(V.tensor_scalar(O_TILE, O_POSI, 7, None, ALU.logical_shift_right))
                V.scalar_tensor_tensor(ADDR[:, :], O_LANE, float(ETILES), O_TILE, ALU.mult, ALU.add).then_inc(pos_ready, 1)

            def pair_groups():
                dve.wait_ge(consts, 6)
                link(V.memset(PAIRSUM[:, 0, :], 0.0))
                for g in range(1, NT):
                    link(V.scalar_tensor_tensor(PAIRSUM[:, 0, :], PAIRSUM[:, 1, :], T10[0:1, 2, g:g + 1], PAIRSUM[:, 0, :],
                                                ALU.is_ge, ALU.add))
                link(V.tensor_copy(GROUP[:, :], PAIRSUM[:, 0, :]))

            def sort_step(n):
                if n == 0:
                    edge_fields()
                elif n == 1:
                    membership()
                elif n - 2 < SCANS:
                    scan_step(n - 2)
                elif n == SCANS + 2:
                    V.tensor_copy(T10[0:EPART, 0, :], PREFIX[:, :, ECOL - 1]).then_inc(rows_total, 1)
                elif n == 15:
                    group_starts()
                elif n == 16:
                    positions_a()
                elif n == 17:
                    positions_b()
                elif n == 18:
                    pair_groups()

            def hot_chunk(c):
                if c == 0:
                    dve.wait_ge(pad_out, 16)
                if c >= 2:
                    dve.wait_ge(chunk_done, c - 1)
                cols = slice(c * CHUNK, (c + 1) * CHUNK)
                V.tensor_tensor(LOCHOT[0:EPART, c % 2, :, :], IOTA[0:EPART, 0:P].unsqueeze(1).to_broadcast([EPART, CHUNK, P]),
                                REC[0:EPART, cols, 2].bitcast(F32).unsqueeze(2).to_broadcast([EPART, CHUNK, P]), ALU.is_equal)
                V.tensor_tensor(KEYHOT[0:EPART, c % 2, :, :], IOTA[0:EPART, 0:NKEY].unsqueeze(1).to_broadcast([EPART, CHUNK, NKEY]),
                                KEY[:, cols].unsqueeze(2).to_broadcast([EPART, CHUNK, NKEY]), ALU.is_equal).then_inc(chunk_ready, 1)


            def inverse_counts():
                dve.wait_ge(chunk_done, ECOL // CHUNK)
                link(V.tensor_scalar(INV[:, :], PM[:, 3, 0:NKEY], 1.0, None, ALU.max))
                V.reciprocal(INV[:, :], INV[:, :]).then_inc(inv_ready, 1)
                link(V.tensor_reduce(DEG[:, :], PM[:, 3, 0:NKEY].rearrange("p (g r) -> p g r", g=NT), AXIS_X, ALU.add))
                V.tensor_scalar(DEG[:, :], DEG[:, :], 1.0, None, ALU.add).then_inc(deg_ready, 1)

            def count_setup():
                dve.wait_ge(sorted_in, 16)
                t_loc = WORK[:, 0:ETILES].bitcast(I32)
                t_grp = WORK[:, ETILES:2 * ETILES].bitcast(I32)
                V.tensor_scalar(t_loc, REC[:, :, 3], P - 1, None, ALU.bitwise_and)
                link(V.tensor_scalar(t_grp, REC[:, :, 3], 7, None, ALU.logical_shift_right))
                V.tensor_copy(SRC_LOC[:, :], t_loc)
                link(V.scalar_tensor_tensor(CELL[:, :], t_grp, float(P), REC[:, :, 2].bitcast(F32), ALU.mult, ALU.add))
                link(V.memset(WORK[:, 0:NT * NPAD // 2].bitcast(I32), 0))
                for g in range(NT):
                    last = V.tensor_copy(COUNT[:, g, g * P:(g + 1) * P], IDENT[:, :])
                link(last)

            def count_hot(i, pr):
                dve.wait_ge(cells_done, (i - 4) * PAIRS_BODY + (pr - 1 + AHEAD))
                for e in range(2):
                    s = (2 * pr + e) % 4
                    tile = bass.ds((i - 4) * (2 * PAIRS_BODY) + (2 * pr + e), 1)
                    hot = DSTHOT[:, s, :] if s < 3 else DSTHOT3[:, 0, :]
                    V.tensor_scalar(SRCHOT[:, s, :], IOTA[:, 0:P], SRC_LOC[:, tile], None, ALU.is_equal)
                    last = V.tensor_scalar(hot, IOTA[:, :], CELL[:, tile], None, ALU.is_equal)
                last.then_inc(hot_ready, 1)

            def group_of(pair):
                return dve.value_load(GROUP[0:1, bass.ds(pair, 1)], min_val=0, max_val=NT - 1)

            def count_add(i, pr):
                pair = (i - 4) * PAIRS_BODY + pr
                g = group_of(pair)
                dve.wait_ge(cells_done, pair + 1 + AHEAD)
                acc = COUNT[:, bass.ds(g, 1), :].rearrange("p a n -> p (a n)")
                V.tensor_tensor(acc, acc, PMALL[:, 0:NPAD], ALU.add).then_inc(cells_added, 1)
                dve.wait_ge(cells_added, pair + 1 + AHEAD)

            def msg_low(i, pr, run):
                for e in range(2):
                    col = bass.ds((i - (6 + 2 * run)) * (2 * PAIRS_BODY) + (2 * pr + e), 1)
                    V.tensor_scalar(ONEHOT[:, pr % 2, e, :], IOTA[:, 0:P], REC[:, col, 2].bitcast(F32), None,
                                    ALU.is_equal).then_inc(pair_ready, 1)
                for e in range(2):
                    tl = 2 * pr + e
                    tile = (i - 6) * (2 * PAIRS_BODY) + tl
                    col = bass.ds((i - (6 + 2 * run)) * (2 * PAIRS_BODY) + tl, 1)
                    dve.wait_ge(msg_hi, tile + 1)
                    V.scalar_tensor_tensor(sp_lo[:, pr % 2, e, :], RAWG[:, tl % 4, :], W_EDGE[:, col],
                                           sp_hi[:, pr % 2, e, :].bitcast(F32), ALU.mult, ALU.subtract).then_inc(msg_split, 1)

            def msg_add(i, pr, run):
                pair = (i - 6) * PAIRS_BODY + pr
                g = group_of((i - (6 + 2 * run)) * PAIRS_BODY + pr)
                dve.wait_ge(pair_done, pair + 1 + AHEAD)
                acc = U[:, bass.ds(g, 1), :].rearrange("p a n -> p (a n)")
                V.tensor_tensor(acc, acc, PM[:, pr % 2, :], ALU.add).then_inc(pair_added, 1)
                dve.wait_ge(pair_added, pair + 1 + AHEAD)

            def body(i, prepare, add):
                for s in range(SUBSTEPS):
                    if prepare is not None:
                        for pr in PAIRS_OF[s]:
                            prepare(i, pr)
                            if pr > 0:
                                add(i, pr - 1)
                    if s % 2 == 0 and s > 0:
                        w_low_next(i, s // 2 - 1)
                if add is not None:
                    add(i, PAIRS_BODY - 1)

            dve.sem_inc(pair_added, AHEAD)
            dve.sem_inc(cells_added, AHEAD)
            x_low(0)
            for k in range(KT):
                if k == KT // 2:
                    x_low(1)
                w_low(k, k, whi[:, 0, :, :], wlo[:, 0, :, :], wraw[:, 0, :, :])
            for jt in range(TILES_BODY):
                if jt + 2 < NT:
                    x_low(jt + 2)
                w_low_next(0, jt)
                sort_step(jt)
            dve.wait_ge(consts, 2)
            for jt in range(TILES_BODY):
                w_low_next(1, jt)
                if jt < ECOL // CHUNK:
                    hot_chunk(jt)
                if jt == ECOL // CHUNK + 2:
                    inverse_counts()
            with dve.Fori(2, 4) as i:
                body(i, None, None)
            count_setup()
            with dve.Fori(4, 6) as i:
                body(i, count_hot, count_add)
            dve.wait_ge(count_out, 16)
            V.memset(WORK[:, NT * HW:7 * D], 0.0)
            V.memset(WORK[:, 0:NT * HW], 0.0).then_inc(work_clear, 1)
            dve.wait_ge(work_clear, 1)
            with dve.Fori(6, 8) as i:
                body(i, lambda a, b: msg_low(a, b, 0), lambda a, b: msg_add(a, b, 0))
            dve.wait_ge(agg_out, 16)
            V.memset(WORK[:, 0:NT * HW], 0.0).then_inc(work_clear, 1)
            dve.wait_ge(work_clear, 2)
            with dve.Fori(8, 10) as i:
                body(i, lambda a, b: msg_low(a, b, 1), lambda a, b: msg_add(a, b, 1))

            for k in range(KT):
                w_low((UNITS_Y + 5) * KT + k, k, whi[:, 1, :, :], wlo[:, 1, :, :], wraw[:, 1, :, :])

            def gcn_low(h):
                cols = slice(h * HW, (h + 1) * HW)
                for k in range(KT):
                    w_low((UNITS_Y + 6 + h) * KT + k, k, gcn_hi[:, :, cols], gcn_lo[:, :, cols], gcn_raw[:, :, cols])

            def make_u(t):
                dve.wait_ge(root_ready, t + 1)
                after(dve, u_turned, t)
                after(dve, tanh_done, t)
                V.tensor_tensor(slot[4], slot[0], slot[1], ALU.add).then_inc(u_ready, 1)

            def u_low(t):
                dve.wait_ge(u_hi, t * 2 + 2)
                V.tensor_tensor(ut_lo[:, 0:HW], PM[:, 0, :], ut_hi[:, 0:HW].bitcast(F32), ALU.subtract)
                V.tensor_tensor(ut_lo[:, HW:D], PM[:, 1, :], ut_hi[:, HW:D].bitcast(F32), ALU.subtract).then_inc(u_split, 1)

            def norm(y, ready, t):
                for h in range(2):
                    last = V.bn_stats(STATS[:, h, :], y[:, h * HW:(h + 1) * HW])
                link(last)
                dve.sem_inc(passed_dve, 1)
                link(V.bn_aggr(MV[:, :], STATS[:, :, :].rearrange("p a b -> p (a b)")))
                V.tensor_scalar(VAR[:, :], MV[:, 1:2], EPS, None, ALU.add).then_inc(var_ready, 1)
                dve.wait_ge(rstd_ready, t + 1)
                V.tensor_scalar(y, y, MV[:, 0:1], RSTD[:, 0:1], ALU.subtract, ALU.mult).then_inc(ready, 1)

            def make_x1(t):
                dve.wait_ge(tanh_done, t + 1)
                dve.wait_ge(gate_ready, t + 1)
                V.tensor_tensor(slot[5], slot[5], slot[3], ALU.subtract)
                dve.wait_ge(z_done, t + 1)
                V.tensor_tensor(slot[2][:, 0:HW], PG[:, 0, :], slot[2][:, 0:HW], ALU.add)
                V.tensor_tensor(slot[2][:, HW:D], PG[:, 1, :], slot[2][:, HW:D], ALU.add).then_inc(z_read, 1)
                dve.wait_ge(z_read, t + 1)
                after(dve, x1_turned, t)
                after(dve, x1_out, t * 16)
                link(V.tensor_tensor(slot[2], slot[2], slot[5], ALU.mult))
                link(V.scalar_tensor_tensor(slot[6], slot[3], 2.0, slot[2], ALU.mult, ALU.add))
                norm(slot[6], x1_ready, t)

            def h_low(t, high, low):
                dve.wait_ge(h_hi, t * 2 + 2)
                sc = DINV[:, bass.ds(t, 1)]
                V.scalar_tensor_tensor(low[:, 0:HW], PG[:, 2, :], sc, high[:, 0:HW].bitcast(F32), ALU.mult, ALU.subtract)
                V.scalar_tensor_tensor(low[:, HW:D], PG[:, 3, :], sc, high[:, HW:D].bitcast(F32), ALU.mult,
                                       ALU.subtract).then_inc(h_split, 1)

            def x1_low(t):
                dve.wait_ge(x1_hi, t * 2 + 2)
                V.tensor_tensor(SPLO[:, 0:HW], PM[:, 2, :], SPHI[:, 0:HW].bitcast(F32), ALU.subtract)
                V.tensor_tensor(SPLO[:, HW:D], PM[:, 3, :], SPHI[:, HW:D].bitcast(F32), ALU.subtract).then_inc(x1_split, 1)

            X1_STEPS = 4
            make_u(0)
            u_low(0)
            make_u(1)
            gcn_low(0)
            u_low(1)
            make_x1(0)
            make_u(2)
            gcn_low(1)
            x1_low(0)
            with dve.Fori(0, NT - 3) as i:
                chain.enter(i, X1_STEPS)
                u_low(i + 2)
                make_x1(i + 1)
                h_low(i, HST_HI[:, :], HST_LO[:, :])
                x1_low(i + 1)
                make_u(i + 3)
            chain.leave(NT - 3, X1_STEPS)
            u_low(NT - 1)
            make_x1(NT - 2)
            h_low(NT - 3, HST_HI[:, :], HST_LO[:, :])
            x1_low(NT - 2)
            make_x1(NT - 1)
            h_low(NT - 2, SPHI[:, D:2 * D], SPLO[:, D:2 * D])
            x1_low(NT - 1)
            h_low(NT - 1, ut_hi, ut_lo)

            def counts_split(d, b):
                dve.wait_ge(c_in[b], (d - b) * 8 + 16)
                dve.wait_ge(h_done, NT)
                after(dve, conv_done, d - 1)
                hi = XHI[:, b * NPAD:(b + 1) * NPAD]
                link(V.tensor_copy(hi, CIN[b][:, :]))
                V.tensor_tensor(XLO[:, b * NPAD:(b + 1) * NPAD], CIN[b][:, :], hi.bitcast(F32), ALU.subtract).then_inc(c_split, 1)

            def finish(d, b):
                y = slot[2 + b]
                dve.wait_ge(conv_done, d + 1)
                after(dve, out_done[b], (d - b) * 8)
                for h in range(2):
                    last = V.scalar_tensor_tensor(y[:, h * HW:(h + 1) * HW], PG[:, 2 * b + h, :], DINV[:, bass.ds(d, 1)],
                                                  BIAS_GCN[:, h * HW:(h + 1) * HW], ALU.mult, ALU.add)
                last.then_inc(conv_read, 1)
                dve.wait_ge(conv_read, d + 1)
                dve.wait_ge(res_in[b], (d - b) * 8 + 16)
                link(V.scalar_tensor_tensor(y, y, 0.0, slot[b], ALU.max, ALU.add))
                norm(y, out_ready, d + NT)

            counts_split(0, 0)
            counts_split(1, 1)
            dve.wait_ge(bias1_in, 16)
            finish(0, 0)

            def two_tiles(i):
                counts_split(2 * i + 2, 0)
                finish(2 * i + 1, 1)
                counts_split(2 * i + 3, 1)
                finish(2 * i + 2, 0)

            two_tiles(0)
            with dve.Fori(1, NT // 2 - 1) as i:
                chain.enter(i - 1, 8)
                two_tiles(i)
            chain.leave(NT // 2 - 2, 8)
            finish(NT - 1, 1)


_INS = ['x', 'src', 'dst', 'edge_type_8', 'L0_gnn_weight', 'L0_gnn_root', 'L0_gnn_bias', 'L0_gnn_w_gate', 'L0_gnn_b_gate',
        'L1_gnn_W', 'L1_gnn_b']
_OUTS = [((N, D), 'float32')]


def kernel(**inputs):
    import numpy as _np
    import concourse.bacc as _bacc
    from concourse import mybir as _mybir
    from concourse.bass_utils import run_bass_kernel_spmd as _run

    nc = _bacc.Bacc("TRN2", target_bir_lowering=False, num_devices=1)
    arrays, args = {}, []
    for name in _INS:
        a = _np.ascontiguousarray(inputs[name])
        arrays[f"in_{name}_dram"] = a
        args.append(nc.dram_tensor(f"in_{name}_dram", a.shape, _mybir.dt.from_np(a.dtype), kind="ExternalInput").ap())
    for i, (shape, dtype) in enumerate(_OUTS):
        dt = _mybir.dt.from_np(_np.dtype(dtype))
        args.append(nc.dram_tensor(f"out_{i}_dram", shape, dt, kind="ExternalOutput").ap())
    gnn_resnorm_kernel(nc, *args)
    r = _run(nc, [arrays], core_ids=[0])
    return r.results[0]["out_0_dram"]
```

```python
import concourse.bass as bass
from concourse import mybir
from contextlib import ExitStack

F32 = mybir.dt.float32
F32R = mybir.dt.float32r
F16 = mybir.dt.float16
I32 = mybir.dt.int32
I16 = mybir.dt.int16
ALU = mybir.AluOpType
ACT = mybir.ActivationFunctionType
AXIS_X = mybir.AxisListType.X

P = 128
N, D, R, E = 1250, 1024, 8, 20000
NT = (N + P - 1) // P
NPAD = NT * P
LAST = N - (NT - 1) * P
KT = D // P
HW = 512
EPART, ECOL = 125, E // 125
PAIR = 2 * P
NPAIR = (E + NT * (PAIR - 1)) // PAIR
ETILES = 2 * NPAIR
NKEY = NT * R
FAR = 1 << 20
RING = 8
EPS = 1e-5

UNITS_Y = 2 * R
TILES_BODY = 2 * NT
SUBSTEPS = 2 * TILES_BODY
YROWS = R * NPAD
AHEAD = 2


COUNT_AT = (3, 0)
RUN0_AT = (5, 20)
RUN1_BODY = 8
SETUP_AT = (2, 32)
LATE = 4
DENSE = NPAIR // 2


def dense_pairs():
    steps = SUBSTEPS - LATE
    bounds = [0] * LATE + [k * DENSE // steps for k in range(steps + 1)]
    return [range(bounds[s], bounds[s + 1]) for s in range(SUBSTEPS)]


DENSE_PAIRS = dense_pairs()


def one_each(eng, at, step, last=None):
    body, s0 = at
    with eng.Fori(body, body + 2) as i:
        for n in range(SUBSTEPS):
            step(i, s0 + n, [((i - body) * SUBSTEPS + n, n)])
        if last is not None:
            last((i - body) * SUBSTEPS + (SUBSTEPS - 1), SUBSTEPS - 1)
    rest = NPAIR - 2 * SUBSTEPS
    for n in range(rest):
        step(body + 2, s0 + n, [(2 * SUBSTEPS + n, n)])
    if last is not None:
        last(NPAIR - 1, rest - 1)


def dense(eng, body, step, last=None):
    with eng.Fori(body, body + 2) as i:
        for s in range(SUBSTEPS):
            step(i, s, [((i - body) * DENSE + n, n) for n in DENSE_PAIRS[s]])
        if last is not None:
            last((i - body) * DENSE + (DENSE - 1), DENSE - 1)


def plain(start, end, step):
    for n in range(start[0] * SUBSTEPS + start[1], end[0] * SUBSTEPS + end[1]):
        step(n // SUBSTEPS, n % SUBSTEPS, [])


def phase_end(at):
    return at[0] + (at[1] + NPAIR) // SUBSTEPS, (at[1] + NPAIR) % SUBSTEPS


def normal(i, s):
    return (i + s // SUBSTEPS if s >= SUBSTEPS else i), s % SUBSTEPS


class Chain:

    def __init__(self, eng, sem):
        self.eng, self.sem, self.at, self.steps = eng, sem, 0, 0

    def link(self, ins):
        ins.then_inc(self.sem, 1)
        self.at = self.at + 1
        self.steps += 1
        self.eng.wait_ge(self.sem, self.at)

    def enter(self, turn, per_turn):
        self.before, self.steps = self.at, 0
        self.at = turn * per_turn + self.before

    def leave(self, turns, per_turn):
        assert self.steps == per_turn, (self.steps, per_turn)
        self.at = self.before + turns * per_turn


def gnn_resnorm_kernel(nc, x, src, dst, edge_type, w_rel, w_root, b_root, w_gate, b_gate, w_gcn, b_gcn, out):
    def dram(name, shape, dt=F32):
        return nc.dram_tensor(name, shape, dt, kind="Internal").ap()

    y_d = dram("y", ((UNITS_Y + 4) * NPAD, HW))
    agg_d = dram("agg", (2 * NPAD, HW))
    x1_d = dram("x1", (NPAD, D))
    count_d = dram("edge_count", (P, NT * NPAD), I16)
    hhi_d = dram("h_hi", (KT * P, D))
    hlo_d = dram("h_lo", (KT * P, D))
    rec_d = dram("records", (P * ETILES, 4), I32)
    inv_d = dram("inverse_count", (P * NKEY, 1))

    ctx = ExitStack()
    with ctx:
        KB = 1024
        base = (nc.sbuf_base + 63) // 64 * 64
        at = {}
        for name, size in (("xt_hi", KT * NPAD * 4), ("xt_lo", KT * NPAD * 4), ("w_hi", 32 * KB), ("w_lo", 32 * KB),
                           ("work", 28 * KB), ("split_hi", 8 * KB), ("split_lo", 8 * KB), ("raw_w", 4 * KB),
                           ("stage", 4 * KB), ("onehot", 2 * KB)):
            at[name] = base
            base += size

        def place(name, shape, dt, where, skip=0):
            return nc.alloc_sbuf_tensor_at(name, shape, dt, offset=at[where] + skip)

        def small(name, shape, dt):
            nonlocal base
            t = nc.alloc_sbuf_tensor_at(name, shape, dt, offset=base)
            size = mybir.dt.size(dt)
            for s in shape[1:]:
                size *= s
            base += (size + 31) // 32 * 32
            return t

        XHI = place("XHI", [P, KT * NPAD], F32R, "xt_hi")
        XLO = place("XLO", [P, KT * NPAD], F32R, "xt_lo")
        WHI = place("WHI", [P, 2 * KT * HW], F32R, "w_hi")
        WLO = place("WLO", [P, 2 * KT * HW], F32R, "w_lo")
        WORK = place("WORK", [P, 7 * D], F32, "work")
        SPHI = place("SPHI", [P, 2 * D], F32R, "split_hi")
        SPLO = place("SPLO", [P, 2 * D], F32R, "split_lo")
        STAGE = place("STAGE", [P, 2, HW], F32, "stage")
        ONEHOT = place("ONEHOT", [P, 2, 2, P], F32R, "onehot")
        xhi = XHI[:, :].rearrange("p (k n) -> p k n", k=KT)
        xlo = XLO[:, :].rearrange("p (k n) -> p k n", k=KT)
        GCN = 2 * KT * HW
        gcn_hi = XHI[:, 0:GCN].rearrange("p (k n) -> p k n", k=KT)
        gcn_lo = XLO[:, 0:GCN].rearrange("p (k n) -> p k n", k=KT)
        UT = GCN
        ut_hi, ut_lo = XHI[:, UT:UT + D], XLO[:, UT:UT + D]
        BIAS_ROOT = place("BIAS_ROOT", [P, D], F32, "xt_hi", (UT + D) * 4)
        BIAS_GATE = place("BIAS_GATE", [P, D], F32, "xt_lo", (UT + D) * 4)
        BIAS_GCN = place("BIAS_GCN", [P, D], F32, "xt_hi", 4 * NPAD * 4)
        wraw = place("WRAW", [P, 2 * KT * HW], F32, "w_lo")[:, :].rearrange("p (b k n) -> p b k n", b=2, k=KT)
        gcn_raw = place("GCNRAW", [P, GCN], F32, "xt_lo")[:, :].rearrange("p (k n) -> p k n", k=KT)
        whi = WHI[:, :].rearrange("p (b k n) -> p b k n", b=2, k=KT)
        wlo = WLO[:, :].rearrange("p (b k n) -> p b k n", b=2, k=KT)
        hhi = WHI[:, :].rearrange("p (s n) -> p s n", s=KT)
        hlo = WLO[:, :].rearrange("p (s n) -> p s n", s=KT)
        sp_hi = SPHI[:, :].rearrange("p (r e n) -> p r e n", r=2, e=2)
        sp_lo = SPLO[:, :].rearrange("p (r e n) -> p r e n", r=2, e=2)
        HST_HI = place("HST_HI", [P, D], F32R, "stage")
        HST_LO = place("HST_LO", [P, D], F32R, "raw_w")
        CIN = [place("CIN0", [P, NPAD], I16, "stage"), place("CIN1", [P, NPAD], I16, "raw_w")]
        U = WORK[:, 0:NT * HW].rearrange("p (g n) -> p g n", g=NT)
        COUNT = WORK[:, 0:NT * NPAD // 2].bitcast(I16).rearrange("p (g n) -> p g n", g=NT)
        RAWG = WORK[:, 5 * D:7 * D].rearrange("p (r n) -> p r n", r=4)
        XIN = WORK[:, 5 * D:7 * D].rearrange("p (r n) -> p r n", r=2)
        slot = [WORK[:, s * D:(s + 1) * D] for s in (5, 6, 2, 3, 0, 1, 4)]
        CHUNK = 16
        KEYHOT = place("KEYHOT", [P, 2, CHUNK, NKEY], F16, "split_hi")
        LOCHOT = place("LOCHOT", [P, 2, CHUNK, P], F16, "split_lo")
        DSTHOT = place("DSTHOT", [P, 3, NPAD], F16, "split_hi")
        DSTHOT3 = place("DSTHOT3", [P, 1, NPAD], F16, "split_lo")
        SRCHOT = place("SRCHOT", [P, 4, P], F16, "split_lo", 2 * NPAD)
        PADREC = place("PADREC", [P, ETILES, 4], I32, "split_hi")
        MEMB = WORK[0:EPART, 0:NT * ECOL].rearrange("p (g c) -> p g c", g=NT)
        SCAN = [WORK[0:EPART, (1 + b) * NT * ECOL:(2 + b) * NT * ECOL].rearrange("p (g c) -> p g c", g=NT) for b in range(2)]

        def temp(n, dt=F32):
            return WORK[0:EPART, NT * ECOL + n * ECOL:NT * ECOL + (n + 1) * ECOL].bitcast(dt)

        T_SRC, T_DST, T_TYPE, T_LOC, T_GRP, T_GRPF = temp(0, I32), temp(1, I32), temp(2, I32), temp(3, I32), temp(4, I32), temp(5)
        T_LOCF = temp(6)
        O_POS = temp(0)
        O_POSI, O_LANE, O_TILE = temp(1, I32), temp(2, I32), temp(3, I32)
        EARLIER = WORK[0:EPART, 3 * NT * ECOL:3 * NT * ECOL + EPART]
        ONES = WORK[0:EPART, 3 * NT * ECOL + P:3 * NT * ECOL + 2 * P]
        KEY = place("KEY", [EPART, ECOL], F32, "onehot")

        REC = small("REC", [P, ETILES, 4], I32)
        W_EDGE = small("W_EDGE", [P, ETILES], F32)
        SRC_LOC = small("SRC_LOC", [P, ETILES], F32)
        CELL = small("CELL", [P, ETILES], F32)
        ADDR = small("ADDR", [EPART, ECOL], I32)
        IOTA = small("IOTA", [P, NPAD], F16)
        IDENT = small("IDENT", [P, P], F32)
        IDX = small("IDX", [P, 2, RING], I32)
        RREC = small("RREC", [P, 2, RING, 4], I32)
        WGOT = small("WGOT", [P, 2, RING], F32)
        GROUP = small("GROUP", [1, NPAIR], I32)
        INV = small("INV", [P, NKEY], F32)
        DINV = small("DINV", [P, NT], F32)
        T10 = place("T10", [P, 4, NT], F32, "onehot", 768)
        T10I = place("T10I", [P, NT], I32, "onehot", 928)
        DEG = place("DEG", [P, NT], F32, "onehot", 1792)
        STATS = small("STATS", [P, 2, 6], F32)
        MV = small("MV", [P, 2], F32)
        VAR = small("VAR", [P, 1], F32)
        RSTD = small("RSTD", [P, 1], F32)
        MINUS_HALF = small("MINUS_HALF", [P, NT], F32)
        assert base <= nc.sbuf_usable_end, (base, nc.sbuf_usable_end)
        PAIRSUM = place("PAIRSUM", [1, 2, NPAIR], F32, "onehot", 1024)

        PG = ctx.enter_context(nc.psum_tensor("PG", [P, 4, HW], F32))
        PM = ctx.enter_context(nc.psum_tensor("PM", [P, 4, HW], F32))
        PMALL = PM[:, :, :].rearrange("p b n -> p (b n)")

        def sem(name):
            return ctx.enter_context(nc.semaphore(name))

        x_in = [sem(f"x_in{b}") for b in range(2)]
        x_turned = sem("x_turned")
        x_hi = sem("x_hi")
        x_split = sem("x_split")
        w0_in = [sem(f"w0_in{k}") for k in range(KT)]
        w_in = [sem(f"w_in{b}") for b in range(2)]
        w_hi = sem("w_hi")
        w_split = sem("w_split")
        gemm_done = sem("gemm_done")
        evac_done = sem("evac_done")
        y_out = [sem(f"y_out{b}") for b in range(2)]
        edges_in = sem("edges_in")
        consts = sem("consts")
        rows_total = sem("rows_total")
        offsets = sem("offsets")
        pos_ready = sem("pos_ready")
        pad_set = sem("pad_set")
        pad_out = sem("pad_out")
        idx_set = sem("idx_set")
        scattered = [sem(f"scattered{b}") for b in range(2)]
        sorted_in = sem("sorted_in")
        chunk_ready = sem("chunk_ready")
        chunk_done = sem("chunk_done")
        inv_ready = sem("inv_ready")
        inv_out = sem("inv_out")
        w_got = [sem(f"w_got{b}") for b in range(2)]
        w_ready = sem("w_ready")
        deg_ready = sem("deg_ready")
        dinv_ready = sem("dinv_ready")
        hot_ready = sem("hot_ready")
        cells_done = sem("cells_done")
        cells_added = sem("cells_added")
        count_out = sem("count_out")
        work_clear = sem("work_clear")
        got = [sem(f"got{b}") for b in range(4)]
        msg_hi = sem("msg_hi")
        msg_split = sem("msg_split")
        pair_ready = sem("pair_ready")
        pair_done = sem("pair_done")
        pair_added = sem("pair_added")
        agg_out = sem("agg_out")
        agg1_out = sem("agg1_out")
        bias_in = sem("bias_in")
        bias_gate_in = sem("bias_gate_in")
        u_in = sem("u_in")
        z_in = sem("z_in")
        root_ready = sem("root_ready")
        gate_ready = sem("gate_ready")
        u_ready = sem("u_ready")
        u_turned = sem("u_turned")
        u_hi = sem("u_hi")
        u_split = sem("u_split")
        tanh_done = sem("tanh_done")
        z_done = sem("z_done")
        z_read = sem("z_read")
        x1_ready = sem("x1_ready")
        x1_turned = sem("x1_turned")
        x1_hi = sem("x1_hi")
        x1_split = sem("x1_split")
        x1_out = sem("x1_out")
        var_ready = sem("var_ready")
        rstd_ready = sem("rstd_ready")
        h_done = sem("h_done")
        h_hi = sem("h_hi")
        h_split = sem("h_split")
        h_out = sem("h_out")
        h_in = [sem(f"h_in{s}") for s in range(KT)]
        c_in = [sem(f"c_in{b}") for b in range(2)]
        c_split = sem("c_split")
        conv_done = sem("conv_done")
        conv_read = sem("conv_read")
        res_in = [sem(f"res_in{b}") for b in range(2)]
        bias1_in = sem("bias1_in")
        out_ready = sem("out_ready")
        out_done = [sem(f"out_done{b}") for b in range(2)]
        passed_pool = sem("passed_pool")
        passed_dve = sem("passed_dve")
        dve_chain = sem("dve_chain")
        pool_chain = sem("pool_chain")

        block = ctx.enter_context(nc.Block())

        def after(eng, s, value):
            if not (isinstance(value, int) and value <= 0):
                eng.wait_ge(s, value)

        @block.sync
        def _(sp):
            def load_w(raw, b, weight, h):
                for c in range(2):
                    rows = weight[c * (D // 2):(c + 1) * (D // 2), h * HW:(h + 1) * HW]
                    sp.dma_start(raw[:, c * (KT // 2):(c + 1) * (KT // 2), :],
                                 rows.rearrange("(k p) n -> p k n", p=P)).then_inc(w_in[b], 16)

            def load_unit(n, b, weight, h):
                sp.wait_ge(gemm_done, (n - 1) * NT)
                load_w(wraw[:, b, :, :], b, weight, h)

            def load_x(t):
                if t >= 2:
                    sp.wait_ge(x_turned, 2 * (t - 1))
                rows = min(P, N - t * P)
                sp.dma_start(XIN[0:rows, t % 2, :], x[t * P:t * P + rows, :]).then_inc(x_in[t % 2], 16)

            def first_unit(k):
                sp.dma_start(wraw[:, 0, k, :], w_rel[0][k * P:(k + 1) * P, 0:HW]).then_inc(w0_in[k], 16)

            load_x(0)
            for k in range(KT // 2):
                first_unit(k)
            load_x(1)
            for k in range(KT // 2, KT):
                first_unit(k)
            for temp_i, a in ((T_SRC, src), (T_DST, dst), (T_TYPE, edge_type)):
                sp.dma_start(temp_i, a.rearrange("(p c) -> p c", p=EPART)).then_inc(edges_in, 16)
            load_x(2)
            load_x(3)
            load_w(wraw[:, 1, :, :], 1, w_rel[1], 0)
            for t in range(4, NT):
                load_x(t)
            for h in range(2):
                with sp.Fori(1 - h, R // 2) as i:
                    for b in range(2):
                        weight = w_rel[bass.ds(2 * i + b, 1), :, :].rearrange("a p n -> (a p) n")
                        load_unit(2 * i + (b + h * R), b, weight, h)
            for n, (weight, h) in enumerate([(w_root, 0), (w_root, 1), (w_gate[D:2 * D], 0), (w_gate[D:2 * D], 1),
                                             (w_gate[0:D], 0)]):
                load_unit(UNITS_Y + n, n % 2, weight, h)

            root_d, gate_d = (y_d[u * NPAD:(u + 2) * NPAD, :].rearrange("(h n) c -> n h c", h=2) for u in (UNITS_Y, UNITS_Y + 2))

            def load_sums(t, h):
                sp.dma_start(slot[0][:, h * HW:(h + 1) * HW], agg_d[bass.ds(t * P + h * NPAD, P), :]).then_inc(u_in, 16)

            def load_root(t):
                sp.dma_start(slot[1].rearrange("p (h n) -> p h n", h=2), root_d[bass.ds(t * P, P), :, :]).then_inc(u_in, 16)

            def load_u(t):
                after(sp, u_ready, t)
                for h in range(2):
                    load_sums(t, h)
                load_root(t)

            def load_z(t):
                after(sp, x1_ready, t)
                sp.dma_start(slot[2].rearrange("p (h n) -> p h n", h=2), gate_d[bass.ds(t * P, P), :, :]).then_inc(z_in, 16)
                if isinstance(t, int) and t == NT - 1:
                    sp.dma_start(slot[3][0:LAST, :], x[t * P:N, :]).then_inc(z_in, 16)
                else:
                    sp.dma_start(slot[3], x[bass.ds(t * P, P), :]).then_inc(z_in, 16)

            def spill_sums(g0, g1):
                sp.dma_start(agg_d[NPAD + g0 * P:NPAD + g1 * P, :].rearrange("(g p) n -> p g n", p=P), U[:, g0:g1, :]).then_inc(agg1_out, 16)

            for b in range(2):
                sp.wait_ge(y_out[b], 16 * (UNITS_Y + 2) * NT // 2)
            sp.wait_ge(agg_out, 16)
            sp.wait_ge(msg_split, 2 * ETILES)
            load_root(0)
            load_sums(0, 0)
            load_unit(UNITS_Y + 5, 1, w_gate[0:D], 1)
            sp.wait_ge(gemm_done, (UNITS_Y + 4) * NT)
            sp.dma_start(BIAS_ROOT[:, :], b_root.partition_broadcast(P)).then_inc(bias_in, 16)
            sp.wait_ge(pair_added, 2 * NPAIR + AHEAD)
            spill_sums(0, 4)
            sp.wait_ge(agg1_out, 16)
            load_sums(0, 1)
            spill_sums(4, NT)
            sp.dma_start(BIAS_GATE[:, :], b_gate.partition_broadcast(P)).then_inc(bias_gate_in, 16)
            load_w(gcn_raw[:, :, 0:HW], 0, w_gcn, 0)
            load_u(1)
            for b in range(2):
                sp.wait_ge(y_out[b], 16 * (UNITS_Y + 4) * NT // 2)
            sp.wait_ge(agg1_out, 32)
            load_z(0)
            sp.wait_ge(w_split, (UNITS_Y + 6) * KT)
            load_w(gcn_raw[:, :, HW:D], 1, w_gcn, 1)
            load_u(2)
            with sp.Fori(0, NT - 3) as i:
                load_z(i + 1)
                load_u(i + 3)
            load_z(NT - 2)
            load_z(NT - 1)

            sp.wait_ge(z_done, NT)
            for s in range(KT):
                sp.wait_ge(h_out, 32 * (s + 1))
                sp.dma_start(hhi[:, s, :].bitcast(F32), hhi_d[s * P:(s + 1) * P, :]).then_inc(h_in[s], 16)
                sp.dma_start(hlo[:, s, :].bitcast(F32), hlo_d[s * P:(s + 1) * P, :]).then_inc(h_in[s], 16)

            def load_c(d, b):
                after(sp, c_split, d - 1)
                sp.dma_start(CIN[b][:, :], count_d[:, bass.ds(d * NPAD, NPAD)]).then_inc(c_in[b], 16)

            def load_res(d, b):
                after(sp, out_ready, d - 1)
                sp.dma_start(slot[b], x1_d[bass.ds(d * P, P), :]).then_inc(res_in[b], 16)

            sp.wait_ge(x1_out, 16 * NT)
            sp.wait_ge(h_done, NT)
            sp.dma_start(BIAS_GCN[:, :], b_gcn.partition_broadcast(P)).then_inc(bias1_in, 16)
            for b in range(2):
                load_c(b, b)
                load_res(b, b)
            with sp.Fori(1, NT // 2) as i:
                for b in range(2):
                    load_c(2 * i + b, b)
                    load_res(2 * i + b, b)

        @block.gpsimd
        def _(pool):
            chain = Chain(pool, pool_chain)
            link = chain.link
            link(nc.gpsimd.memset(IDENT[:, :], 0.0))
            nc.gpsimd.affine_select(out=IDENT[:, :], in_=IDENT[:, :], compare_op=ALU.not_equal, fill=1.0, base=0,
                                    pattern=[[-1, P]], channel_multiplier=1).then_inc(consts, 1)
            nc.gpsimd.iota(IOTA[:, :], pattern=[[1, NPAD]], base=0, channel_multiplier=0,
                           allow_small_or_imprecise_dtypes=True).then_inc(consts, 1)
            link(nc.gpsimd.memset(EARLIER, 1.0))
            nc.gpsimd.affine_select(out=EARLIER, in_=EARLIER, compare_op=ALU.is_gt, fill=0.0, base=0,
                                    pattern=[[1, EPART]], channel_multiplier=-1).then_inc(consts, 1)
            nc.gpsimd.memset(ONES, 1.0).then_inc(consts, 1)
            nc.gpsimd.memset(MINUS_HALF[:, :], -0.5).then_inc(consts, 1)
            nc.gpsimd.iota(PAIRSUM[:, 1, :], pattern=[[PAIR, NPAIR]], base=0, channel_multiplier=0,
                           allow_small_or_imprecise_dtypes=True).then_inc(consts, 1)
            link(nc.gpsimd.memset(WGOT[:, :, :], 0.0))
            nc.gpsimd.memset(PADREC[:, :, 0:2], FAR).then_inc(pad_set, 1)
            nc.gpsimd.memset(PADREC[:, :, 2:3].bitcast(F32), -1.0).then_inc(pad_set, 1)
            nc.gpsimd.memset(PADREC[:, :, 3:4], 0).then_inc(pad_set, 1)
            pool.wait_ge(pad_set, 3)
            pool.dma_start(rec_d.rearrange("(p t) f -> p (t f)", p=P),
                           PADREC[:, :, :].rearrange("p t f -> p (t f)")).then_inc(pad_out, 16)
            pool.wait_ge(pad_out, 16)

            pool.wait_ge(pos_ready, 1)

            def scatter_half(i, b, peeled):
                if not peeled:
                    pool.wait_ge(scattered[b], i * (16 * RING))
                pool.wait_ge(pos_ready, 1)
                col = bass.ds(i * (2 * RING) + b * RING, RING)
                nc.gpsimd.tensor_copy(IDX[0:EPART, b, :], ADDR[:, col]).then_inc(idx_set, 1)
                nc.gpsimd.tensor_copy(RREC[0:EPART, b, :, :], REC[0:EPART, col, :]).then_inc(idx_set, 1)
                pool.wait_ge(idx_set, i * 4 + (2 * b + 2))
                pool.sem_inc(passed_pool, 1)
                for j in range(RING):
                    pool.indirect_dma_start(
                        out=rec_d, out_offset=bass.IndirectOffsetOnAxis(ap=IDX[0:EPART, b, j:j + 1], axis=0),
                        in_=RREC[0:EPART, b, j, :], in_offset=None).then_inc(scattered[b], 16)

            turns = ECOL // (2 * RING)
            for b in range(2):
                scatter_half(0, b, True)
            with pool.Fori(1, turns) as i:
                for b in range(2):
                    scatter_half(i, b, False)
            for b in range(2):
                pool.wait_ge(scattered[b], 16 * RING * turns)
            pool.wait_ge(chunk_ready, ECOL // CHUNK)
            pool.dma_start(REC[:, :, :].rearrange("p t f -> p (t f)"),
                           rec_d.rearrange("(p t) f -> p (t f)", p=P)).then_inc(sorted_in, 16)
            pool.wait_ge(sorted_in, 16)

            pool.wait_ge(deg_ready, 1)
            nc.gpsimd.tensor_tensor(DINV[:, :], DEG[:, :], MINUS_HALF[:, :], ALU.pow).then_inc(dinv_ready, 1)
            pool.wait_ge(inv_ready, 1)
            pool.dma_start(inv_d.rearrange("(p k) a -> p (k a)", p=P), INV[:, :]).then_inc(inv_out, 16)
            pool.wait_ge(inv_out, 16)

            IDX_BASE = 2 * 2 * turns

            def weight_half(i, b, peeled):
                tiles = bass.ds(i * (2 * RING) + b * RING, RING)
                if not peeled:
                    pool.wait_ge(w_got[b], i * (16 * RING))
                    pool.wait_ge(sorted_in, 16)
                    nc.gpsimd.tensor_copy(W_EDGE[:, bass.ds((i - 1) * (2 * RING) + b * RING, RING)], WGOT[:, b, :]).then_inc(w_ready, 1)
                    pool.wait_ge(w_ready, (i - 1) * 2 + (b + 1))
                pool.wait_ge(sorted_in, 16)
                nc.gpsimd.tensor_copy(IDX[:, b, :], REC[:, tiles, 1]).then_inc(idx_set, 1)
                pool.wait_ge(idx_set, i * 2 + (IDX_BASE + b + 1))
                pool.sem_inc(passed_pool, 1)
                for j in range(RING):
                    pool.indirect_dma_start(
                        out=WGOT[:, b, j:j + 1], out_offset=None, in_=inv_d,
                        in_offset=bass.IndirectOffsetOnAxis(ap=IDX[:, b, j:j + 1], axis=0),
                        bounds_check=P * NKEY - 1, oob_is_err=False).then_inc(w_got[b], 16)

            turns_w = ETILES // (2 * RING)
            for b in range(2):
                weight_half(0, b, True)
            with pool.Fori(1, turns_w) as i:
                for b in range(2):
                    weight_half(i, b, False)
            for b in range(2):
                pool.wait_ge(w_got[b], 16 * RING * turns_w)
                nc.gpsimd.tensor_copy(W_EDGE[:, (turns_w - 1) * 2 * RING + b * RING:(turns_w - 1) * 2 * RING + (b + 1) * RING],
                                      WGOT[:, b, :]).then_inc(w_ready, 1)
            IDX_BASE2 = IDX_BASE + 2 * turns_w

            pool.wait_ge(cells_added, NPAIR + AHEAD)
            pool.dma_start(count_d, COUNT.rearrange("p g n -> p (g n)")).then_inc(count_out, 16)

            for run in range(2):
                for b in range(2):
                    pool.wait_ge(y_out[b], 16 * R * NT // 2 * (run + 1))
                pool.wait_ge(work_clear, run + 1)

                def gather_half(i, b, peeled, run=run):
                    if not (peeled and run == 0):
                        pool.wait_ge(msg_split, i * (2 * RING) + (run * ETILES + b * RING - RING))
                    pool.wait_ge(sorted_in, 16)
                    nc.gpsimd.tensor_copy(IDX[:, b, :], REC[:, bass.ds(i * (2 * RING) + b * RING, RING), 0]).then_inc(idx_set, 1)
                    pool.wait_ge(idx_set, i * 2 + (IDX_BASE2 + run * 2 * turns_w + b + 1))
                    for j in range(RING):
                        tile = i * (2 * RING) + (run * ETILES + b * RING + j)
                        after(pool, msg_split, tile - 3)
                        pool.sem_inc(passed_pool, 1)
                        pool.indirect_dma_start(
                            out=RAWG[:, j % 4, :], out_offset=None, in_=y_d[0:(run + 1) * YROWS, :],
                            in_offset=bass.IndirectOffsetOnAxis(ap=IDX[:, b, j:j + 1], axis=0),
                            bounds_check=(run + 1) * YROWS - 1, oob_is_err=False).then_inc(got[j % 4], 16)

                if run == 0:
                    pool.wait_ge(w_ready, 2 * turns_w)
                for b in range(2):
                    if run == 0 and b == 0:
                        gather_half(0, b, True)
                    else:
                        gather_half(0, b, False)
                with pool.Fori(1, turns_w) as i:
                    for b in range(2):
                        gather_half(i, b, False)
                if run == 0:
                    pool.wait_ge(pair_added, NPAIR + AHEAD)
                    pool.dma_start(agg_d[0:NPAD, :].rearrange("(g p) n -> p g n", p=P), U).then_inc(agg_out, 16)

            pool.wait_ge(bias_in, 16)

            def add_root(t):
                pool.wait_ge(u_in, t * 48 + 48)
                nc.gpsimd.tensor_tensor(slot[1], slot[1], BIAS_ROOT[:, :], ALU.add).then_inc(root_ready, 1)

            def add_gate(t):
                pool.wait_ge(z_in, t * 32 + 32)
                nc.gpsimd.tensor_tensor(slot[2], slot[2], BIAS_GATE[:, :], ALU.add).then_inc(gate_ready, 1)

            def rstd(t):
                pool.wait_ge(var_ready, t + 1)
                nc.gpsimd.tensor_tensor(RSTD[:, :], VAR[:, :], MINUS_HALF[:, 0:1], ALU.pow).then_inc(rstd_ready, 1)

            add_root(0)
            add_root(1)
            pool.wait_ge(bias_gate_in, 16)
            add_gate(0)
            rstd(0)
            add_root(2)
            with pool.Fori(0, NT - 3) as i:
                add_gate(i + 1)
                rstd(i + 1)
                add_root(i + 3)
            for t in (NT - 2, NT - 1):
                add_gate(t)
                rstd(t)
            with pool.Fori(NT, 2 * NT) as t:
                rstd(t)
            pool.wait_ge(count_out, 16)
            pool.wait_ge(agg_out, 16)
            pool.wait_ge(agg1_out, 32)

        @block.tensor
        def _(pe):
            def turn_x(t):
                pe.wait_ge(x_in[t % 2], 16 * (t // 2 + 1))
                if t == 0:
                    pe.wait_ge(consts, 1)
                for half in range(2):
                    g = 2 * t + half
                    after(pe, x_split, g - 3)
                    for j in range(4):
                        k = 4 * half + j
                        last = pe.transpose(PM[:, g % 4, j * P:(j + 1) * P], XIN[:, t % 2, k * P:(k + 1) * P], IDENT[:, :])
                    last.then_inc(x_turned, 1)

            def gemm(i, jt, b, first_unit=False):
                j, t = jt // NT, jt % NT
                q = i * TILES_BODY + jt
                bank = jt % 4
                if b == 0:
                    if t == 0 and not first_unit:
                        pe.wait_ge(w_split, i * (2 * KT) + KT * (j + 1))
                    if first_unit:
                        pe.wait_ge(x_split, 2 * (t + 1))
                    after(pe, evac_done, q - 3)
                for k in range(4 * b, 4 * b + 4):
                    if first_unit and t == 0:
                        pe.wait_ge(w_split, k + 1)
                    for n, (lhs, rhs) in enumerate(((xhi, whi), (xhi, wlo), (xlo, whi))):
                        last = pe.matmul(PG[:, bank, :], lhs[:, k, t * P:(t + 1) * P], rhs[:, j % 2, k, :],
                                         start=(k == 0 and n == 0), stop=(k == KT - 1 and n == 2))
                if b == 1:
                    last.then_inc(gemm_done, 1)

            def count_pair(pair, n):
                pe.wait_ge(hot_ready, pair + 1)
                pe.wait_ge(cells_added, pair + AHEAD)
                for e in range(2):
                    s = (2 * n + e) % 4
                    hot = DSTHOT[:, s, :] if s < 3 else DSTHOT3[:, 0, :]
                    for c0, c1 in ((0, HW), (HW, 2 * HW), (2 * HW, NPAD)):
                        last = pe.matmul(PMALL[:, c0:c1], SRCHOT[:, s, :], hot[:, c0:c1], start=(e == 0), stop=(e == 1))
                last.then_inc(cells_done, 1)

            def message_pair(pair, n, run):
                pair = pair + run * NPAIR
                pe.wait_ge(pair_ready, pair * 2 + 2)
                pe.wait_ge(msg_split, pair * 2 + 2)
                pe.wait_ge(pair_added, pair - 1 + AHEAD)
                for e in range(2):
                    for a, part in enumerate((sp_hi, sp_lo)):
                        last = pe.matmul(PM[:, n % 2, :], ONEHOT[:, n % 2, e, :], part[:, n % 2, e, :],
                                         start=(e == 0 and a == 0), stop=(e == 1 and a == 1))
                last.then_inc(pair_done, 1)

            def steps(pair_step):
                def step(i, s, pairs):
                    i, s = normal(i, s)
                    gemm(i, s // 2, s % 2)
                    for pair, n in pairs:
                        pair_step(pair, n)
                return step

            pe.sem_inc(cells_done, AHEAD)
            pe.sem_inc(pair_done, AHEAD)
            turn_x(0)
            for jt in range(TILES_BODY):
                gemm(0, jt, 0, first_unit=jt < NT)
                if jt == 0:
                    turn_x(1)
                gemm(0, jt, 1, first_unit=jt < NT)
                if jt + 2 < NT:
                    turn_x(jt + 2)
                if jt == 14:
                    pe.wait_ge(rows_total, 1)
                    pe.wait_ge(consts, 4)
                    pe.matmul(PM[0:EPART, 0, 0:NT], EARLIER, T10[0:EPART, 0, :], start=True, stop=True)
                    pe.matmul(PM[:, 1, 0:NT], WORK[0:EPART, 3 * NT * ECOL + P:3 * NT * ECOL + 2 * P], T10[0:EPART, 0, :],
                              start=True, stop=True).then_inc(offsets, 1)
            for jt in range(TILES_BODY):
                gemm(1, jt, 0)
                gemm(1, jt, 1)
                if 1 <= jt <= ECOL // CHUNK:
                    c = jt - 1
                    pe.wait_ge(chunk_ready, c + 1)
                    for e in range(CHUNK):
                        last = pe.matmul(PM[:, 3, 0:NKEY], LOCHOT[0:EPART, c % 2, e, :], KEYHOT[0:EPART, c % 2, e, :],
                                         start=(c == 0 and e == 0), stop=(c == ECOL // CHUNK - 1 and e == CHUNK - 1))
                    last.then_inc(chunk_done, 1)
            plain((2, 0), COUNT_AT, steps(None))
            one_each(pe, COUNT_AT, steps(count_pair))
            plain(phase_end(COUNT_AT), RUN0_AT, steps(None))
            one_each(pe, RUN0_AT, steps(lambda pair, n: message_pair(pair, n, 0)))
            plain(phase_end(RUN0_AT), (RUN1_BODY, 0), steps(None))
            dense(pe, RUN1_BODY, steps(lambda pair, n: message_pair(pair, n, 1)))

            def turn_u(t):
                pe.wait_ge(u_ready, t + 1)
                after(pe, u_split, t)
                for k in range(KT):
                    last = pe.transpose(PM[:, k // 4, (k % 4) * P:(k % 4 + 1) * P], slot[4][:, k * P:(k + 1) * P], IDENT[:, :])
                last.then_inc(u_turned, 1)

            def gate(t):
                pe.wait_ge(u_split, t + 1)
                after(pe, z_read, t)
                for h in range(2):
                    for k in range(KT):
                        for n, (lhs, rhs) in enumerate(((ut_hi, whi), (ut_hi, wlo), (ut_lo, whi))):
                            last = pe.matmul(PG[:, h, :], lhs[:, k * P:(k + 1) * P], rhs[:, h, k, :],
                                             start=(k == 0 and n == 0), stop=(k == KT - 1 and n == 2))
                last.then_inc(z_done, 1)

            def turn_x1(t):
                pe.wait_ge(x1_ready, t + 1)
                after(pe, x1_split, t)
                for k in range(KT):
                    last = pe.transpose(PM[:, 2 + k // 4, (k % 4) * P:(k % 4 + 1) * P], slot[6][:, k * P:(k + 1) * P], IDENT[:, :])
                last.then_inc(x1_turned, 1)

            def conv_in(t):
                pe.wait_ge(x1_split, t + 1)
                after(pe, h_split, t)
                for h in range(2):
                    for k in range(KT):
                        for n, (lhs, rhs) in enumerate(((SPHI, gcn_hi), (SPHI, gcn_lo), (SPLO, gcn_hi))):
                            last = pe.matmul(PG[:, 2 + h, :], lhs[:, k * P:(k + 1) * P], rhs[:, k, h * HW:(h + 1) * HW],
                                             start=(k == 0 and n == 0), stop=(k == KT - 1 and n == 2))
                last.then_inc(h_done, 1)

            pe.wait_ge(w_split, (UNITS_Y + 6) * KT)
            turn_u(0)
            gate(0)
            turn_u(1)
            gate(1)
            turn_x1(0)
            turn_u(2)
            pe.wait_ge(w_split, (UNITS_Y + 8) * KT)
            conv_in(0)
            turn_x1(1)
            with pe.Fori(1, NT - 2) as i:
                gate(i + 1)
                turn_u(i + 2)
                conv_in(i)
                turn_x1(i + 1)
            gate(NT - 1)
            conv_in(NT - 2)
            turn_x1(NT - 1)
            conv_in(NT - 1)

            def conv(d, b, first):
                pe.wait_ge(c_split, d + 1)
                after(pe, conv_read, d - 1)
                order = [KT, KT + 1] + list(range(KT))
                for at_s, s in enumerate(order):
                    if first and s < KT:
                        pe.wait_ge(h_in[s], 32)
                    if first and s >= KT:
                        pe.wait_ge(h_split, s + 1)
                    c_hi = XHI[:, b * NPAD + s * P:b * NPAD + (s + 1) * P]
                    c_lo = XLO[:, b * NPAD + s * P:b * NPAD + (s + 1) * P]
                    if s < KT:
                        r_hi, r_lo = hhi[:, s, :], hlo[:, s, :]
                    elif s == KT:
                        r_hi, r_lo = SPHI[:, D:2 * D], SPLO[:, D:2 * D]
                    else:
                        r_hi, r_lo = ut_hi, ut_lo
                    for n, (lhs, rhs) in enumerate(((c_hi, r_hi), (c_hi, r_lo), (c_lo, r_hi))):
                        for h in range(2):
                            last = pe.matmul(PG[:, 2 * b + h, :], lhs, rhs[:, h * HW:(h + 1) * HW],
                                             start=(at_s == 0 and n == 0), stop=(at_s == NT - 1 and n == 2))
                last.then_inc(conv_done, 1)

            for b in range(2):
                conv(b, b, b == 0)
            with pe.Fori(1, NT // 2) as i:
                for b in range(2):
                    conv(2 * i + b, b, False)

        @block.scalar
        def _(act):
            def x_high(t):
                for half in range(2):
                    g = 2 * t + half
                    act.wait_ge(x_turned, g + 1)
                    nc.scalar.activation(xhi[:, 4 * half:4 * half + 4, t * P:(t + 1) * P],
                                         PM[:, g % 4, :].rearrange("p (k n) -> p k n", k=4), ACT.Copy).then_inc(x_hi, 1)

            def w_high(k, high, raw):
                nc.scalar.activation(high[:, k, :], raw[:, k, :], ACT.Copy).then_inc(w_hi, 1)

            def evac(i, jt):
                q = i * TILES_BODY + jt
                b = jt % 2
                act.wait_ge(gemm_done, q + 1)
                after(act, y_out[b], i * (16 * NT) + 16 * (jt // 2))
                nc.scalar.activation(STAGE[:, b, :], PG[:, jt % 4, :], ACT.Copy).then_inc(evac_done, 1)

            def store_y(i, jt):
                q = i * TILES_BODY + jt
                b = jt % 2
                act.wait_ge(evac_done, q + 1)
                act.dma_start(y_d[bass.ds(q * P, P), :], STAGE[:, b, :]).then_inc(y_out[b], 16)

            def w_high_next(i, jt):
                j, k = jt // NT, jt % NT - 1
                b = (j + 1) % 2
                if 0 <= k < KT:
                    if k == 0:
                        act.wait_ge(w_in[b], i * 32 + 32)
                    w_high(k, whi[:, b, :, :], wraw[:, b, :, :])

            def msg_high(pair, n, run):
                for e in range(2):
                    act.wait_ge(got[(2 * n + e) % 4], (pair + run * NPAIR - n % 2) * 8 + 16)
                    if e == 0:
                        act.wait_ge(pair_done, pair + (run * NPAIR - 1 + AHEAD))
                    act.wait_ge(w_ready, 2 * (ETILES // (2 * RING)))
                    nc.scalar.activation(sp_hi[:, n % 2, e, :], RAWG[:, (2 * n + e) % 4, :], ACT.Copy,
                                         scale=W_EDGE[:, bass.ds(pair * 2 + e, 1)]).then_inc(msg_hi, 1)

            def steps(run):
                def step(i, s, pairs):
                    i, s = normal(i, s)
                    if run is not None:
                        for pair, n in pairs:
                            msg_high(pair, n, run)
                    if s % 2 == 0:
                        i, jt = (i, s // 2 - 1) if s > 0 else (i - 1, TILES_BODY - 1)
                        evac(i, jt)
                        w_high_next(i, jt)
                        store_y(i, jt)
                return step

            x_high(0)
            for k in range(KT):
                if k == KT // 2:
                    x_high(1)
                act.wait_ge(w0_in[k], 16)
                w_high(k, whi[:, 0, :, :], wraw[:, 0, :, :])
            for jt in range(TILES_BODY - 1):
                evac(0, jt)
                store_y(0, jt)
                if jt + 2 < NT:
                    x_high(jt + 2)
                w_high_next(0, jt)
            plain((1, 0), COUNT_AT, steps(None))
            one_each(act, COUNT_AT, steps(None))
            plain(phase_end(COUNT_AT), RUN0_AT, steps(None))
            one_each(act, RUN0_AT, steps(0))
            plain(phase_end(RUN0_AT), (RUN1_BODY, 0), steps(None))
            dense(act, RUN1_BODY, steps(1))
            evac(RUN1_BODY + 1, TILES_BODY - 1)
            store_y(RUN1_BODY + 1, TILES_BODY - 1)

            act.wait_ge(w_in[1], (UNITS_Y + 6) // 2 * 32)
            for k in range(KT):
                w_high(k, whi[:, 1, :, :], wraw[:, 1, :, :])

            def gcn_high(h):
                cols = slice(h * HW, (h + 1) * HW)
                act.wait_ge(w_in[h], (UNITS_Y + 7 + h) // 2 * 32)
                for k in range(KT):
                    w_high(k, gcn_hi[:, :, cols], gcn_raw[:, :, cols])

            def u_high(t):
                act.wait_ge(u_turned, t + 1)
                after(act, z_done, t)
                for half in range(2):
                    nc.scalar.activation(ut_hi[:, half * HW:(half + 1) * HW], PM[:, half, :], ACT.Copy).then_inc(u_hi, 1)

            def tanh_u(t):
                act.wait_ge(u_ready, t + 1)
                after(act, x1_ready, t)
                nc.scalar.activation(slot[5], slot[4], ACT.Tanh).then_inc(tanh_done, 1)

            def h_high(t, d0, d1):
                act.wait_ge(h_done, t + 1)
                act.wait_ge(dinv_ready, 1)
                for half, d_ap in ((0, d0), (1, d1)):
                    nc.scalar.activation(d_ap, PG[:, 2 + half, :], ACT.Copy, scale=DINV[:, bass.ds(t, 1)]).then_inc(h_hi, 1)

            def x1_high(t):
                act.wait_ge(x1_turned, t + 1)
                after(act, h_done, t)
                for half in range(2):
                    nc.scalar.activation(SPHI[:, half * HW:(half + 1) * HW], PM[:, 2 + half, :], ACT.Copy).then_inc(x1_hi, 1)
                act.dma_start(x1_d[bass.ds(t * P, P), :], slot[6]).then_inc(x1_out, 16)

            def h_store(t):
                act.wait_ge(h_split, t + 1)
                act.dma_start(hhi_d[bass.ds(t * P, P), :], HST_HI[:, :].bitcast(F32)).then_inc(h_out, 16)
                act.dma_start(hlo_d[bass.ds(t * P, P), :], HST_LO[:, :].bitcast(F32)).then_inc(h_out, 16)

            u_high(0)
            tanh_u(0)
            gcn_high(0)
            u_high(1)
            tanh_u(1)
            gcn_high(1)
            x1_high(0)
            for b in range(2):
                act.wait_ge(y_out[b], 16 * (UNITS_Y + 4) * NT // 2)

            def tile_body(t, staged):
                if t_in(t + 2):
                    u_high(t + 2)
                if staged:
                    after(act, h_out, t * 32)
                    h_high(t, HST_HI[:, 0:HW], HST_HI[:, HW:D])
                else:
                    place_h = SPHI[:, D:2 * D] if t == NT - 2 else ut_hi
                    h_high(t, place_h[:, 0:HW], place_h[:, HW:D])
                if t_in(t + 1):
                    x1_high(t + 1)
                if t_in(t + 2):
                    tanh_u(t + 2)
                if staged:
                    h_store(t)

            def t_in(t):
                return not isinstance(t, int) or t < NT

            tile_body(0, True)
            with act.Fori(1, NT - 2) as i:
                tile_body(i, True)
            tile_body(NT - 2, False)
            tile_body(NT - 1, False)
            act.wait_ge(h_out, 32 * KT)
            act.wait_ge(x1_out, 16 * NT)

            def store(d, b, rows):
                act.wait_ge(out_ready, d + 1)
                if rows == P:
                    act.dma_start(out[bass.ds(d * P, P), :], slot[2 + b]).then_inc(out_done[b], 16)
                else:
                    act.dma_start(out[d * P:N, :], slot[2 + b][0:rows, :]).then_inc(out_done[b], 16)

            with act.Fori(0, NT // 2 - 1) as i:
                for b in range(2):
                    store(2 * i + b, b, P)
            store(NT - 2, 0, P)
            store(NT - 1, 1, LAST)
            for b in range(2):
                act.wait_ge(out_done[b], 16 * NT // 2)

        @block.vector
        def _(dve):
            chain = Chain(dve, dve_chain)
            link = chain.link
            V = nc.vector

            def x_low(t):
                for half in range(2):
                    g = 2 * t + half
                    dve.wait_ge(x_hi, g + 1)
                    dst_ap = xlo[:, 4 * half:4 * half + 4, t * P:(t + 1) * P]
                    hi_ap = xhi[:, 4 * half:4 * half + 4, t * P:(t + 1) * P].bitcast(F32)
                    V.tensor_tensor(dst_ap, PM[:, g % 4, :].rearrange("p (k n) -> p k n", k=4), hi_ap,
                                    ALU.subtract).then_inc(x_split, 1)

            def w_low(m, k, high, low, raw):
                dve.wait_ge(w_hi, m + 1)
                V.tensor_tensor(low[:, k, :], raw[:, k, :], high[:, k, :].bitcast(F32), ALU.subtract).then_inc(w_split, 1)

            def w_low_next(i, jt):
                j, k = jt // NT, jt % NT - 1
                b = (j + 1) % 2
                if 0 <= k < KT:
                    w_low(i * (2 * KT) + (KT * (j + 1) + k), k, whi[:, b, :, :], wlo[:, b, :, :], wraw[:, b, :, :])

            def edge_fields():
                dve.wait_ge(edges_in, 48)
                V.tensor_scalar(T_GRP, T_DST, 7, None, ALU.logical_shift_right)
                link(V.tensor_scalar(T_LOC, T_DST, P - 1, None, ALU.bitwise_and))
                V.tensor_copy(T_GRPF, T_GRP)
                V.tensor_copy(T_LOCF, T_LOC)
                link(V.tensor_copy(REC[0:EPART, 0:ECOL, 2].bitcast(F32), T_LOC))
                link(V.scalar_tensor_tensor(KEY[:, :], T_GRPF, float(R), T_TYPE, ALU.mult, ALU.add))
                V.scalar_tensor_tensor(REC[0:EPART, 0:ECOL, 1], T_LOCF, float(NKEY), KEY[:, :], ALU.mult, ALU.add)
                V.scalar_tensor_tensor(REC[0:EPART, 0:ECOL, 0], T_TYPE, float(NPAD), T_SRC, ALU.mult, ALU.add)
                link(V.tensor_copy(REC[0:EPART, 0:ECOL, 3], T_SRC))

            def membership():
                for g in range(NT):
                    last = V.tensor_scalar(MEMB[:, g, :], T_GRPF, float(g), None, ALU.is_equal)
                link(last)

            def scan_step(n):
                a = MEMB if n == 0 else SCAN[(n - 1) % 2]
                b, s = SCAN[n % 2], 1 << n
                V.tensor_copy(b[:, :, 0:s], a[:, :, 0:s])
                link(V.tensor_tensor(b[:, :, s:ECOL], a[:, :, s:ECOL], a[:, :, 0:ECOL - s], ALU.add))

            SCANS = (ECOL - 1).bit_length()
            PREFIX = SCAN[(SCANS - 1) % 2]

            def group_starts():
                dve.wait_ge(offsets, 1)
                link(V.tensor_scalar(T10I[:, :], PM[:, 1, 0:NT], float(PAIR - 1), None, ALU.add))
                link(V.tensor_scalar(T10I[:, :], T10I[:, :], 8, 8, ALU.logical_shift_right, ALU.logical_shift_left))
                link(V.tensor_copy(T10[:, 1, :], T10I[:, :]))
                link(V.memset(T10[:, 2, 0:1], 0.0))
                for g in range(1, NT):
                    link(V.tensor_tensor(T10[:, 2, g:g + 1], T10[:, 2, g - 1:g], T10[:, 1, g - 1:g], ALU.add))
                link(V.scalar_tensor_tensor(T10[0:EPART, 3, :], PM[0:EPART, 0, 0:NT], -1.0, T10[0:EPART, 2, :], ALU.add, ALU.add))

            def positions_a():
                link(V.tensor_tensor(PREFIX, PREFIX, T10[0:EPART, 3, :].unsqueeze(2).to_broadcast([EPART, NT, ECOL]), ALU.add))
                link(V.tensor_tensor(PREFIX, PREFIX, MEMB, ALU.mult))

            def positions_b():
                link(V.tensor_reduce(O_POS, PREFIX.rearrange("p g c -> p c g"), AXIS_X, ALU.add))
                link(V.tensor_copy(O_POSI, O_POS))
                V.tensor_scalar(O_LANE, O_POSI, P - 1, None, ALU.bitwise_and)
                link(V.tensor_scalar(O_TILE, O_POSI, 7, None, ALU.logical_shift_right))
                V.scalar_tensor_tensor(ADDR[:, :], O_LANE, float(ETILES), O_TILE, ALU.mult, ALU.add).then_inc(pos_ready, 1)

            def pair_groups():
                dve.wait_ge(consts, 6)
                link(V.memset(PAIRSUM[:, 0, :], 0.0))
                for g in range(1, NT):
                    link(V.scalar_tensor_tensor(PAIRSUM[:, 0, :], PAIRSUM[:, 1, :], T10[0:1, 2, g:g + 1], PAIRSUM[:, 0, :],
                                                ALU.is_ge, ALU.add))
                link(V.tensor_copy(GROUP[:, :], PAIRSUM[:, 0, :]))

            def sort_step(n):
                if n == 0:
                    edge_fields()
                elif n == 1:
                    membership()
                elif n - 2 < SCANS:
                    scan_step(n - 2)
                elif n == SCANS + 2:
                    V.tensor_copy(T10[0:EPART, 0, :], PREFIX[:, :, ECOL - 1]).then_inc(rows_total, 1)
                elif n == 15:
                    group_starts()
                elif n == 16:
                    positions_a()
                elif n == 17:
                    positions_b()
                elif n == 18:
                    pair_groups()

            def hot_chunk(c):
                if c == 0:
                    dve.wait_ge(pad_out, 16)
                if c >= 2:
                    dve.wait_ge(chunk_done, c - 1)
                cols = slice(c * CHUNK, (c + 1) * CHUNK)
                V.tensor_tensor(LOCHOT[0:EPART, c % 2, :, :], IOTA[0:EPART, 0:P].unsqueeze(1).to_broadcast([EPART, CHUNK, P]),
                                REC[0:EPART, cols, 2].bitcast(F32).unsqueeze(2).to_broadcast([EPART, CHUNK, P]), ALU.is_equal)
                V.tensor_tensor(KEYHOT[0:EPART, c % 2, :, :], IOTA[0:EPART, 0:NKEY].unsqueeze(1).to_broadcast([EPART, CHUNK, NKEY]),
                                KEY[:, cols].unsqueeze(2).to_broadcast([EPART, CHUNK, NKEY]), ALU.is_equal).then_inc(chunk_ready, 1)


            def inverse_counts():
                dve.wait_ge(chunk_done, ECOL // CHUNK)
                link(V.tensor_scalar(INV[:, :], PM[:, 3, 0:NKEY], 1.0, None, ALU.max))
                V.reciprocal(INV[:, :], INV[:, :]).then_inc(inv_ready, 1)
                link(V.tensor_reduce(DEG[:, :], PM[:, 3, 0:NKEY].rearrange("p (g r) -> p g r", g=NT), AXIS_X, ALU.add))
                V.tensor_scalar(DEG[:, :], DEG[:, :], 1.0, None, ALU.add).then_inc(deg_ready, 1)

            def count_setup():
                dve.wait_ge(sorted_in, 16)
                t_loc = WORK[:, 0:ETILES].bitcast(I32)
                t_grp = WORK[:, ETILES:2 * ETILES].bitcast(I32)
                V.tensor_scalar(t_loc, REC[:, :, 3], P - 1, None, ALU.bitwise_and)
                link(V.tensor_scalar(t_grp, REC[:, :, 3], 7, None, ALU.logical_shift_right))
                V.tensor_copy(SRC_LOC[:, :], t_loc)
                link(V.scalar_tensor_tensor(CELL[:, :], t_grp, float(P), REC[:, :, 2].bitcast(F32), ALU.mult, ALU.add))
                link(V.memset(WORK[:, 0:NT * NPAD // 2].bitcast(I32), 0))
                for g in range(NT):
                    last = V.tensor_copy(COUNT[:, g, g * P:(g + 1) * P], IDENT[:, :])
                link(last)

            def count_hot(pair, n):
                dve.wait_ge(cells_done, pair + (AHEAD - 1))
                for e in range(2):
                    s = (2 * n + e) % 4
                    tile = bass.ds(pair * 2 + e, 1)
                    hot = DSTHOT[:, s, :] if s < 3 else DSTHOT3[:, 0, :]
                    V.tensor_scalar(SRCHOT[:, s, :], IOTA[:, 0:P], SRC_LOC[:, tile], None, ALU.is_equal)
                    last = V.tensor_scalar(hot, IOTA[:, :], CELL[:, tile], None, ALU.is_equal)
                last.then_inc(hot_ready, 1)

            def group_of(pair):
                return dve.value_load(GROUP[0:1, bass.ds(pair, 1)], min_val=0, max_val=NT - 1)

            def count_add(pair, n):
                g = group_of(pair)
                dve.wait_ge(cells_done, pair + 1 + AHEAD)
                acc = COUNT[:, bass.ds(g, 1), :].rearrange("p a n -> p (a n)")
                V.tensor_tensor(acc, acc, PMALL[:, 0:NPAD], ALU.add).then_inc(cells_added, 1)
                dve.wait_ge(cells_added, pair + 1 + AHEAD)

            def msg_low(pair, n, run):
                for e in range(2):
                    V.tensor_scalar(ONEHOT[:, n % 2, e, :], IOTA[:, 0:P], REC[:, bass.ds(pair * 2 + e, 1), 2].bitcast(F32), None,
                                    ALU.is_equal).then_inc(pair_ready, 1)
                for e in range(2):
                    dve.wait_ge(msg_hi, pair * 2 + (2 * run * NPAIR + e + 1))
                    V.scalar_tensor_tensor(sp_lo[:, n % 2, e, :], RAWG[:, (2 * n + e) % 4, :], W_EDGE[:, bass.ds(pair * 2 + e, 1)],
                                           sp_hi[:, n % 2, e, :].bitcast(F32), ALU.mult, ALU.subtract).then_inc(msg_split, 1)

            def msg_add(pair, n, run):
                g = group_of(pair)
                dve.wait_ge(pair_done, pair + (run * NPAIR + 1 + AHEAD))
                acc = U[:, bass.ds(g, 1), :].rearrange("p a n -> p (a n)")
                V.tensor_tensor(acc, acc, PM[:, n % 2, :], ALU.add).then_inc(pair_added, 1)
                dve.wait_ge(pair_added, pair + (run * NPAIR + 1 + AHEAD))

            def steps(prepare, add):
                def step(i, s, pairs):
                    i, s = normal(i, s)
                    for pair, n in pairs:
                        prepare(pair, n)
                        if n > 0:
                            add(pair - 1, n - 1)
                    if s % 2 == 0 and s > 0:
                        w_low_next(i, s // 2 - 1)
                return step

            dve.sem_inc(pair_added, AHEAD)
            dve.sem_inc(cells_added, AHEAD)
            x_low(0)
            for k in range(KT):
                if k == KT // 2:
                    x_low(1)
                w_low(k, k, whi[:, 0, :, :], wlo[:, 0, :, :], wraw[:, 0, :, :])
            for jt in range(TILES_BODY):
                if jt + 2 < NT:
                    x_low(jt + 2)
                w_low_next(0, jt)
                sort_step(jt)
            dve.wait_ge(consts, 2)
            for jt in range(TILES_BODY):
                w_low_next(1, jt)
                if jt < ECOL // CHUNK:
                    hot_chunk(jt)
                if jt == ECOL // CHUNK + 2:
                    inverse_counts()
            nothing = steps(None, None)
            plain((2, 0), SETUP_AT, nothing)
            count_setup()
            plain(SETUP_AT, COUNT_AT, nothing)
            one_each(dve, COUNT_AT, steps(count_hot, count_add), count_add)
            dve.wait_ge(count_out, 16)
            V.memset(WORK[:, NT * HW:7 * D], 0.0)
            V.memset(WORK[:, 0:NT * HW], 0.0).then_inc(work_clear, 1)
            dve.wait_ge(work_clear, 1)
            plain(phase_end(COUNT_AT), RUN0_AT, nothing)

            def add0(pair, n):
                msg_add(pair, n, 0)

            def add1(pair, n):
                msg_add(pair, n, 1)

            one_each(dve, RUN0_AT, steps(lambda pair, n: msg_low(pair, n, 0), add0), add0)
            dve.wait_ge(agg_out, 16)
            V.tensor_scalar(REC[:, :, 0], REC[:, :, 0], float(YROWS), None, ALU.add)
            V.memset(WORK[:, 0:NT * HW], 0.0).then_inc(work_clear, 1)
            dve.wait_ge(work_clear, 2)
            plain(phase_end(RUN0_AT), (RUN1_BODY, 0), nothing)
            dense(dve, RUN1_BODY, steps(lambda pair, n: msg_low(pair, n, 1), add1), add1)

            for k in range(KT):
                w_low((UNITS_Y + 5) * KT + k, k, whi[:, 1, :, :], wlo[:, 1, :, :], wraw[:, 1, :, :])

            def gcn_low(h):
                cols = slice(h * HW, (h + 1) * HW)
                for k in range(KT):
                    w_low((UNITS_Y + 6 + h) * KT + k, k, gcn_hi[:, :, cols], gcn_lo[:, :, cols], gcn_raw[:, :, cols])

            def make_u(t):
                dve.wait_ge(root_ready, t + 1)
                after(dve, u_turned, t)
                after(dve, tanh_done, t)
                V.tensor_tensor(slot[4], slot[0], slot[1], ALU.add).then_inc(u_ready, 1)

            def u_low(t):
                dve.wait_ge(u_hi, t * 2 + 2)
                V.tensor_tensor(ut_lo[:, 0:HW], PM[:, 0, :], ut_hi[:, 0:HW].bitcast(F32), ALU.subtract)
                V.tensor_tensor(ut_lo[:, HW:D], PM[:, 1, :], ut_hi[:, HW:D].bitcast(F32), ALU.subtract).then_inc(u_split, 1)

            def norm(y, ready, t):
                for h in range(2):
                    last = V.bn_stats(STATS[:, h, :], y[:, h * HW:(h + 1) * HW])
                link(last)
                dve.sem_inc(passed_dve, 1)
                link(V.bn_aggr(MV[:, :], STATS[:, :, :].rearrange("p a b -> p (a b)")))
                V.tensor_scalar(VAR[:, :], MV[:, 1:2], EPS, None, ALU.add).then_inc(var_ready, 1)
                dve.wait_ge(rstd_ready, t + 1)
                V.tensor_scalar(y, y, MV[:, 0:1], RSTD[:, 0:1], ALU.subtract, ALU.mult).then_inc(ready, 1)

            def make_x1(t):
                dve.wait_ge(tanh_done, t + 1)
                dve.wait_ge(gate_ready, t + 1)
                V.tensor_tensor(slot[5], slot[5], slot[3], ALU.subtract)
                dve.wait_ge(z_done, t + 1)
                V.tensor_tensor(slot[2][:, 0:HW], PG[:, 0, :], slot[2][:, 0:HW], ALU.add)
                V.tensor_tensor(slot[2][:, HW:D], PG[:, 1, :], slot[2][:, HW:D], ALU.add).then_inc(z_read, 1)
                dve.wait_ge(z_read, t + 1)
                after(dve, x1_turned, t)
                after(dve, x1_out, t * 16)
                link(V.tensor_tensor(slot[2], slot[2], slot[5], ALU.mult))
                link(V.scalar_tensor_tensor(slot[6], slot[3], 2.0, slot[2], ALU.mult, ALU.add))
                norm(slot[6], x1_ready, t)

            def h_low(t, high, low):
                dve.wait_ge(h_hi, t * 2 + 2)
                sc = DINV[:, bass.ds(t, 1)]
                V.scalar_tensor_tensor(low[:, 0:HW], PG[:, 2, :], sc, high[:, 0:HW].bitcast(F32), ALU.mult, ALU.subtract)
                V.scalar_tensor_tensor(low[:, HW:D], PG[:, 3, :], sc, high[:, HW:D].bitcast(F32), ALU.mult,
                                       ALU.subtract).then_inc(h_split, 1)

            def x1_low(t):
                dve.wait_ge(x1_hi, t * 2 + 2)
                V.tensor_tensor(SPLO[:, 0:HW], PM[:, 2, :], SPHI[:, 0:HW].bitcast(F32), ALU.subtract)
                V.tensor_tensor(SPLO[:, HW:D], PM[:, 3, :], SPHI[:, HW:D].bitcast(F32), ALU.subtract).then_inc(x1_split, 1)

            X1_STEPS = 4
            make_u(0)
            u_low(0)
            make_u(1)
            gcn_low(0)
            u_low(1)
            make_x1(0)
            make_u(2)
            gcn_low(1)
            x1_low(0)
            with dve.Fori(0, NT - 3) as i:
                chain.enter(i, X1_STEPS)
                u_low(i + 2)
                make_x1(i + 1)
                h_low(i, HST_HI[:, :], HST_LO[:, :])
                x1_low(i + 1)
                make_u(i + 3)
            chain.leave(NT - 3, X1_STEPS)
            u_low(NT - 1)
            make_x1(NT - 2)
            h_low(NT - 3, HST_HI[:, :], HST_LO[:, :])
            x1_low(NT - 2)
            make_x1(NT - 1)
            h_low(NT - 2, SPHI[:, D:2 * D], SPLO[:, D:2 * D])
            x1_low(NT - 1)
            h_low(NT - 1, ut_hi, ut_lo)

            def counts_split(d, b):
                dve.wait_ge(c_in[b], (d - b) * 8 + 16)
                dve.wait_ge(h_done, NT)
                after(dve, conv_done, d - 1)
                hi = XHI[:, b * NPAD:(b + 1) * NPAD]
                link(V.tensor_copy(hi, CIN[b][:, :]))
                V.tensor_tensor(XLO[:, b * NPAD:(b + 1) * NPAD], CIN[b][:, :], hi.bitcast(F32), ALU.subtract).then_inc(c_split, 1)

            def finish(d, b):
                y = slot[2 + b]
                dve.wait_ge(conv_done, d + 1)
                after(dve, out_done[b], (d - b) * 8)
                for h in range(2):
                    last = V.scalar_tensor_tensor(y[:, h * HW:(h + 1) * HW], PG[:, 2 * b + h, :], DINV[:, bass.ds(d, 1)],
                                                  BIAS_GCN[:, h * HW:(h + 1) * HW], ALU.mult, ALU.add)
                last.then_inc(conv_read, 1)
                dve.wait_ge(conv_read, d + 1)
                dve.wait_ge(res_in[b], (d - b) * 8 + 16)
                link(V.scalar_tensor_tensor(y, y, 0.0, slot[b], ALU.max, ALU.add))
                norm(y, out_ready, d + NT)

            counts_split(0, 0)
            counts_split(1, 1)
            dve.wait_ge(bias1_in, 16)
            finish(0, 0)

            def two_tiles(i):
                counts_split(2 * i + 2, 0)
                finish(2 * i + 1, 1)
                counts_split(2 * i + 3, 1)
                finish(2 * i + 2, 0)

            two_tiles(0)
            with dve.Fori(1, NT // 2 - 1) as i:
                chain.enter(i - 1, 8)
                two_tiles(i)
            chain.leave(NT // 2 - 2, 8)
            finish(NT - 1, 1)


_INS = ['x', 'src', 'dst', 'edge_type_8', 'L0_gnn_weight', 'L0_gnn_root', 'L0_gnn_bias', 'L0_gnn_w_gate', 'L0_gnn_b_gate',
        'L1_gnn_W', 'L1_gnn_b']
_OUTS = [((N, D), 'float32')]


def kernel(**inputs):
    import numpy as _np
    import concourse.bacc as _bacc
    from concourse import mybir as _mybir
    from concourse.bass_utils import run_bass_kernel_spmd as _run

    nc = _bacc.Bacc("TRN2", target_bir_lowering=False, num_devices=1)
    arrays, args = {}, []
    for name in _INS:
        a = _np.ascontiguousarray(inputs[name])
        arrays[f"in_{name}_dram"] = a
        args.append(nc.dram_tensor(f"in_{name}_dram", a.shape, _mybir.dt.from_np(a.dtype), kind="ExternalInput").ap())
    for i, (shape, dtype) in enumerate(_OUTS):
        dt = _mybir.dt.from_np(_np.dtype(dtype))
        args.append(nc.dram_tensor(f"out_{i}_dram", shape, dt, kind="ExternalOutput").ap())
    gnn_resnorm_kernel(nc, *args)
    r = _run(nc, [arrays], core_ids=[0])
    return r.results[0]["out_0_dram"]
```

```python
import concourse.bass as bass
from concourse import mybir
from contextlib import ExitStack

F32 = mybir.dt.float32
F32R = mybir.dt.float32r
F16 = mybir.dt.float16
BF16 = mybir.dt.bfloat16
I32 = mybir.dt.int32
I16 = mybir.dt.int16
ALU = mybir.AluOpType
ACT = mybir.ActivationFunctionType
AXIS_X = mybir.AxisListType.X

P = 128
N, D, R, E = 1250, 1024, 8, 20000
NT = (N + P - 1) // P
NPAD = NT * P
LAST = N - (NT - 1) * P
KT = D // P
HW = 512
EPART, ECOL = 125, E // 125
PAIR = 2 * P
NPAIR = (E + NT * (PAIR - 1)) // PAIR
ETILES = 2 * NPAIR
NKEY = NT * R
FAR = 1 << 20
RING = 8
EPS = 1e-5

UNITS_Y = 2 * R
TILES_BODY = 2 * NT
SUBSTEPS = 2 * TILES_BODY
YROWS = R * NPAD
NCOL = NPAD // 2
HIGH_CELL = 1 << 16
EXACT = 256
AHEAD = 2


COUNT_AT = (3, 0)
RUN0_AT = (5, 20)
RUN1_BODY = 8
SETUP_AT = (2, 32)
LATE = 5
DENSE = NPAIR // 2


def dense_pairs():
    steps = SUBSTEPS - LATE
    bounds = [0] * LATE + [k * DENSE // steps for k in range(steps + 1)]
    return [range(bounds[s], bounds[s + 1]) for s in range(SUBSTEPS)]


DENSE_PAIRS = dense_pairs()


def one_each(eng, at, step, last=None):
    body, s0 = at
    with eng.Fori(body, body + 2) as i:
        for n in range(SUBSTEPS):
            step(i, s0 + n, [((i - body) * SUBSTEPS + n, n)])
        if last is not None:
            last((i - body) * SUBSTEPS + (SUBSTEPS - 1), SUBSTEPS - 1)
    rest = NPAIR - 2 * SUBSTEPS
    for n in range(rest):
        step(body + 2, s0 + n, [(2 * SUBSTEPS + n, n)])
    if last is not None:
        last(NPAIR - 1, rest - 1)


def dense(eng, body, step, last=None):
    with eng.Fori(body, body + 2) as i:
        for s in range(SUBSTEPS):
            step(i, s, [((i - body) * DENSE + n, n) for n in DENSE_PAIRS[s]])
        if last is not None:
            last((i - body) * DENSE + (DENSE - 1), DENSE - 1)


def plain(start, end, step):
    for n in range(start[0] * SUBSTEPS + start[1], end[0] * SUBSTEPS + end[1]):
        step(n // SUBSTEPS, n % SUBSTEPS, [])


def phase_end(at):
    return at[0] + (at[1] + NPAIR) // SUBSTEPS, (at[1] + NPAIR) % SUBSTEPS


def normal(i, s):
    return (i + s // SUBSTEPS if s >= SUBSTEPS else i), s % SUBSTEPS


class Chain:

    def __init__(self, eng, sem):
        self.eng, self.sem, self.at, self.steps = eng, sem, 0, 0

    def link(self, ins):
        ins.then_inc(self.sem, 1)
        self.at = self.at + 1
        self.steps += 1
        self.eng.wait_ge(self.sem, self.at)

    def enter(self, turn, per_turn):
        self.before, self.steps = self.at, 0
        self.at = turn * per_turn + self.before

    def leave(self, turns, per_turn):
        assert self.steps == per_turn, (self.steps, per_turn)
        self.at = self.before + turns * per_turn


def gnn_resnorm_kernel(nc, x, src, dst, edge_type, w_rel, w_root, b_root, w_gate, b_gate, w_gcn, b_gcn, out):
    def dram(name, shape, dt=F32):
        return nc.dram_tensor(name, shape, dt, kind="Internal").ap()

    y_d = dram("y", ((UNITS_Y + 4) * NPAD, HW))
    agg_d = dram("agg", (NPAD, HW))
    x1_d = dram("x1", (NPAD, D))
    count_d = dram("edge_count", (P, NT * NPAD), I16)
    hhi_d = dram("h_hi", (KT * P, D))
    hlo_d = dram("h_lo", (KT * P, D))
    rec_d = dram("records", (P * ETILES, 4), I32)
    inv_d = dram("inverse_count", (P * NKEY, 1))

    ctx = ExitStack()
    with ctx:
        KB = 1024
        base = (nc.sbuf_base + 63) // 64 * 64
        at = {}
        for name, size in (("xt_hi", KT * NPAD * 4), ("xt_lo", KT * NPAD * 4), ("w_hi", 32 * KB), ("w_lo", 32 * KB),
                           ("work", 28 * KB), ("split_hi", 8 * KB), ("split_lo", 8 * KB), ("raw_w", 4 * KB),
                           ("stage", 4 * KB), ("onehot", 2 * KB), ("early", 4 * KB), ("records", 4 * KB)):
            at[name] = base
            base += size

        def place(name, shape, dt, where, skip=0):
            return nc.alloc_sbuf_tensor_at(name, shape, dt, offset=at[where] + skip)

        def small(name, shape, dt):
            nonlocal base
            t = nc.alloc_sbuf_tensor_at(name, shape, dt, offset=base)
            size = mybir.dt.size(dt)
            for s in shape[1:]:
                size *= s
            base += (size + 31) // 32 * 32
            return t

        XHI = place("XHI", [P, KT * NPAD], F32R, "xt_hi")
        XLO = place("XLO", [P, KT * NPAD], F32R, "xt_lo")
        WHI = place("WHI", [P, 2 * KT * HW], F32R, "w_hi")
        WLO = place("WLO", [P, 2 * KT * HW], F32R, "w_lo")
        WORK = place("WORK", [P, 7 * D], F32, "work")
        SPHI = place("SPHI", [P, 2 * D], F32R, "split_hi")
        SPLO = place("SPLO", [P, 2 * D], F32R, "split_lo")
        STAGE = place("STAGE", [P, 2, HW], F32, "stage")
        ONEHOT = place("ONEHOT", [P, 2, 2, P], F32R, "onehot")
        xhi = XHI[:, :].rearrange("p (k n) -> p k n", k=KT)
        xlo = XLO[:, :].rearrange("p (k n) -> p k n", k=KT)
        GCN = 2 * KT * HW
        gcn_hi = XHI[:, 0:GCN].rearrange("p (k n) -> p k n", k=KT)
        gcn_lo = XLO[:, 0:GCN].rearrange("p (k n) -> p k n", k=KT)
        UT = GCN
        ut_hi, ut_lo = XHI[:, UT:UT + D], XLO[:, UT:UT + D]
        BIAS_GATE = place("BIAS_GATE", [P, D], F32, "xt_lo", (UT + D) * 4)
        BIAS_GCN = place("BIAS_GCN", [P, D], F32, "xt_hi", 4 * NPAD * 4)
        wraw = place("WRAW", [P, 2 * KT * HW], F32, "w_lo")[:, :].rearrange("p (b k n) -> p b k n", b=2, k=KT)
        gcn_raw = place("GCNRAW", [P, GCN], F32, "xt_lo")[:, :].rearrange("p (k n) -> p k n", k=KT)
        whi = WHI[:, :].rearrange("p (b k n) -> p b k n", b=2, k=KT)
        wlo = WLO[:, :].rearrange("p (b k n) -> p b k n", b=2, k=KT)
        hhi = WHI[:, :].rearrange("p (s n) -> p s n", s=KT)
        hlo = WLO[:, :].rearrange("p (s n) -> p s n", s=KT)
        sp_hi = SPHI[:, :].rearrange("p (r e n) -> p r e n", r=2, e=2)
        sp_lo = SPLO[:, :].rearrange("p (r e n) -> p r e n", r=2, e=2)
        HST_HI = place("HST_HI", [P, D], F32R, "stage")
        HST_LO = place("HST_LO", [P, D], F32R, "xt_hi", (UT + D) * 4)
        CIN = [place("CIN0", [P, NPAD], I16, "stage"), place("CIN1", [P, NPAD], I16, "raw_w")]
        U = WORK[:, 0:NT * HW].rearrange("p (g n) -> p g n", g=NT)
        COUNT = WORK[:, 0:NT * NPAD // 2].bitcast(I16).rearrange("p (g n) -> p g n", g=NT)
        RAW2 = place("RAW2", [P, 2, HW], F32, "raw_w")
        RAW3 = place("RAW3", [P, 2, HW], F32, "early")
        raw = [WORK[:, 5 * D + r * HW:5 * D + (r + 1) * HW] for r in range(4)] + [RAW2[:, 0, :], RAW2[:, 1, :], RAW3[:, 0, :], RAW3[:, 1, :]]
        ROWS = len(raw)
        XIN = WORK[:, 5 * D:7 * D].rearrange("p (r n) -> p r n", r=2)
        BIAS_ROOT, ROOT = WORK[:, 5 * D:6 * D], WORK[:, 6 * D:7 * D]
        USUM = place("USUM", [P, D], F32, "raw_w")[:, :]
        SUMS = place("SUMS", [P, HW], F32, "onehot")[:, :]
        XROWS = place("XROWS", [P, D], F32, "records")[:, :]
        TANH = place("TANH", [P, D], F32, "early")[:, :]
        GATE = place("GATE", [P, D], F32, "split_hi", 4 * D)[:, :]
        X1 = place("X1", [P, D], F32, "split_lo", 4 * D)[:, :]
        HLAST = place("HLAST", [P, 2, D], F32R, "work")
        res = [WORK[:, (2 + b) * D:(3 + b) * D] for b in range(2)]
        result = [WORK[:, (5 + b) * D:(6 + b) * D] for b in range(2)]
        CHUNK = 16
        KEYHOT = place("KEYHOT", [P, 2, CHUNK, NKEY], F16, "split_hi")
        LOCHOT = place("LOCHOT", [P, 2, CHUNK, P], F16, "split_lo")
        DSTHOT = place("DSTHOT", [P, 4, NCOL], BF16, "split_hi")
        SRCHOT = place("SRCHOT", [P, 4, P], BF16, "split_hi", 4 * NCOL * 2)
        TALLY = place("TALLY", [P, 2, NCOL], I32, "split_lo")
        WORTH = place("WORTH", [P, ETILES], F32, "raw_w")
        PADREC = place("PADREC", [P, ETILES, 4], I32, "split_hi")
        MEMB = WORK[0:EPART, 0:NT * ECOL].rearrange("p (g c) -> p g c", g=NT)
        SCAN = [WORK[0:EPART, (1 + b) * NT * ECOL:(2 + b) * NT * ECOL].rearrange("p (g c) -> p g c", g=NT) for b in range(2)]

        def temp(n, dt=F32):
            return WORK[0:EPART, NT * ECOL + n * ECOL:NT * ECOL + (n + 1) * ECOL].bitcast(dt)

        T_SRC, T_DST, T_TYPE, T_LOC, T_GRP, T_GRPF = temp(0, I32), temp(1, I32), temp(2, I32), temp(3, I32), temp(4, I32), temp(5)
        T_LOCF = temp(6)
        O_POS = temp(0)
        O_POSI, O_LANE, O_TILE = temp(1, I32), temp(2, I32), temp(3, I32)
        EARLIER = WORK[0:EPART, 3 * NT * ECOL:3 * NT * ECOL + EPART]
        ONES = WORK[0:EPART, 3 * NT * ECOL + P:3 * NT * ECOL + 2 * P]
        KEY = place("KEY", [EPART, ECOL], F32, "onehot")

        REC = place("REC", [P, ETILES, 4], I32, "records")
        W_EDGE = place("W_EDGE", [P, ETILES], F32, "records", 16 * ETILES)
        RREC = place("RREC", [P, 2, RING, 4], I32, "records", 20 * ETILES)
        IOTA = small("IOTA", [P, P], F16)
        IDENT = small("IDENT", [P, P], F32)
        IDX = small("IDX", [P, 2, RING], I32)
        WGOT = small("WGOT", [P, 2, RING], F32)
        GROUP = small("GROUP", [1, NPAIR], I32)
        DINV = small("DINV", [P, NT], F32)
        SRC_LOC = place("SRC_LOC", [P, ETILES], F32, "early")
        CELL = place("CELL", [P, ETILES], F32, "early", 4 * ETILES)
        ADDR = place("ADDR", [EPART, ECOL], I32, "early", 8 * ETILES)
        COLS = place("COLS", [P, NCOL], F16, "early", 8 * ETILES + 4 * ECOL)
        INV = place("INV", [P, NKEY], F32, "early", 8 * ETILES + 4 * ECOL + 2 * NCOL)
        T10 = place("T10", [P, 4, NT], F32, "onehot", 768)
        T10I = place("T10I", [P, NT], I32, "onehot", 928)
        DEG = place("DEG", [P, NT], F32, "onehot", 1792)
        DEG_MAX = small("DEG_MAX", [P, 1], F32)
        LARGE = small("LARGE", [1, 1], I32)
        STATS = small("STATS", [P, 2, 6], F32)
        MV = small("MV", [P, 2], F32)
        VAR = small("VAR", [P, 1], F32)
        RSTD = small("RSTD", [P, 1], F32)
        MINUS_HALF = small("MINUS_HALF", [P, NT], F32)
        assert base <= nc.sbuf_usable_end, (base, nc.sbuf_usable_end)
        PAIRSUM = place("PAIRSUM", [1, 2, NPAIR], F32, "onehot", 1024)

        PG = ctx.enter_context(nc.psum_tensor("PG", [P, 4, HW], F32))
        PM = ctx.enter_context(nc.psum_tensor("PM", [P, 4, HW], F32))

        def sem(name):
            return ctx.enter_context(nc.semaphore(name))

        x_in = [sem(f"x_in{b}") for b in range(2)]
        x_turned = sem("x_turned")
        x_hi = sem("x_hi")
        x_split = sem("x_split")
        w0_in = [sem(f"w0_in{k}") for k in range(KT)]
        w_in = [sem(f"w_in{b}") for b in range(2)]
        w_hi = sem("w_hi")
        w_split = sem("w_split")
        gemm_done = sem("gemm_done")
        evac_done = sem("evac_done")
        y_out = [sem(f"y_out{b}") for b in range(2)]
        edges_in = sem("edges_in")
        consts = sem("consts")
        rows_total = sem("rows_total")
        offsets = sem("offsets")
        pos_ready = sem("pos_ready")
        pad_set = sem("pad_set")
        pad_out = sem("pad_out")
        idx_set = sem("idx_set")
        scattered = [sem(f"scattered{b}") for b in range(2)]
        sorted_in = sem("sorted_in")
        chunk_ready = sem("chunk_ready")
        chunk_done = sem("chunk_done")
        inv_ready = sem("inv_ready")
        inv_out = sem("inv_out")
        w_got = [sem(f"w_got{b}") for b in range(2)]
        w_ready = sem("w_ready")
        deg_ready = sem("deg_ready")
        dinv_ready = sem("dinv_ready")
        hot_ready = sem("hot_ready")
        cells_done = sem("cells_done")
        deg_max_ready = sem("deg_max_ready")
        deg_max_turned = sem("deg_max_turned")
        large_ready = sem("large_ready")
        cells_taken = sem("cells_taken")
        cells_added = sem("cells_added")
        count_out = sem("count_out")
        work_clear = sem("work_clear")
        got = [sem(f"got{b}") for b in range(ROWS)]
        msg_hi = sem("msg_hi")
        msg_split = sem("msg_split")
        pair_ready = sem("pair_ready")
        pair_done = sem("pair_done")
        pair_added = sem("pair_added")
        agg_out = sem("agg_out")
        bias_in = sem("bias_in")
        bias_gate_in = sem("bias_gate_in")
        sums0_in = sem("sums0_in")
        u_in = sem("u_in")
        z_in = sem("z_in")
        root_ready = sem("root_ready")
        gate_ready = sem("gate_ready")
        u_ready = sem("u_ready")
        u_turned = sem("u_turned")
        u_hi = sem("u_hi")
        u_split = sem("u_split")
        tanh_done = sem("tanh_done")
        z_done = sem("z_done")
        z_read = sem("z_read")
        x1_ready = sem("x1_ready")
        x1_turned = sem("x1_turned")
        x1_hi = sem("x1_hi")
        x1_split = sem("x1_split")
        x1_out = sem("x1_out")
        var_ready = sem("var_ready")
        rstd_ready = sem("rstd_ready")
        h_done = sem("h_done")
        h_hi = sem("h_hi")
        h_split = sem("h_split")
        h_out = sem("h_out")
        h_in = [sem(f"h_in{s}") for s in range(KT)]
        c_in = [sem(f"c_in{b}") for b in range(2)]
        c_high = sem("c_high")
        c_split = sem("c_split")
        conv_done = sem("conv_done")
        conv_read = sem("conv_read")
        res_in = [sem(f"res_in{b}") for b in range(2)]
        bias1_in = sem("bias1_in")
        out_ready = sem("out_ready")
        out_done = [sem(f"out_done{b}") for b in range(2)]
        passed_pool = sem("passed_pool")
        passed_dve = sem("passed_dve")
        dve_chain = sem("dve_chain")
        pool_chain = sem("pool_chain")

        block = ctx.enter_context(nc.Block())

        def after(eng, s, value):
            if not (isinstance(value, int) and value <= 0):
                eng.wait_ge(s, value)

        @block.sync
        def _(sp):
            def load_w(raw, b, weight, h):
                for c in range(2):
                    rows = weight[c * (D // 2):(c + 1) * (D // 2), h * HW:(h + 1) * HW]
                    sp.dma_start(raw[:, c * (KT // 2):(c + 1) * (KT // 2), :],
                                 rows.rearrange("(k p) n -> p k n", p=P)).then_inc(w_in[b], 16)

            def load_unit(n, b, weight, h):
                sp.wait_ge(gemm_done, (n - 1) * NT)
                load_w(wraw[:, b, :, :], b, weight, h)

            def load_x(t):
                if t >= 2:
                    sp.wait_ge(x_turned, 2 * (t - 1))
                rows = min(P, N - t * P)
                sp.dma_start(XIN[0:rows, t % 2, :], x[t * P:t * P + rows, :]).then_inc(x_in[t % 2], 16)

            def first_unit(k):
                sp.dma_start(wraw[:, 0, k, :], w_rel[0][k * P:(k + 1) * P, 0:HW]).then_inc(w0_in[k], 16)

            load_x(0)
            for k in range(KT // 2):
                first_unit(k)
            load_x(1)
            for k in range(KT // 2, KT):
                first_unit(k)
            for temp_i, a in ((T_SRC, src), (T_DST, dst), (T_TYPE, edge_type)):
                sp.dma_start(temp_i, a.rearrange("(p c) -> p c", p=EPART)).then_inc(edges_in, 16)
            load_x(2)
            load_x(3)
            load_w(wraw[:, 1, :, :], 1, w_rel[1], 0)
            for t in range(4, NT):
                load_x(t)
            for h in range(2):
                with sp.Fori(1 - h, R // 2) as i:
                    for b in range(2):
                        weight = w_rel[bass.ds(2 * i + b, 1), :, :].rearrange("a p n -> (a p) n")
                        load_unit(2 * i + (b + h * R), b, weight, h)
            for n, (weight, h) in enumerate([(w_root, 0), (w_root, 1), (w_gate[D:2 * D], 0), (w_gate[D:2 * D], 1),
                                             (w_gate[0:D], 0)]):
                load_unit(UNITS_Y + n, n % 2, weight, h)

            root_d, gate_d = (y_d[u * NPAD:(u + 2) * NPAD, :].rearrange("(h n) c -> n h c", h=2) for u in (UNITS_Y, UNITS_Y + 2))

            def load_root(t):
                sp.dma_start(ROOT.rearrange("p (h n) -> p h n", h=2), root_d[bass.ds(t * P, P), :, :]).then_inc(u_in, 16)

            def load_u(t):
                after(sp, u_ready, t)
                sp.dma_start(SUMS, agg_d[bass.ds(t * P, P), :]).then_inc(u_in, 16)
                load_root(t)

            def load_z(t):
                after(sp, x1_ready, t)
                sp.dma_start(GATE.rearrange("p (h n) -> p h n", h=2), gate_d[bass.ds(t * P, P), :, :]).then_inc(z_in, 16)
                if isinstance(t, int) and t == NT - 1:
                    sp.dma_start(XROWS[0:LAST, :], x[t * P:N, :]).then_inc(z_in, 16)
                else:
                    sp.dma_start(XROWS, x[bass.ds(t * P, P), :]).then_inc(z_in, 16)

            for b in range(2):
                sp.wait_ge(y_out[b], 16 * (UNITS_Y + 2) * NT // 2)
            sp.wait_ge(agg_out, 16)
            sp.wait_ge(msg_split, 2 * ETILES - (ROWS - 2))
            sp.dma_start(BIAS_ROOT, b_root.partition_broadcast(P)).then_inc(bias_in, 16)
            sp.wait_ge(msg_split, 2 * ETILES - (ROWS - 4))
            load_root(0)
            sp.wait_ge(msg_split, 2 * ETILES - (ROWS - 6))
            sp.dma_start(USUM[:, 0:HW], agg_d[0:P, :]).then_inc(sums0_in, 16)
            load_unit(UNITS_Y + 5, 1, w_gate[0:D], 1)
            load_u(1)
            sp.wait_ge(gemm_done, (UNITS_Y + 4) * NT)
            sp.dma_start(BIAS_GATE[:, :], b_gate.partition_broadcast(P)).then_inc(bias_gate_in, 16)
            for b in range(2):
                sp.wait_ge(y_out[b], 16 * (UNITS_Y + 4) * NT // 2)
            load_z(0)
            load_w(gcn_raw[:, :, 0:HW], 0, w_gcn, 0)
            sp.wait_ge(w_split, (UNITS_Y + 6) * KT)
            load_w(gcn_raw[:, :, HW:D], 1, w_gcn, 1)
            load_u(2)
            with sp.Fori(0, NT - 3) as i:
                load_z(i + 1)
                load_u(i + 3)
            load_z(NT - 2)
            load_z(NT - 1)

            sp.wait_ge(z_done, NT)
            for s in range(KT):
                sp.wait_ge(h_out, 32 * (s + 1))
                sp.dma_start(hhi[:, s, :].bitcast(F32), hhi_d[s * P:(s + 1) * P, :]).then_inc(h_in[s], 16)
                sp.dma_start(hlo[:, s, :].bitcast(F32), hlo_d[s * P:(s + 1) * P, :]).then_inc(h_in[s], 16)

            def load_c(d, b):
                after(sp, c_split, d - 1)
                sp.dma_start(CIN[b][:, :], count_d[:, bass.ds(d * NPAD, NPAD)]).then_inc(c_in[b], 16)

            def load_res(d, b):
                after(sp, out_ready, d - 1)
                sp.dma_start(res[b], x1_d[bass.ds(d * P, P), :]).then_inc(res_in[b], 16)

            sp.wait_ge(tanh_done, NT)
            for b in range(2):
                load_c(b, b)
            sp.wait_ge(x1_out, 16 * NT)
            sp.wait_ge(h_done, NT)
            sp.dma_start(BIAS_GCN[:, :], b_gcn.partition_broadcast(P)).then_inc(bias1_in, 16)
            for b in range(2):
                load_res(b, b)
            with sp.Fori(1, NT // 2) as i:
                for b in range(2):
                    load_c(2 * i + b, b)
                    load_res(2 * i + b, b)

        @block.gpsimd
        def _(pool):
            chain = Chain(pool, pool_chain)
            link = chain.link
            link(nc.gpsimd.memset(IDENT[:, :], 0.0))
            nc.gpsimd.affine_select(out=IDENT[:, :], in_=IDENT[:, :], compare_op=ALU.not_equal, fill=1.0, base=0,
                                    pattern=[[-1, P]], channel_multiplier=1).then_inc(consts, 1)
            nc.gpsimd.iota(COLS[:, :], pattern=[[1, NCOL]], base=0, channel_multiplier=0,
                           allow_small_or_imprecise_dtypes=True).then_inc(consts, 1)
            nc.gpsimd.iota(IOTA[:, :], pattern=[[1, P]], base=0, channel_multiplier=0,
                           allow_small_or_imprecise_dtypes=True).then_inc(consts, 1)
            link(nc.gpsimd.memset(EARLIER, 1.0))
            nc.gpsimd.affine_select(out=EARLIER, in_=EARLIER, compare_op=ALU.is_gt, fill=0.0, base=0,
                                    pattern=[[1, EPART]], channel_multiplier=-1).then_inc(consts, 1)
            nc.gpsimd.memset(ONES, 1.0).then_inc(consts, 1)
            nc.gpsimd.memset(MINUS_HALF[:, :], -0.5).then_inc(consts, 1)
            nc.gpsimd.iota(PAIRSUM[:, 1, :], pattern=[[PAIR, NPAIR]], base=0, channel_multiplier=0,
                           allow_small_or_imprecise_dtypes=True).then_inc(consts, 1)
            link(nc.gpsimd.memset(WGOT[:, :, :], 0.0))
            nc.gpsimd.memset(PADREC[:, :, 0:2], FAR).then_inc(pad_set, 1)
            nc.gpsimd.memset(PADREC[:, :, 2:3].bitcast(F32), -1.0).then_inc(pad_set, 1)
            nc.gpsimd.memset(PADREC[:, :, 3:4], 0).then_inc(pad_set, 1)
            pool.wait_ge(pad_set, 3)
            pool.dma_start(rec_d.rearrange("(p t) f -> p (t f)", p=P),
                           PADREC[:, :, :].rearrange("p t f -> p (t f)")).then_inc(pad_out, 16)
            pool.wait_ge(pad_out, 16)

            pool.wait_ge(pos_ready, 1)

            def scatter_half(i, b, peeled):
                if not peeled:
                    pool.wait_ge(scattered[b], i * (16 * RING))
                pool.wait_ge(pos_ready, 1)
                col = bass.ds(i * (2 * RING) + b * RING, RING)
                nc.gpsimd.tensor_copy(IDX[0:EPART, b, :], ADDR[:, col]).then_inc(idx_set, 1)
                nc.gpsimd.tensor_copy(RREC[0:EPART, b, :, :], REC[0:EPART, col, :]).then_inc(idx_set, 1)
                pool.wait_ge(idx_set, i * 4 + (2 * b + 2))
                pool.sem_inc(passed_pool, 1)
                for j in range(RING):
                    pool.indirect_dma_start(
                        out=rec_d, out_offset=bass.IndirectOffsetOnAxis(ap=IDX[0:EPART, b, j:j + 1], axis=0),
                        in_=RREC[0:EPART, b, j, :], in_offset=None).then_inc(scattered[b], 16)

            turns = ECOL // (2 * RING)
            for b in range(2):
                scatter_half(0, b, True)
            with pool.Fori(1, turns) as i:
                for b in range(2):
                    scatter_half(i, b, False)
            for b in range(2):
                pool.wait_ge(scattered[b], 16 * RING * turns)
            pool.wait_ge(chunk_ready, ECOL // CHUNK)
            pool.dma_start(REC[:, :, :].rearrange("p t f -> p (t f)"),
                           rec_d.rearrange("(p t) f -> p (t f)", p=P)).then_inc(sorted_in, 16)
            pool.wait_ge(sorted_in, 16)

            pool.wait_ge(deg_ready, 1)
            nc.gpsimd.tensor_tensor(DINV[:, :], DEG[:, :], MINUS_HALF[:, :], ALU.pow).then_inc(dinv_ready, 1)
            pool.wait_ge(inv_ready, 1)
            pool.dma_start(inv_d.rearrange("(p k) a -> p (k a)", p=P), INV[:, :]).then_inc(inv_out, 16)
            pool.wait_ge(inv_out, 16)

            IDX_BASE = 2 * 2 * turns

            def weight_half(i, b, peeled):
                tiles = bass.ds(i * (2 * RING) + b * RING, RING)
                if not peeled:
                    pool.wait_ge(w_got[b], i * (16 * RING))
                    pool.wait_ge(sorted_in, 16)
                    nc.gpsimd.tensor_copy(W_EDGE[:, bass.ds((i - 1) * (2 * RING) + b * RING, RING)], WGOT[:, b, :]).then_inc(w_ready, 1)
                    pool.wait_ge(w_ready, (i - 1) * 2 + (b + 1))
                pool.wait_ge(sorted_in, 16)
                nc.gpsimd.tensor_copy(IDX[:, b, :], REC[:, tiles, 1]).then_inc(idx_set, 1)
                pool.wait_ge(idx_set, i * 2 + (IDX_BASE + b + 1))
                pool.sem_inc(passed_pool, 1)
                for j in range(RING):
                    pool.indirect_dma_start(
                        out=WGOT[:, b, j:j + 1], out_offset=None, in_=inv_d,
                        in_offset=bass.IndirectOffsetOnAxis(ap=IDX[:, b, j:j + 1], axis=0),
                        bounds_check=P * NKEY - 1, oob_is_err=False).then_inc(w_got[b], 16)

            turns_w = ETILES // (2 * RING)
            for b in range(2):
                weight_half(0, b, True)
            with pool.Fori(1, turns_w) as i:
                for b in range(2):
                    weight_half(i, b, False)
            for b in range(2):
                pool.wait_ge(w_got[b], 16 * RING * turns_w)
                nc.gpsimd.tensor_copy(W_EDGE[:, (turns_w - 1) * 2 * RING + b * RING:(turns_w - 1) * 2 * RING + (b + 1) * RING],
                                      WGOT[:, b, :]).then_inc(w_ready, 1)
            IDX_BASE2 = IDX_BASE + 2 * turns_w

            pool.wait_ge(cells_added, NPAIR + AHEAD)
            pool.dma_start(count_d, COUNT.rearrange("p g n -> p (g n)")).then_inc(count_out, 16)

            for run in range(2):
                for b in range(2):
                    pool.wait_ge(y_out[b], 16 * R * NT // 2 * (run + 1))
                pool.wait_ge(work_clear, run + 1)

                def gather_half(i, b, peeled, run=run):
                    if not (peeled and run == 0):
                        after(pool, msg_split, i * (2 * RING) + (run * ETILES + b * RING - RING))
                    pool.wait_ge(sorted_in, 16)
                    nc.gpsimd.tensor_copy(IDX[:, b, :], REC[:, bass.ds(i * (2 * RING) + b * RING, RING), 0]).then_inc(idx_set, 1)
                    pool.wait_ge(idx_set, i * 2 + (IDX_BASE2 + run * 2 * turns_w + b + 1))
                    for j in range(RING):
                        tile = i * (2 * RING) + (run * ETILES + b * RING + j)
                        after(pool, msg_split, tile - (ROWS - 1))
                        pool.sem_inc(passed_pool, 1)
                        pool.indirect_dma_start(
                            out=raw[j % ROWS], out_offset=None, in_=y_d[0:(run + 1) * YROWS, :],
                            in_offset=bass.IndirectOffsetOnAxis(ap=IDX[:, b, j:j + 1], axis=0),
                            bounds_check=(run + 1) * YROWS - 1, oob_is_err=False).then_inc(got[j % ROWS], 16)

                if run == 0:
                    pool.wait_ge(w_ready, 2 * turns_w)
                for b in range(2):
                    if run == 0 and b == 0:
                        gather_half(0, b, True)
                    else:
                        gather_half(0, b, False)
                with pool.Fori(1, turns_w) as i:
                    for b in range(2):
                        gather_half(i, b, False)
                if run == 0:
                    pool.wait_ge(pair_added, NPAIR + AHEAD)
                    pool.dma_start(agg_d[0:NPAD, :].rearrange("(g p) n -> p g n", p=P), U).then_inc(agg_out, 16)

            pool.wait_ge(bias_in, 16)

            def add_root(t):
                pool.wait_ge(u_in, t * 32 + 16)
                nc.gpsimd.tensor_tensor(ROOT, ROOT, BIAS_ROOT, ALU.add).then_inc(root_ready, 1)

            def add_gate(t):
                pool.wait_ge(z_in, t * 32 + 32)
                nc.gpsimd.tensor_tensor(GATE, GATE, BIAS_GATE[:, :], ALU.add).then_inc(gate_ready, 1)

            def rstd(t):
                pool.wait_ge(var_ready, t + 1)
                nc.gpsimd.tensor_tensor(RSTD[:, :], VAR[:, :], MINUS_HALF[:, 0:1], ALU.pow).then_inc(rstd_ready, 1)

            add_root(0)
            add_root(1)
            pool.wait_ge(bias_gate_in, 16)
            add_gate(0)
            rstd(0)
            add_root(2)
            with pool.Fori(0, NT - 3) as i:
                add_gate(i + 1)
                rstd(i + 1)
                add_root(i + 3)
            for t in (NT - 2, NT - 1):
                add_gate(t)
                rstd(t)
            with pool.Fori(NT, 2 * NT) as t:
                rstd(t)
            pool.wait_ge(count_out, 16)
            pool.wait_ge(agg_out, 16)

        @block.tensor
        def _(pe):
            def turn_x(t):
                pe.wait_ge(x_in[t % 2], 16 * (t // 2 + 1))
                if t == 0:
                    pe.wait_ge(consts, 1)
                for half in range(2):
                    g = 2 * t + half
                    after(pe, x_split, g - 3)
                    for j in range(4):
                        k = 4 * half + j
                        last = pe.transpose(PM[:, g % 4, j * P:(j + 1) * P], XIN[:, t % 2, k * P:(k + 1) * P], IDENT[:, :])
                    last.then_inc(x_turned, 1)

            def gemm(i, jt, b, first_unit=False):
                j, t = jt // NT, jt % NT
                q = i * TILES_BODY + jt
                bank = jt % 4
                if b == 0:
                    if t == 0 and not first_unit:
                        pe.wait_ge(w_split, i * (2 * KT) + KT * (j + 1))
                    if first_unit:
                        pe.wait_ge(x_split, 2 * (t + 1))
                    after(pe, evac_done, q - 3)
                for k in range(4 * b, 4 * b + 4):
                    if first_unit and t == 0:
                        pe.wait_ge(w_split, k + 1)
                    for n, (lhs, rhs) in enumerate(((xhi, whi), (xhi, wlo), (xlo, whi))):
                        last = pe.matmul(PG[:, bank, :], lhs[:, k, t * P:(t + 1) * P], rhs[:, j % 2, k, :],
                                         start=(k == 0 and n == 0), stop=(k == KT - 1 and n == 2))
                if b == 1:
                    last.then_inc(gemm_done, 1)

            def count_pair(pair, n):
                pe.wait_ge(hot_ready, pair + 1)
                pe.wait_ge(cells_taken, pair + (AHEAD - 1))
                for e in range(2):
                    for h in range(2):
                        last = pe.matmul(PM[:, 2 * (n % 2) + h, 0:NCOL // 2], SRCHOT[:, (2 * n + e) % 4, :],
                                         DSTHOT[:, (2 * n + e) % 4, h * (NCOL // 2):(h + 1) * (NCOL // 2)],
                                         start=(e == 0), stop=(e == 1))
                last.then_inc(cells_done, 1)

            def message_pair(pair, n, run):
                pair = pair + run * NPAIR
                pe.wait_ge(pair_ready, pair * 2 + 2)
                pe.wait_ge(msg_split, pair * 2 + 2)
                pe.wait_ge(pair_added, pair - 1 + AHEAD)
                for e in range(2):
                    for a, part in enumerate((sp_hi, sp_lo)):
                        last = pe.matmul(PM[:, n % 2, :], ONEHOT[:, n % 2, e, :], part[:, n % 2, e, :],
                                         start=(e == 0 and a == 0), stop=(e == 1 and a == 1))
                last.then_inc(pair_done, 1)

            def steps(pair_step):
                def step(i, s, pairs):
                    i, s = normal(i, s)
                    gemm(i, s // 2, s % 2)
                    for pair, n in pairs:
                        pair_step(pair, n)
                return step

            pe.sem_inc(cells_done, AHEAD)
            pe.sem_inc(pair_done, AHEAD)
            turn_x(0)
            for jt in range(TILES_BODY):
                gemm(0, jt, 0, first_unit=jt < NT)
                if jt == 0:
                    turn_x(1)
                gemm(0, jt, 1, first_unit=jt < NT)
                if jt + 2 < NT:
                    turn_x(jt + 2)
                if jt == 14:
                    pe.wait_ge(rows_total, 1)
                    pe.wait_ge(consts, 5)
                    pe.matmul(PM[0:EPART, 0, 0:NT], EARLIER, T10[0:EPART, 0, :], start=True, stop=True)
                    pe.matmul(PM[:, 1, 0:NT], WORK[0:EPART, 3 * NT * ECOL + P:3 * NT * ECOL + 2 * P], T10[0:EPART, 0, :],
                              start=True, stop=True).then_inc(offsets, 1)
            for jt in range(TILES_BODY):
                gemm(1, jt, 0)
                gemm(1, jt, 1)
                if 1 <= jt <= ECOL // CHUNK:
                    c = jt - 1
                    pe.wait_ge(chunk_ready, c + 1)
                    for e in range(CHUNK):
                        last = pe.matmul(PM[:, 3, 0:NKEY], LOCHOT[0:EPART, c % 2, e, :], KEYHOT[0:EPART, c % 2, e, :],
                                         start=(c == 0 and e == 0), stop=(c == ECOL // CHUNK - 1 and e == CHUNK - 1))
                    last.then_inc(chunk_done, 1)
            plain((2, 0), COUNT_AT, steps(None))
            one_each(pe, COUNT_AT, steps(count_pair))
            plain(phase_end(COUNT_AT), RUN0_AT, steps(None))
            pe.wait_ge(deg_max_ready, 1)
            pe.wait_ge(cells_taken, NPAIR + AHEAD)
            pe.transpose(PM[:, 3, 0:P], DEG_MAX[:, 0:1].to_broadcast([P, P]), IDENT[:, :]).then_inc(deg_max_turned, 1)
            one_each(pe, RUN0_AT, steps(lambda pair, n: message_pair(pair, n, 0)))
            plain(phase_end(RUN0_AT), (RUN1_BODY, 0), steps(None))
            dense(pe, RUN1_BODY, steps(lambda pair, n: message_pair(pair, n, 1)))

            def turn_u(t):
                pe.wait_ge(u_ready, t + 1)
                after(pe, u_split, t)
                for k in range(KT):
                    last = pe.transpose(PM[:, k // 4, (k % 4) * P:(k % 4 + 1) * P], USUM[:, k * P:(k + 1) * P], IDENT[:, :])
                last.then_inc(u_turned, 1)

            def gate(t):
                pe.wait_ge(u_split, t + 1)
                after(pe, z_read, t)
                for h in range(2):
                    for k in range(KT):
                        if h == 1 and isinstance(t, int) and t == 0:
                            pe.wait_ge(w_split, (UNITS_Y + 5) * KT + k + 1)
                        for n, (lhs, rhs) in enumerate(((ut_hi, whi), (ut_hi, wlo), (ut_lo, whi))):
                            last = pe.matmul(PG[:, h, :], lhs[:, k * P:(k + 1) * P], rhs[:, h, k, :],
                                             start=(k == 0 and n == 0), stop=(k == KT - 1 and n == 2))
                last.then_inc(z_done, 1)

            def turn_x1(t):
                pe.wait_ge(x1_ready, t + 1)
                after(pe, x1_split, t)
                for k in range(KT):
                    last = pe.transpose(PM[:, 2 + k // 4, (k % 4) * P:(k % 4 + 1) * P], X1[:, k * P:(k + 1) * P], IDENT[:, :])
                last.then_inc(x1_turned, 1)

            def conv_in(t):
                pe.wait_ge(x1_split, t + 1)
                after(pe, h_split, t)
                for h in range(2):
                    for k in range(KT):
                        if isinstance(t, int) and t == 0:
                            pe.wait_ge(w_split, (UNITS_Y + 6 + h) * KT + k + 1)
                        for n, (lhs, rhs) in enumerate(((SPHI, gcn_hi), (SPHI, gcn_lo), (SPLO, gcn_hi))):
                            last = pe.matmul(PG[:, 2 + h, :], lhs[:, k * P:(k + 1) * P], rhs[:, k, h * HW:(h + 1) * HW],
                                             start=(k == 0 and n == 0), stop=(k == KT - 1 and n == 2))
                last.then_inc(h_done, 1)

            pe.wait_ge(w_split, (UNITS_Y + 5) * KT)
            turn_u(0)
            gate(0)
            turn_u(1)
            gate(1)
            turn_x1(0)
            turn_u(2)
            conv_in(0)
            turn_x1(1)
            with pe.Fori(1, NT - 2) as i:
                gate(i + 1)
                turn_u(i + 2)
                conv_in(i)
                turn_x1(i + 1)
            gate(NT - 1)
            conv_in(NT - 2)
            turn_x1(NT - 1)
            conv_in(NT - 1)

            pe.wait_ge(large_ready, 1)
            large = pe.value_load(LARGE[0:1, 0:1], min_val=0, max_val=1)

            def h_parts(s):
                if s < KT:
                    return hhi[:, s, :], hlo[:, s, :]
                return (HLAST[:, 0, :], HLAST[:, 1, :]) if s == KT else (ut_hi, ut_lo)

            def conv(d, b, first):
                pe.wait_ge(c_high, d + 1)
                after(pe, conv_read, d - 1)
                order = [KT] + list(range(KT)) + [KT + 1]
                for s in order:
                    if first and s < KT:
                        pe.wait_ge(h_in[s], 32)
                    if first and s >= KT:
                        pe.wait_ge(h_split, s + 1)
                    if s == order[-1]:
                        with pe.If(large > 0):
                            pe.wait_ge(c_split, d + 1)
                            for s_low in order:
                                for h in range(2):
                                    pe.matmul(PG[:, 2 * b + h, :], XLO[:, b * NPAD + s_low * P:b * NPAD + (s_low + 1) * P],
                                              h_parts(s_low)[0][:, h * HW:(h + 1) * HW], start=False, stop=False)
                    for n, part in enumerate(h_parts(s)):
                        for h in range(2):
                            last = pe.matmul(PG[:, 2 * b + h, :], XHI[:, b * NPAD + s * P:b * NPAD + (s + 1) * P],
                                             part[:, h * HW:(h + 1) * HW], start=(s == order[0] and n == 0),
                                             stop=(s == order[-1] and n == 1))
                last.then_inc(conv_done, 1)

            for b in range(2):
                conv(b, b, b == 0)
            with pe.Fori(1, NT // 2) as i:
                for b in range(2):
                    conv(2 * i + b, b, False)

        @block.scalar
        def _(act):
            def x_high(t):
                for half in range(2):
                    g = 2 * t + half
                    act.wait_ge(x_turned, g + 1)
                    nc.scalar.activation(xhi[:, 4 * half:4 * half + 4, t * P:(t + 1) * P],
                                         PM[:, g % 4, :].rearrange("p (k n) -> p k n", k=4), ACT.Copy).then_inc(x_hi, 1)

            def w_high(k, high, raw):
                nc.scalar.activation(high[:, k, :], raw[:, k, :], ACT.Copy).then_inc(w_hi, 1)

            def evac(i, jt):
                q = i * TILES_BODY + jt
                b = jt % 2
                act.wait_ge(gemm_done, q + 1)
                after(act, y_out[b], i * (16 * NT) + 16 * (jt // 2))
                nc.scalar.activation(STAGE[:, b, :], PG[:, jt % 4, :], ACT.Copy).then_inc(evac_done, 1)

            def store_y(i, jt):
                q = i * TILES_BODY + jt
                b = jt % 2
                act.wait_ge(evac_done, q + 1)
                act.dma_start(y_d[bass.ds(q * P, P), :], STAGE[:, b, :]).then_inc(y_out[b], 16)

            def w_high_next(i, jt):
                j, k = jt // NT, jt % NT - 1
                b = (j + 1) % 2
                if 0 <= k < KT:
                    if k == 0:
                        act.wait_ge(w_in[b], i * 32 + 32)
                    w_high(k, whi[:, b, :, :], wraw[:, b, :, :])

            def msg_high(pair, n, run):
                for e in range(2):
                    act.wait_ge(got[(2 * n + e) % ROWS], pair * 4 + (run * NPAIR * 4 + 16 - 4 * (n % 4)))
                    if e == 0:
                        act.wait_ge(pair_done, pair + (run * NPAIR - 1 + AHEAD))
                    act.wait_ge(w_ready, 2 * (ETILES // (2 * RING)))
                    nc.scalar.activation(sp_hi[:, n % 2, e, :], raw[(2 * n + e) % ROWS], ACT.Copy,
                                         scale=W_EDGE[:, bass.ds(pair * 2 + e, 1)]).then_inc(msg_hi, 1)

            def take_counts(pair, n):
                act.wait_ge(cells_done, pair + (1 + AHEAD))
                act.wait_ge(cells_added, pair + (AHEAD - 1))
                nc.scalar.activation(TALLY[:, n % 2, :].rearrange("p (h n) -> p h n", h=2),
                                     PM[:, 2 * (n % 2):2 * (n % 2) + 2, 0:NCOL // 2], ACT.Copy).then_inc(cells_taken, 1)

            def steps(run, counts=False):
                def step(i, s, pairs):
                    i, s = normal(i, s)
                    if run is not None:
                        for pair, n in pairs:
                            msg_high(pair, n, run)
                    if s % 2 == 0:
                        i, jt = (i, s // 2 - 1) if s > 0 else (i - 1, TILES_BODY - 1)
                        evac(i, jt)
                        w_high_next(i, jt)
                        store_y(i, jt)
                    if counts:
                        for pair, n in pairs:
                            take_counts(pair, n)
                return step

            act.sem_inc(cells_taken, AHEAD)
            x_high(0)
            for k in range(KT):
                if k == KT // 2:
                    x_high(1)
                act.wait_ge(w0_in[k], 16)
                w_high(k, whi[:, 0, :, :], wraw[:, 0, :, :])
            for jt in range(TILES_BODY - 1):
                evac(0, jt)
                store_y(0, jt)
                if jt + 2 < NT:
                    x_high(jt + 2)
                w_high_next(0, jt)
            plain((1, 0), COUNT_AT, steps(None))
            one_each(act, COUNT_AT, steps(None, True))
            plain(phase_end(COUNT_AT), RUN0_AT, steps(None))
            one_each(act, RUN0_AT, steps(0))
            plain(phase_end(RUN0_AT), (RUN1_BODY, 0), steps(None))
            dense(act, RUN1_BODY, steps(1))
            evac(RUN1_BODY + 1, TILES_BODY - 1)
            store_y(RUN1_BODY + 1, TILES_BODY - 1)

            def gate_high():
                act.wait_ge(w_in[1], (UNITS_Y + 6) // 2 * 32)
                for k in range(KT):
                    w_high(k, whi[:, 1, :, :], wraw[:, 1, :, :])

            def gcn_high(h):
                cols = slice(h * HW, (h + 1) * HW)
                act.wait_ge(w_in[h], (UNITS_Y + 7 + h) // 2 * 32)
                for k in range(KT):
                    w_high(k, gcn_hi[:, :, cols], gcn_raw[:, :, cols])

            def u_high(t):
                act.wait_ge(u_turned, t + 1)
                after(act, z_done, t)
                for half in range(2):
                    nc.scalar.activation(ut_hi[:, half * HW:(half + 1) * HW], PM[:, half, :], ACT.Copy).then_inc(u_hi, 1)

            def tanh_u(t):
                act.wait_ge(u_ready, t + 1)
                after(act, x1_ready, t)
                nc.scalar.activation(TANH, USUM, ACT.Tanh).then_inc(tanh_done, 1)

            def h_high(t, d0, d1):
                act.wait_ge(h_done, t + 1)
                act.wait_ge(dinv_ready, 1)
                for half, d_ap in ((0, d0), (1, d1)):
                    nc.scalar.activation(d_ap, PG[:, 2 + half, :], ACT.Copy, scale=DINV[:, bass.ds(t, 1)]).then_inc(h_hi, 1)

            def x1_high(t):
                act.wait_ge(x1_turned, t + 1)
                after(act, h_done, t)
                for half in range(2):
                    nc.scalar.activation(SPHI[:, half * HW:(half + 1) * HW], PM[:, 2 + half, :], ACT.Copy).then_inc(x1_hi, 1)
                act.dma_start(x1_d[bass.ds(t * P, P), :], X1).then_inc(x1_out, 16)

            def h_store(t):
                act.wait_ge(h_split, t + 1)
                act.dma_start(hhi_d[bass.ds(t * P, P), :], HST_HI[:, :].bitcast(F32)).then_inc(h_out, 16)
                act.dma_start(hlo_d[bass.ds(t * P, P), :], HST_LO[:, :].bitcast(F32)).then_inc(h_out, 16)

            u_high(0)
            gate_high()
            tanh_u(0)
            u_high(1)
            tanh_u(1)
            gcn_high(0)
            x1_high(0)
            gcn_high(1)
            for b in range(2):
                act.wait_ge(y_out[b], 16 * (UNITS_Y + 4) * NT // 2)

            def tile_body(t, staged):
                if t_in(t + 2):
                    u_high(t + 2)
                if staged:
                    after(act, h_out, t * 32)
                    h_high(t, HST_HI[:, 0:HW], HST_HI[:, HW:D])
                else:
                    place_h = HLAST[:, 0, :] if t == NT - 2 else ut_hi
                    h_high(t, place_h[:, 0:HW], place_h[:, HW:D])
                if t_in(t + 1):
                    x1_high(t + 1)
                if t_in(t + 2):
                    tanh_u(t + 2)
                if staged:
                    h_store(t)

            def t_in(t):
                return not isinstance(t, int) or t < NT

            tile_body(0, True)
            with act.Fori(1, NT - 2) as i:
                tile_body(i, True)
            tile_body(NT - 2, False)
            tile_body(NT - 1, False)
            act.wait_ge(h_out, 32 * KT)
            act.wait_ge(x1_out, 16 * NT)

            def store(d, b, rows):
                act.wait_ge(out_ready, d + 1)
                if rows == P:
                    act.dma_start(out[bass.ds(d * P, P), :], result[b]).then_inc(out_done[b], 16)
                else:
                    act.dma_start(out[d * P:N, :], result[b][0:rows, :]).then_inc(out_done[b], 16)

            with act.Fori(0, NT // 2 - 1) as i:
                for b in range(2):
                    store(2 * i + b, b, P)
            store(NT - 2, 0, P)
            store(NT - 1, 1, LAST)
            for b in range(2):
                act.wait_ge(out_done[b], 16 * NT // 2)

        @block.vector
        def _(dve):
            chain = Chain(dve, dve_chain)
            link = chain.link
            V = nc.vector

            def x_low(t):
                for half in range(2):
                    g = 2 * t + half
                    dve.wait_ge(x_hi, g + 1)
                    dst_ap = xlo[:, 4 * half:4 * half + 4, t * P:(t + 1) * P]
                    hi_ap = xhi[:, 4 * half:4 * half + 4, t * P:(t + 1) * P].bitcast(F32)
                    V.tensor_tensor(dst_ap, PM[:, g % 4, :].rearrange("p (k n) -> p k n", k=4), hi_ap,
                                    ALU.subtract).then_inc(x_split, 1)

            def w_low(m, k, high, low, raw):
                dve.wait_ge(w_hi, m + 1)
                V.tensor_tensor(low[:, k, :], raw[:, k, :], high[:, k, :].bitcast(F32), ALU.subtract).then_inc(w_split, 1)

            def w_low_next(i, jt):
                j, k = jt // NT, jt % NT - 1
                b = (j + 1) % 2
                if 0 <= k < KT:
                    w_low(i * (2 * KT) + (KT * (j + 1) + k), k, whi[:, b, :, :], wlo[:, b, :, :], wraw[:, b, :, :])

            def edge_fields():
                dve.wait_ge(edges_in, 48)
                V.tensor_scalar(T_GRP, T_DST, 7, None, ALU.logical_shift_right)
                link(V.tensor_scalar(T_LOC, T_DST, P - 1, None, ALU.bitwise_and))
                V.tensor_copy(T_GRPF, T_GRP)
                V.tensor_copy(T_LOCF, T_LOC)
                link(V.tensor_copy(REC[0:EPART, 0:ECOL, 2].bitcast(F32), T_LOC))
                link(V.scalar_tensor_tensor(KEY[:, :], T_GRPF, float(R), T_TYPE, ALU.mult, ALU.add))
                V.scalar_tensor_tensor(REC[0:EPART, 0:ECOL, 1], T_LOCF, float(NKEY), KEY[:, :], ALU.mult, ALU.add)
                V.scalar_tensor_tensor(REC[0:EPART, 0:ECOL, 0], T_TYPE, float(NPAD), T_SRC, ALU.mult, ALU.add)
                link(V.tensor_copy(REC[0:EPART, 0:ECOL, 3], T_SRC))

            def membership():
                for g in range(NT):
                    last = V.tensor_scalar(MEMB[:, g, :], T_GRPF, float(g), None, ALU.is_equal)
                link(last)

            def scan_step(n):
                a = MEMB if n == 0 else SCAN[(n - 1) % 2]
                b, s = SCAN[n % 2], 1 << n
                V.tensor_copy(b[:, :, 0:s], a[:, :, 0:s])
                link(V.tensor_tensor(b[:, :, s:ECOL], a[:, :, s:ECOL], a[:, :, 0:ECOL - s], ALU.add))

            SCANS = (ECOL - 1).bit_length()
            PREFIX = SCAN[(SCANS - 1) % 2]

            def group_starts():
                dve.wait_ge(offsets, 1)
                link(V.tensor_scalar(T10I[:, :], PM[:, 1, 0:NT], float(PAIR - 1), None, ALU.add))
                link(V.tensor_scalar(T10I[:, :], T10I[:, :], 8, 8, ALU.logical_shift_right, ALU.logical_shift_left))
                link(V.tensor_copy(T10[:, 1, :], T10I[:, :]))
                link(V.memset(T10[:, 2, 0:1], 0.0))
                for g in range(1, NT):
                    link(V.tensor_tensor(T10[:, 2, g:g + 1], T10[:, 2, g - 1:g], T10[:, 1, g - 1:g], ALU.add))
                link(V.scalar_tensor_tensor(T10[0:EPART, 3, :], PM[0:EPART, 0, 0:NT], -1.0, T10[0:EPART, 2, :], ALU.add, ALU.add))

            def positions_a():
                link(V.tensor_tensor(PREFIX, PREFIX, T10[0:EPART, 3, :].unsqueeze(2).to_broadcast([EPART, NT, ECOL]), ALU.add))
                link(V.tensor_tensor(PREFIX, PREFIX, MEMB, ALU.mult))

            def positions_b():
                link(V.tensor_reduce(O_POS, PREFIX.rearrange("p g c -> p c g"), AXIS_X, ALU.add))
                link(V.tensor_copy(O_POSI, O_POS))
                V.tensor_scalar(O_LANE, O_POSI, P - 1, None, ALU.bitwise_and)
                link(V.tensor_scalar(O_TILE, O_POSI, 7, None, ALU.logical_shift_right))
                V.scalar_tensor_tensor(ADDR[:, :], O_LANE, float(ETILES), O_TILE, ALU.mult, ALU.add).then_inc(pos_ready, 1)

            def pair_groups():
                dve.wait_ge(consts, 7)
                link(V.memset(PAIRSUM[:, 0, :], 0.0))
                for g in range(1, NT):
                    link(V.scalar_tensor_tensor(PAIRSUM[:, 0, :], PAIRSUM[:, 1, :], T10[0:1, 2, g:g + 1], PAIRSUM[:, 0, :],
                                                ALU.is_ge, ALU.add))
                link(V.tensor_copy(GROUP[:, :], PAIRSUM[:, 0, :]))

            def sort_step(n):
                if n == 0:
                    edge_fields()
                elif n == 1:
                    membership()
                elif n - 2 < SCANS:
                    scan_step(n - 2)
                elif n == SCANS + 2:
                    V.tensor_copy(T10[0:EPART, 0, :], PREFIX[:, :, ECOL - 1]).then_inc(rows_total, 1)
                elif n == 15:
                    group_starts()
                elif n == 16:
                    positions_a()
                elif n == 17:
                    positions_b()
                elif n == 18:
                    pair_groups()

            def hot_chunk(c):
                if c == 0:
                    dve.wait_ge(pad_out, 16)
                if c >= 2:
                    dve.wait_ge(chunk_done, c - 1)
                cols = slice(c * CHUNK, (c + 1) * CHUNK)
                V.tensor_tensor(LOCHOT[0:EPART, c % 2, :, :], IOTA[0:EPART, 0:P].unsqueeze(1).to_broadcast([EPART, CHUNK, P]),
                                REC[0:EPART, cols, 2].bitcast(F32).unsqueeze(2).to_broadcast([EPART, CHUNK, P]), ALU.is_equal)
                V.tensor_tensor(KEYHOT[0:EPART, c % 2, :, :], IOTA[0:EPART, 0:NKEY].unsqueeze(1).to_broadcast([EPART, CHUNK, NKEY]),
                                KEY[:, cols].unsqueeze(2).to_broadcast([EPART, CHUNK, NKEY]), ALU.is_equal).then_inc(chunk_ready, 1)


            def inverse_counts():
                dve.wait_ge(chunk_done, ECOL // CHUNK)
                link(V.tensor_scalar(INV[:, :], PM[:, 3, 0:NKEY], 1.0, None, ALU.max))
                V.reciprocal(INV[:, :], INV[:, :]).then_inc(inv_ready, 1)
                link(V.tensor_reduce(DEG[:, :], PM[:, 3, 0:NKEY].rearrange("p (g r) -> p g r", g=NT), AXIS_X, ALU.add))
                V.tensor_scalar(DEG[:, :], DEG[:, :], 1.0, None, ALU.add).then_inc(deg_ready, 1)

            def count_setup():
                dve.wait_ge(deg_ready, 1)
                V.tensor_reduce(DEG_MAX[:, :], DEG[:, :], AXIS_X, ALU.max).then_inc(deg_max_ready, 1)
                dve.wait_ge(sorted_in, 16)
                t_loc = WORK[:, 0:ETILES].bitcast(I32)
                t_grp = WORK[:, ETILES:2 * ETILES].bitcast(I32)
                V.tensor_scalar(t_loc, REC[:, :, 3], P - 1, None, ALU.bitwise_and)
                link(V.tensor_scalar(t_grp, REC[:, :, 3], 7, None, ALU.logical_shift_right))
                V.tensor_copy(SRC_LOC[:, :], t_loc)
                t_dst = WORK[:, 2 * ETILES:3 * ETILES].bitcast(I32)
                t_half = WORK[:, 3 * ETILES:4 * ETILES].bitcast(I32)
                t_odd = WORK[:, 4 * ETILES:5 * ETILES].bitcast(I32)
                link(V.tensor_copy(t_dst, REC[:, :, 2].bitcast(F32)))
                V.tensor_scalar(t_half, t_dst, 1, None, ALU.arith_shift_right)
                link(V.tensor_scalar(t_odd, t_dst, 1, None, ALU.bitwise_and))
                V.tensor_scalar(WORTH[:, :], t_odd, float(HIGH_CELL - 1), 1.0, ALU.mult, ALU.add)
                link(V.scalar_tensor_tensor(CELL[:, :], t_grp, float(P // 2), t_half, ALU.mult, ALU.add))
                link(V.memset(WORK[:, 0:NT * NPAD // 2].bitcast(I32), 0))
                for g in range(NT):
                    last = V.tensor_copy(COUNT[:, g, g * P:(g + 1) * P], IDENT[:, :])
                link(last)

            def count_hot(pair, n):
                dve.wait_ge(cells_done, pair + (AHEAD - 1))
                for e in range(2):
                    s = (2 * n + e) % 4
                    tile = bass.ds(pair * 2 + e, 1)
                    V.tensor_scalar(SRCHOT[:, s, :], IOTA[:, 0:P], SRC_LOC[:, tile], None, ALU.is_equal)
                    last = V.tensor_scalar(DSTHOT[:, s, :], COLS[:, :], CELL[:, tile], WORTH[:, tile], ALU.is_equal, ALU.mult)
                last.then_inc(hot_ready, 1)

            def group_of(pair):
                return dve.value_load(GROUP[0:1, bass.ds(pair, 1)], min_val=0, max_val=NT - 1)

            def count_add(pair, n):
                g = group_of(pair)
                dve.wait_ge(cells_taken, pair + 1 + AHEAD)
                acc = COUNT[:, bass.ds(g, 1), :].rearrange("p a n -> p (a n)")
                V.tensor_tensor(acc, acc, TALLY[:, n % 2, :].bitcast(I16), ALU.add).then_inc(cells_added, 1)
                dve.wait_ge(cells_added, pair + 1 + AHEAD)

            def msg_low(pair, n, run):
                for e in range(2):
                    V.tensor_scalar(ONEHOT[:, n % 2, e, :], IOTA[:, 0:P], REC[:, bass.ds(pair * 2 + e, 1), 2].bitcast(F32), None,
                                    ALU.is_equal).then_inc(pair_ready, 1)
                for e in range(2):
                    dve.wait_ge(msg_hi, pair * 2 + (2 * run * NPAIR + e + 1))
                    V.scalar_tensor_tensor(sp_lo[:, n % 2, e, :], raw[(2 * n + e) % ROWS], W_EDGE[:, bass.ds(pair * 2 + e, 1)],
                                           sp_hi[:, n % 2, e, :].bitcast(F32), ALU.mult, ALU.subtract).then_inc(msg_split, 1)

            def msg_add(pair, n, run):
                g = group_of(pair)
                dve.wait_ge(pair_done, pair + (run * NPAIR + 1 + AHEAD))
                acc = U[:, bass.ds(g, 1), :].rearrange("p a n -> p (a n)")
                V.tensor_tensor(acc, acc, PM[:, n % 2, :], ALU.add).then_inc(pair_added, 1)
                dve.wait_ge(pair_added, pair + (run * NPAIR + 1 + AHEAD))

            def steps(prepare, add):
                def step(i, s, pairs):
                    i, s = normal(i, s)
                    for pair, n in pairs:
                        prepare(pair, n)
                        if n > 0:
                            add(pair - 1, n - 1)
                    if s % 2 == 0 and s > 0:
                        w_low_next(i, s // 2 - 1)
                return step

            dve.sem_inc(pair_added, AHEAD)
            dve.sem_inc(cells_added, AHEAD)
            x_low(0)
            for k in range(KT):
                if k == KT // 2:
                    x_low(1)
                w_low(k, k, whi[:, 0, :, :], wlo[:, 0, :, :], wraw[:, 0, :, :])
            for jt in range(TILES_BODY):
                if jt + 2 < NT:
                    x_low(jt + 2)
                w_low_next(0, jt)
                sort_step(jt)
            dve.wait_ge(consts, 3)
            for jt in range(TILES_BODY):
                w_low_next(1, jt)
                if jt < ECOL // CHUNK:
                    hot_chunk(jt)
                if jt == ECOL // CHUNK + 2:
                    inverse_counts()
            nothing = steps(None, None)
            plain((2, 0), SETUP_AT, nothing)
            count_setup()
            plain(SETUP_AT, COUNT_AT, nothing)
            one_each(dve, COUNT_AT, steps(count_hot, count_add), count_add)
            dve.wait_ge(count_out, 16)
            for row in raw:
                V.memset(row, 0.0)
            V.memset(WORK[:, 0:NT * HW], 0.0).then_inc(work_clear, 1)
            dve.wait_ge(work_clear, 1)
            plain(phase_end(COUNT_AT), RUN0_AT, nothing)

            def add0(pair, n):
                msg_add(pair, n, 0)

            def add1(pair, n):
                msg_add(pair, n, 1)

            dve.wait_ge(deg_max_turned, 1)
            link(V.tensor_reduce(DEG_MAX[0:1, :], PM[0:1, 3, 0:P], AXIS_X, ALU.max))
            V.tensor_scalar(LARGE[:, :], DEG_MAX[0:1, :], float(EXACT), None, ALU.is_gt).then_inc(large_ready, 1)
            one_each(dve, RUN0_AT, steps(lambda pair, n: msg_low(pair, n, 0), add0), add0)
            dve.wait_ge(agg_out, 16)
            V.tensor_scalar(REC[:, :, 0], REC[:, :, 0], float(YROWS), None, ALU.add)
            V.memset(WORK[:, 0:NT * HW], 0.0).then_inc(work_clear, 1)
            dve.wait_ge(work_clear, 2)
            plain(phase_end(RUN0_AT), (RUN1_BODY, 0), nothing)
            dense(dve, RUN1_BODY, steps(lambda pair, n: msg_low(pair, n, 1), add1), add1)

            def gate_low():
                for k in range(KT):
                    w_low((UNITS_Y + 5) * KT + k, k, whi[:, 1, :, :], wlo[:, 1, :, :], wraw[:, 1, :, :])

            def gcn_low(h):
                cols = slice(h * HW, (h + 1) * HW)
                for k in range(KT):
                    w_low((UNITS_Y + 6 + h) * KT + k, k, gcn_hi[:, :, cols], gcn_lo[:, :, cols], gcn_raw[:, :, cols])

            def make_first_u():
                dve.wait_ge(sums0_in, 16)
                dve.wait_ge(root_ready, 1)
                V.tensor_tensor(USUM[:, 0:HW], USUM[:, 0:HW], ROOT[:, 0:HW], ALU.add)
                V.tensor_tensor(USUM[:, HW:D], U[:, 0, :], ROOT[:, HW:D], ALU.add).then_inc(u_ready, 1)

            def make_u(t):
                dve.wait_ge(root_ready, t + 1)
                after(dve, u_turned, t)
                after(dve, tanh_done, t)
                V.tensor_tensor(USUM[:, 0:HW], SUMS, ROOT[:, 0:HW], ALU.add)
                V.tensor_tensor(USUM[:, HW:D], U[:, bass.ds(t, 1), :].rearrange("p a n -> p (a n)"), ROOT[:, HW:D],
                                ALU.add).then_inc(u_ready, 1)

            def u_low(t):
                dve.wait_ge(u_hi, t * 2 + 2)
                V.tensor_tensor(ut_lo[:, 0:HW], PM[:, 0, :], ut_hi[:, 0:HW].bitcast(F32), ALU.subtract)
                V.tensor_tensor(ut_lo[:, HW:D], PM[:, 1, :], ut_hi[:, HW:D].bitcast(F32), ALU.subtract).then_inc(u_split, 1)

            def norm(y, ready, t):
                for h in range(2):
                    last = V.bn_stats(STATS[:, h, :], y[:, h * HW:(h + 1) * HW])
                link(last)
                dve.sem_inc(passed_dve, 1)
                link(V.bn_aggr(MV[:, :], STATS[:, :, :].rearrange("p a b -> p (a b)")))
                V.tensor_scalar(VAR[:, :], MV[:, 1:2], EPS, None, ALU.add).then_inc(var_ready, 1)
                dve.wait_ge(rstd_ready, t + 1)
                V.tensor_scalar(y, y, MV[:, 0:1], RSTD[:, 0:1], ALU.subtract, ALU.mult).then_inc(ready, 1)

            def make_z(t):
                dve.wait_ge(tanh_done, t + 1)
                dve.wait_ge(gate_ready, t + 1)
                V.tensor_tensor(TANH, TANH, XROWS, ALU.subtract)
                dve.wait_ge(z_done, t + 1)
                V.tensor_tensor(GATE[:, 0:HW], PG[:, 0, :], GATE[:, 0:HW], ALU.add)
                V.tensor_tensor(GATE[:, HW:D], PG[:, 1, :], GATE[:, HW:D], ALU.add).then_inc(z_read, 1)

            def blend(t):
                dve.wait_ge(z_read, t + 1)
                after(dve, x1_turned, t)
                after(dve, x1_out, t * 16)
                link(V.tensor_tensor(GATE, GATE, TANH, ALU.mult))
                link(V.scalar_tensor_tensor(X1, XROWS, 2.0, GATE, ALU.mult, ALU.add))
                norm(X1, x1_ready, t)

            def make_x1(t):
                make_z(t)
                blend(t)

            def h_low(t, high, low):
                dve.wait_ge(h_hi, t * 2 + 2)
                sc = DINV[:, bass.ds(t, 1)]
                V.scalar_tensor_tensor(low[:, 0:HW], PG[:, 2, :], sc, high[:, 0:HW].bitcast(F32), ALU.mult, ALU.subtract)
                V.scalar_tensor_tensor(low[:, HW:D], PG[:, 3, :], sc, high[:, HW:D].bitcast(F32), ALU.mult,
                                       ALU.subtract).then_inc(h_split, 1)

            def x1_low(t):
                dve.wait_ge(x1_hi, t * 2 + 2)
                V.tensor_tensor(SPLO[:, 0:HW], PM[:, 2, :], SPHI[:, 0:HW].bitcast(F32), ALU.subtract)
                V.tensor_tensor(SPLO[:, HW:D], PM[:, 3, :], SPHI[:, HW:D].bitcast(F32), ALU.subtract).then_inc(x1_split, 1)

            X1_STEPS = 4
            make_first_u()
            u_low(0)
            gate_low()
            make_u(1)
            make_z(0)
            u_low(1)
            blend(0)
            make_u(2)
            gcn_low(0)
            x1_low(0)
            gcn_low(1)
            with dve.Fori(0, NT - 3) as i:
                chain.enter(i, X1_STEPS)
                u_low(i + 2)
                make_x1(i + 1)
                h_low(i, HST_HI[:, :], HST_LO[:, :])
                x1_low(i + 1)
                make_u(i + 3)
            chain.leave(NT - 3, X1_STEPS)
            u_low(NT - 1)
            make_x1(NT - 2)
            h_low(NT - 3, HST_HI[:, :], HST_LO[:, :])
            x1_low(NT - 2)
            make_x1(NT - 1)
            h_low(NT - 2, HLAST[:, 0, :], HLAST[:, 1, :])
            x1_low(NT - 1)

            def counts_high(d, b):
                dve.wait_ge(c_in[b], (d - b) * 8 + 16)
                dve.wait_ge(h_done, NT)
                after(dve, conv_done, d - 1)
                V.tensor_copy(XHI[:, b * NPAD:(b + 1) * NPAD], CIN[b][:, :]).then_inc(c_high, 1)

            def counts_low(d, b):
                dve.wait_ge(c_high, d + 1)
                V.tensor_tensor(XLO[:, b * NPAD:(b + 1) * NPAD], CIN[b][:, :], XHI[:, b * NPAD:(b + 1) * NPAD].bitcast(F32),
                                ALU.subtract).then_inc(c_split, 1)

            def counts_split(d, b):
                counts_high(d, b)
                counts_low(d, b)

            def finish(d, b):
                y = result[b]
                dve.wait_ge(conv_done, d + 1)
                after(dve, out_done[b], (d - b) * 8)
                for h in range(2):
                    last = V.scalar_tensor_tensor(y[:, h * HW:(h + 1) * HW], PG[:, 2 * b + h, :], DINV[:, bass.ds(d, 1)],
                                                  BIAS_GCN[:, h * HW:(h + 1) * HW], ALU.mult, ALU.add)
                last.then_inc(conv_read, 1)
                dve.wait_ge(conv_read, d + 1)
                dve.wait_ge(res_in[b], (d - b) * 8 + 16)
                link(V.scalar_tensor_tensor(y, y, 0.0, res[b], ALU.max, ALU.add))
                norm(y, out_ready, d + NT)

            counts_high(0, 0)
            h_low(NT - 1, ut_hi, ut_lo)
            counts_low(0, 0)
            counts_split(1, 1)
            dve.wait_ge(bias1_in, 16)
            finish(0, 0)

            def two_tiles(i):
                counts_split(2 * i + 2, 0)
                finish(2 * i + 1, 1)
                counts_split(2 * i + 3, 1)
                finish(2 * i + 2, 0)

            two_tiles(0)
            with dve.Fori(1, NT // 2 - 1) as i:
                chain.enter(i - 1, 6)
                two_tiles(i)
            chain.leave(NT // 2 - 2, 6)
            finish(NT - 1, 1)


_INS = ['x', 'src', 'dst', 'edge_type_8', 'L0_gnn_weight', 'L0_gnn_root', 'L0_gnn_bias', 'L0_gnn_w_gate', 'L0_gnn_b_gate',
        'L1_gnn_W', 'L1_gnn_b']
_OUTS = [((N, D), 'float32')]


def kernel(**inputs):
    import numpy as _np
    import concourse.bacc as _bacc
    from concourse import mybir as _mybir
    from concourse.bass_utils import run_bass_kernel_spmd as _run

    nc = _bacc.Bacc("TRN2", target_bir_lowering=False, num_devices=1)
    arrays, args = {}, []
    for name in _INS:
        a = _np.ascontiguousarray(inputs[name])
        arrays[f"in_{name}_dram"] = a
        args.append(nc.dram_tensor(f"in_{name}_dram", a.shape, _mybir.dt.from_np(a.dtype), kind="ExternalInput").ap())
    for i, (shape, dtype) in enumerate(_OUTS):
        dt = _mybir.dt.from_np(_np.dtype(dtype))
        args.append(nc.dram_tensor(f"out_{i}_dram", shape, dt, kind="ExternalOutput").ap())
    gnn_resnorm_kernel(nc, *args)
    r = _run(nc, [arrays], core_ids=[0])
    return r.results[0]["out_0_dram"]
```
